# Optimizing a Trainium2 kernel written in Bass

```python
import numpy as np
import jax
import jax.numpy as jnp

def _softmax(x, axis=-1):
    return jax.nn.softmax(x, axis=axis)

def _gelu(x):
    return jax.nn.gelu(x, approximate=True)

def _silu(x):
    return jax.nn.silu(x)

def _sigmoid(x):
    return jax.nn.sigmoid(x)

def _layernorm(x, axis=-1, eps=1e-05):
    m = jnp.mean(x, axis=axis, keepdims=True)
    v = jnp.var(x, axis=axis, keepdims=True)
    return (x - m) / jnp.sqrt(v + eps)

def _scatter_add(tgt, idx, src, axis=0):
    return tgt.at[idx].add(src)

def _segment_sum(src, seg, n):
    return jax.ops.segment_sum(src, seg, n)
kernel_name = 'mk_gps_d4_gnn_r8_c1e22a'

def setup_inputs(seed: int=0):
    np.random.seed(seed)
    _w = jnp.asarray

    def _rec_inputs():
        import jax
        import jax.numpy as jnp
        _gk = jax.random.key(seed)
        x = -0.001003 + 1 * jax.random.normal(jax.random.fold_in(_gk, 1), (256, 768), jnp.float32)
        src = jax.random.randint(jax.random.fold_in(_gk, 2), (4096,), 0, 256, jnp.int32)
        dst = jnp.minimum((256 * jax.random.uniform(jax.random.fold_in(_gk, 3), (4096,)) ** 2.0).astype(jnp.int32), 2047)
        _o = jnp.argsort(dst, stable=True)
        src = src[_o]
        dst = dst[_o]
        edge_type_3 = jax.random.randint(jax.random.fold_in(_gk, 13), (4096,), 0, 3, jnp.int32)
        return (x, src, dst, edge_type_3)
    x, src, dst, edge_type_3 = _rec_inputs()

    def _L0_gnn_setup():
        import jax, jax.numpy as jnp
        import numpy as np
        NUM_RELATIONS = 3

        def _rgcn(x, W_rel, W_root, bias, src, dst, etype):
            n = x.shape[0]
            xr = jnp.einsum('ni,rio->rno', x, W_rel)
            msg = xr[etype, src]
            out = x @ W_root + bias
            for r in range(NUM_RELATIONS):
                m = etype == r
                s = jax.ops.segment_sum(jnp.where(m[:, None], msg, 0.0), dst, num_segments=n)
                c = jax.ops.segment_sum(m.astype(x.dtype), dst, num_segments=n)
                out = out + s / jnp.maximum(c, 1.0)[:, None]
            return out

        def _gate(h, q, Wg, bg, Wq, bq):
            B, L, F = q.shape
            N = h.shape[0] // B
            h3 = h.reshape(B, N, F)
            hg = jnp.einsum('bnf,gf->bng', h3, Wg[:, :F])
            qg = jnp.einsum('blf,gf->blg', q, Wg[:, F:]) + bg
            attn = jax.nn.sigmoid(hg[:, :, None, :] + qg[:, None, :, :])
            qi = jnp.einsum('bnlf,blf->bnf', attn, q)
            alpha = jax.nn.sigmoid(jnp.einsum('bnf,gf->bng', h3, Wq[:, :F]) + jnp.einsum('bnf,gf->bng', qi, Wq[:, F:]) + bq)
            hn = alpha * jnp.tanh(qi) + (1.0 - alpha) * h3
            return hn.reshape(B * N, F)
        key = jax.random.key(seed)
        ks = jax.random.split(key, 16)
        F = 768
        BN, E, B, L = (256, 8192, 8, 64)
        s = 0.02
        return {'x': jax.random.normal(ks[0], (BN, F), jnp.float32), 'edge_index': jax.random.randint(ks[1], (2, E), 0, BN), 'edge_type': jax.random.randint(ks[2], (E,), 0, NUM_RELATIONS), 'query_embs': jax.random.normal(ks[3], (B, L, F), jnp.float32), 'W_rel1': jax.random.normal(ks[4], (NUM_RELATIONS, F, F), jnp.float32) * s, 'W_root1': jax.random.normal(ks[5], (F, F), jnp.float32) * s, 'b1': jnp.zeros((F,), jnp.float32), 'W_rel2': jax.random.normal(ks[6], (NUM_RELATIONS, F, F), jnp.float32) * s, 'W_root2': jax.random.normal(ks[7], (F, F), jnp.float32) * s, 'b2': jnp.zeros((F,), jnp.float32), 'Wg': jax.random.normal(ks[8], (F, 2 * F), jnp.float32) * s, 'bg': jnp.zeros((F,), jnp.float32), 'Wq': jax.random.normal(ks[9], (F, 2 * F), jnp.float32) * s, 'bq': jnp.zeros((F,), jnp.float32)}
    _L0_gnn_all = _L0_gnn_setup()
    _L0_gnn_in = {k: v for k, v in _L0_gnn_all.items() if k in ('query_embs', 'W_rel1', 'W_root1', 'b1', 'W_rel2', 'W_root2', 'b2', 'Wg', 'bg', 'Wq', 'bq')}
    del _L0_gnn_all

    def _L0_mix_setup():
        import jax, jax.numpy as jnp
        import numpy as np
        DIM = 768
        NUM_HEADS = 12
        HEAD_DIM = DIM // NUM_HEADS
        HIDDEN = int(DIM * 4.0)
        EPS = 1e-08

        def layer_norm(x, w, b):
            mu = jnp.mean(x, axis=-1, keepdims=True)
            var = jnp.mean(jnp.square(x - mu), axis=-1, keepdims=True)
            return (x - mu) * jax.lax.rsqrt(var + EPS) * w + b

        def linear_attention(x, qkv_w, qkv_b, proj_w, proj_b):
            B, N, C = x.shape
            qkv = (x @ qkv_w + qkv_b).reshape(B, N, 3, NUM_HEADS, HEAD_DIM)
            qkv = qkv.transpose(2, 0, 3, 1, 4)
            q, k, v = (qkv[0], qkv[1], qkv[2])
            q = jax.nn.elu(q) + 1.0
            k = jax.nn.elu(k) + 1.0
            kv = jnp.einsum('bhsd,bhse->bhde', k, v)
            z = 1.0 / jnp.einsum('bhsd,bhd->bhs', q, k.sum(axis=-2))
            out = jnp.einsum('bhde,bhsd,bhs->bhse', kv, q, z)
            out = out.transpose(0, 2, 1, 3).reshape(B, N, C)
            return out @ proj_w + proj_b
        key = jax.random.key(seed)
        ks = jax.random.split(key, 10)
        s = 0.02
        return {'x': jax.random.normal(ks[0], (16, 512, DIM), dtype=jnp.float32), 'qkv_w': jax.random.normal(ks[1], (DIM, 3 * DIM), dtype=jnp.float32) * s, 'qkv_b': jnp.zeros((3 * DIM,), dtype=jnp.float32), 'proj_w': jax.random.normal(ks[2], (DIM, DIM), dtype=jnp.float32) * s, 'proj_b': jnp.zeros((DIM,), dtype=jnp.float32), 'fc1_w': jax.random.normal(ks[3], (DIM, HIDDEN), dtype=jnp.float32) * s, 'fc1_b': jnp.zeros((HIDDEN,), dtype=jnp.float32), 'fc2_w': jax.random.normal(ks[4], (HIDDEN, DIM), dtype=jnp.float32) * s, 'fc2_b': jnp.zeros((DIM,), dtype=jnp.float32), 'ln1_w': jnp.ones((DIM,), dtype=jnp.float32), 'ln1_b': jnp.zeros((DIM,), dtype=jnp.float32), 'ln2_w': jnp.ones((DIM,), dtype=jnp.float32), 'ln2_b': jnp.zeros((DIM,), dtype=jnp.float32)}
    _L0_mix_all = _L0_mix_setup()
    _L0_mix_in = {k: v for k, v in _L0_mix_all.items() if k in ('qkv_w', 'qkv_b', 'proj_w', 'proj_b', 'fc1_w', 'fc1_b', 'fc2_w', 'fc2_b', 'ln1_w', 'ln1_b', 'ln2_w', 'ln2_b')}
    del _L0_mix_all

    def _L0_ffn_setup():
        import jax, jax.numpy as jnp
        import numpy as np
        D_MODEL = 768
        D_HID = 384
        NUM_EXPERTS = 8
        TOP_K = 2
        B, T = (1, 256)
        key = jax.random.key(seed)
        k0, k1, k2, k3 = jax.random.split(key, 4)
        x = jax.random.normal(k0, (B, T, D_MODEL), dtype=jnp.float32)
        gate_w = jax.random.normal(k1, (D_MODEL, NUM_EXPERTS), dtype=jnp.float32) * (1.0 / np.sqrt(D_MODEL))
        s1 = float(np.sqrt(2.0 / D_MODEL))
        s2 = float(np.sqrt(2.0 / D_HID))
        w1 = jax.random.normal(k2, (NUM_EXPERTS, D_MODEL, D_HID), dtype=jnp.float32) * s1
        w2 = jax.random.normal(k3, (NUM_EXPERTS, D_HID, D_MODEL), dtype=jnp.float32) * s2
        b1 = jnp.zeros((NUM_EXPERTS, 1, D_HID), dtype=jnp.float32)
        b2 = jnp.zeros((NUM_EXPERTS, 1, D_MODEL), dtype=jnp.float32)
        return {'x': x, 'gate_w': gate_w, 'w1': w1, 'b1': b1, 'w2': w2, 'b2': b2}
    _L0_ffn_all = _L0_ffn_setup()
    _L0_ffn_in = {k: v for k, v in _L0_ffn_all.items() if k in ('gate_w', 'w1', 'b1', 'w2', 'b2')}
    del _L0_ffn_all

    def _L1_gnn_setup():
        import jax, jax.numpy as jnp
        import numpy as np
        N_NODES = 1250
        N_EDGES = 12500
        DIM = 768
        key = jax.random.key(seed)
        k1, k2, k3, k4 = jax.random.split(key, 4)
        x = jax.random.normal(k1, (N_NODES, DIM), dtype=jnp.float32)
        edge_index = jax.random.randint(k2, (2, N_EDGES), 0, N_NODES, dtype=jnp.int32)
        W = jax.random.normal(k3, (DIM, DIM), dtype=jnp.float32) / np.sqrt(DIM)
        b = jnp.zeros((DIM,), dtype=jnp.float32)
        return {'x': x, 'edge_index': edge_index, 'W': W, 'b': b}
    _L1_gnn_all = _L1_gnn_setup()
    _L1_gnn_in = {k: v for k, v in _L1_gnn_all.items() if k in ('W', 'b')}
    del _L1_gnn_all

    def _L1_mix_setup():
        import jax, jax.numpy as jnp
        import numpy as np
        B, N, C = (8, 512, 768)
        H, HD = (12, 64)
        M = HD * 2
        LAM = 0.3
        NUM_STEP = 5

        def _soft(z, t):
            return jnp.sign(z) * jax.nn.relu(jnp.abs(z) - t)
        key = jax.random.key(seed)
        k1, k2, k3, k4 = jax.random.split(key, 4)
        x = jax.random.normal(k1, (B, N, C), dtype=jnp.float32)
        Wqkv = jax.random.normal(k2, (C, 2 * C), dtype=jnp.float32) * 0.02
        Wproj = jax.random.normal(k3, (C, C), dtype=jnp.float32) * 0.02
        bproj = jnp.zeros((C,), dtype=jnp.float32)
        rand_matrix = jax.random.normal(k4, (H, HD, M), dtype=jnp.float32)
        return {'x': x, 'Wqkv': Wqkv, 'Wproj': Wproj, 'bproj': bproj, 'rand_matrix': rand_matrix}
    _L1_mix_all = _L1_mix_setup()
    _L1_mix_in = {k: v for k, v in _L1_mix_all.items() if k in ('Wqkv', 'Wproj', 'bproj', 'rand_matrix')}
    del _L1_mix_all

    def _L1_ffn_setup():
        import jax, jax.numpy as jnp
        import numpy as np
        B, L, D, H, F = (4, 256, 768, 12, 384)
        ROUTE_FRAC = 0.15
        LN_EPS = 1e-05

        def _ln(x, g, b):
            m = jnp.mean(x, axis=-1, keepdims=True)
            v = jnp.mean((x - m) ** 2, axis=-1, keepdims=True)
            return (x - m) * jax.lax.rsqrt(v + LN_EPS) * g + b
        key = jax.random.key(seed)
        ks = jax.random.split(key, 20)
        s = 0.02
        return {'hidden_states': jax.random.normal(ks[0], (B, L, D), dtype=jnp.float32), 'g1': jnp.ones((D,), jnp.float32), 'b1': jnp.zeros((D,), jnp.float32), 'g2': jnp.ones((D,), jnp.float32), 'b2': jnp.zeros((D,), jnp.float32), 'Wr': jax.random.normal(ks[1], (D,), jnp.float32) * s, 'br': jnp.zeros((), jnp.float32), 'Wq': jax.random.normal(ks[2], (D, D), jnp.float32) * s, 'bq': jnp.zeros((D,), jnp.float32), 'Wk': jax.random.normal(ks[3], (D, D), jnp.float32) * s, 'bk': jnp.zeros((D,), jnp.float32), 'Wv': jax.random.normal(ks[4], (D, D), jnp.float32) * s, 'bv': jnp.zeros((D,), jnp.float32), 'Wo': jax.random.normal(ks[5], (D, D), jnp.float32) * s, 'bo': jnp.zeros((D,), jnp.float32), 'Wm': jax.random.normal(ks[6], (D, D), jnp.float32) * s, 'bm': jnp.zeros((D,), jnp.float32), 'W1': jax.random.normal(ks[7], (D, F), jnp.float32) * s, 'bf1': jnp.zeros((F,), jnp.float32), 'W2': jax.random.normal(ks[8], (F, D), jnp.float32) * s, 'bf2': jnp.zeros((D,), jnp.float32)}
    _L1_ffn_all = _L1_ffn_setup()
    _L1_ffn_in = {k: v for k, v in _L1_ffn_all.items() if k in ('g1', 'b1', 'g2', 'b2', 'Wr', 'br', 'Wq', 'bq', 'Wk', 'bk', 'Wv', 'bv', 'Wo', 'bo', 'Wm', 'bm', 'W1', 'bf1', 'W2', 'bf2')}
    del _L1_ffn_all

    def _L2_gnn_setup():
        import jax, jax.numpy as jnp
        import numpy as np
        N_NODES = 1250
        N_EDGES = 12500
        DIM = 768
        NEG_SLOPE = 0.2

        def gat_conv(x, src, dst, W, att_src, att_dst, bias, num_nodes):
            h = x @ W
            a_s = h @ att_src
            a_d = h @ att_dst
            e = jax.nn.leaky_relu(a_s[src] + a_d[dst], NEG_SLOPE)
            m = jax.ops.segment_max(e, dst, num_segments=num_nodes)
            e = jnp.exp(e - m[dst])
            denom = jax.ops.segment_sum(e, dst, num_segments=num_nodes)
            alpha = e / denom[dst]
            msg = alpha[:, None] * h[src]
            out = jax.ops.segment_sum(msg, dst, num_segments=num_nodes)
            return out + bias
        key = jax.random.key(seed)
        ks = jax.random.split(key, 12)
        s = 1.0 / np.sqrt(DIM)
        inp = {'x': jax.random.normal(ks[0], (N_NODES, DIM), dtype=jnp.float32), 'edge_index': jax.random.randint(ks[1], (2, N_EDGES), 0, N_NODES, dtype=jnp.int64), 'W1': jax.random.normal(ks[2], (DIM, DIM), dtype=jnp.float32) * s, 'att_src1': jax.random.normal(ks[3], (DIM,), dtype=jnp.float32) * s, 'att_dst1': jax.random.normal(ks[4], (DIM,), dtype=jnp.float32) * s, 'b1': jnp.zeros((DIM,), dtype=jnp.float32), 'W2': jax.random.normal(ks[5], (DIM, DIM), dtype=jnp.float32) * s, 'att_src2': jax.random.normal(ks[6], (DIM,), dtype=jnp.float32) * s, 'att_dst2': jax.random.normal(ks[7], (DIM,), dtype=jnp.float32) * s, 'b2': jnp.zeros((DIM,), dtype=jnp.float32)}
        return inp
    _L2_gnn_all = _L2_gnn_setup()
    _L2_gnn_in = {k: v for k, v in _L2_gnn_all.items() if k in ('W1', 'att_src1', 'att_dst1', 'b1', 'W2', 'att_src2', 'att_dst2', 'b2')}
    del _L2_gnn_all

    def _L2_mix_setup():
        import jax, jax.numpy as jnp
        import numpy as np
        B, N, C = (16, 512, 768)
        H = 12
        D = C // H
        SCALE = D ** (-0.5)
        key = jax.random.key(seed)
        k1, k2, k3, k4 = jax.random.split(key, 4)
        x = jax.random.normal(k1, (B, N, C), dtype=jnp.float32)
        w_qkv = jax.random.normal(k2, (C, 3 * C), dtype=jnp.float32) * 0.02
        w_proj = jax.random.normal(k3, (C, C), dtype=jnp.float32) * 0.02
        b_proj = jax.random.normal(k4, (C,), dtype=jnp.float32) * 0.02
        return {'x': x, 'w_qkv': w_qkv, 'w_proj': w_proj, 'b_proj': b_proj}
    _L2_mix_all = _L2_mix_setup()
    _L2_mix_in = {k: v for k, v in _L2_mix_all.items() if k in ('w_qkv', 'w_proj', 'b_proj')}
    del _L2_mix_all

    def _L2_ffn_setup():
        import jax, jax.numpy as jnp
        import numpy as np
        DIM = 768
        H = 12
        HD = 64
        SHARED = 2
        ROUTED = 2
        E_ROUTED = H - SHARED
        LN_EPS = 1e-05

        def _layernorm(x, w, b):
            m = x.mean(-1, keepdims=True)
            v = ((x - m) ** 2).mean(-1, keepdims=True)
            return (x - m) * jax.lax.rsqrt(v + LN_EPS) * w + b
        key = jax.random.key(seed)
        ks = jax.random.split(key, 12)
        B, N = (4, 256)
        s = 0.02
        return {'x': jax.random.normal(ks[0], (B, N, DIM), jnp.float32), 'qkv_w': jax.random.normal(ks[1], (DIM, 3 * H * HD), jnp.float32) * s, 'qkv_b': jnp.zeros((3 * H * HD,), jnp.float32), 'q_norm_w': jnp.ones((HD,), jnp.float32), 'q_norm_b': jnp.zeros((HD,), jnp.float32), 'k_norm_w': jnp.ones((HD,), jnp.float32), 'k_norm_b': jnp.zeros((HD,), jnp.float32), 'wg_w': jax.random.normal(ks[2], (DIM, E_ROUTED), jnp.float32) * s, 'wg0_w': jax.random.normal(ks[3], (DIM, 2), jnp.float32) * s, 'wg1_w': jax.random.normal(ks[4], (DIM, SHARED), jnp.float32) * s, 'proj_w': jax.random.normal(ks[5], (H * HD, DIM), jnp.float32) * s, 'proj_b': jnp.zeros((DIM,), jnp.float32)}
    _L2_ffn_all = _L2_ffn_setup()
    _L2_ffn_in = {k: v for k, v in _L2_ffn_all.items() if k in ('qkv_w', 'qkv_b', 'q_norm_w', 'q_norm_b', 'k_norm_w', 'k_norm_b', 'wg_w', 'wg0_w', 'wg1_w', 'proj_w', 'proj_b')}
    del _L2_ffn_all

    def _L3_gnn_setup():
        import jax, jax.numpy as jnp
        import numpy as np
        N = 6250
        E = 31250
        H = 12
        D = 64
        NEG_SLOPE = 0.2
        key = jax.random.key(seed)
        k1, k2, k3, k4, k5, k6, k7 = jax.random.split(key, 7)
        h = jax.random.normal(k1, (N, H * D), dtype=jnp.float32)
        src = jnp.concatenate([jnp.arange(N, dtype=jnp.int32), jax.random.randint(k2, (E - N,), 0, N, dtype=jnp.int32)])
        dst = jnp.concatenate([jnp.arange(N, dtype=jnp.int32), jax.random.randint(k3, (E - N,), 0, N, dtype=jnp.int32)])
        xav = 1.414 / np.sqrt(D)
        W_fc = jax.random.normal(k4, (D, D), dtype=jnp.float32) * xav
        attn_l = jax.random.normal(k5, (H, D), dtype=jnp.float32) * 0.15
        attn_r = jax.random.normal(k6, (H, D), dtype=jnp.float32) * 0.15
        W_res = jax.random.normal(k7, (D, D), dtype=jnp.float32) * xav
        return {'h': h, 'W_fc': W_fc, 'attn_l': attn_l, 'attn_r': attn_r, 'W_res': W_res, 'src': src, 'dst': dst}
    _L3_gnn_all = _L3_gnn_setup()
    _L3_gnn_in = {k: v for k, v in _L3_gnn_all.items() if k in ('W_fc', 'attn_l', 'attn_r', 'W_res')}
    del _L3_gnn_all

    def _L3_mix_setup():
        import jax, jax.numpy as jnp
        import numpy as np
        DIM = 768
        NUM_HEADS = 12
        HEAD_DIM = DIM // NUM_HEADS
        SCALE = HEAD_DIM ** (-0.5)
        key = jax.random.key(seed)
        ks = jax.random.split(key, 5)
        B, N = (4, 1024)
        s = DIM ** (-0.5)
        return {'x': jax.random.normal(ks[0], (B, N, DIM), dtype=jnp.float32), 'w_qkv': jax.random.normal(ks[1], (DIM, 3 * DIM), dtype=jnp.float32) * s, 'b_qkv': jnp.zeros((3 * DIM,), dtype=jnp.float32), 'w_proj': jax.random.normal(ks[2], (DIM, DIM), dtype=jnp.float32) * s, 'b_proj': jnp.zeros((DIM,), dtype=jnp.float32)}
    _L3_mix_all = _L3_mix_setup()
    _L3_mix_in = {k: v for k, v in _L3_mix_all.items() if k in ('w_qkv', 'b_qkv', 'w_proj', 'b_proj')}
    del _L3_mix_all

    def _L3_ffn_setup():
        import jax, jax.numpy as jnp
        import numpy as np
        DIM = 768
        NUM_HEADS = 12
        HEAD_DIM = DIM // NUM_HEADS
        SCALE = HEAD_DIM ** (-0.5)
        NUM_EXPERTS = 8
        RANK = 16
        ALPHA = 32
        TOPK = 2
        SCALING = ALPHA / RANK
        B, S = (8, 1024)
        key = jax.random.key(seed)
        ks = jax.random.split(key, 12)
        d, e, r = (DIM, NUM_EXPERTS, RANK)
        inp = {'x': jax.random.normal(ks[0], (B, S, d), jnp.float32), 'Wg': jax.random.normal(ks[1], (e, d), jnp.float32) * 0.02, 'bg': jax.random.normal(ks[2], (e,), jnp.float32) * 0.02, 'Wqkv': jax.random.normal(ks[3], (3 * d, d), jnp.float32) * 0.02, 'bqkv': jax.random.normal(ks[4], (3 * d,), jnp.float32) * 0.02, 'Wproj': jax.random.normal(ks[5], (d, d), jnp.float32) * 0.02, 'bproj': jax.random.normal(ks[6], (d,), jnp.float32) * 0.02, 'A': jax.random.normal(ks[7], (e, r, d), jnp.float32) * 0.05, 'ba': jax.random.normal(ks[8], (e, r), jnp.float32) * 0.02, 'Bm': jax.random.normal(ks[9], (e, 3 * d, r), jnp.float32) * 0.05, 'bb': jax.random.normal(ks[10], (e, 3 * d), jnp.float32) * 0.02}
        return inp
    _L3_ffn_all = _L3_ffn_setup()
    _L3_ffn_in = {k: v for k, v in _L3_ffn_all.items() if k in ('Wg', 'bg', 'Wqkv', 'bqkv', 'Wproj', 'bproj', 'A', 'ba', 'Bm', 'bb')}
    del _L3_ffn_all
    return {'x': x, 'src': src, 'dst': dst, 'edge_type_3': edge_type_3, 'L0_gnn_query_embs': _L0_gnn_in['query_embs'], 'L0_gnn_W_rel1': _L0_gnn_in['W_rel1'], 'L0_gnn_W_root1': _L0_gnn_in['W_root1'], 'L0_gnn_b1': _L0_gnn_in['b1'], 'L0_gnn_W_rel2': _L0_gnn_in['W_rel2'], 'L0_gnn_W_root2': _L0_gnn_in['W_root2'], 'L0_gnn_b2': _L0_gnn_in['b2'], 'L0_gnn_Wg': _L0_gnn_in['Wg'], 'L0_gnn_bg': _L0_gnn_in['bg'], 'L0_gnn_Wq': _L0_gnn_in['Wq'], 'L0_gnn_bq': _L0_gnn_in['bq'], 'L0_mix_qkv_w': _L0_mix_in['qkv_w'], 'L0_mix_qkv_b': _L0_mix_in['qkv_b'], 'L0_mix_proj_w': _L0_mix_in['proj_w'], 'L0_mix_proj_b': _L0_mix_in['proj_b'], 'L0_mix_fc1_w': _L0_mix_in['fc1_w'], 'L0_mix_fc1_b': _L0_mix_in['fc1_b'], 'L0_mix_fc2_w': _L0_mix_in['fc2_w'], 'L0_mix_fc2_b': _L0_mix_in['fc2_b'], 'L0_mix_ln1_w': _L0_mix_in['ln1_w'], 'L0_mix_ln1_b': _L0_mix_in['ln1_b'], 'L0_mix_ln2_w': _L0_mix_in['ln2_w'], 'L0_mix_ln2_b': _L0_mix_in['ln2_b'], 'L0_ffn_gate_w': _L0_ffn_in['gate_w'], 'L0_ffn_w1': _L0_ffn_in['w1'], 'L0_ffn_b1': _L0_ffn_in['b1'], 'L0_ffn_w2': _L0_ffn_in['w2'], 'L0_ffn_b2': _L0_ffn_in['b2'], 'L1_gnn_W': _L1_gnn_in['W'], 'L1_gnn_b': _L1_gnn_in['b'], 'L1_mix_Wqkv': _L1_mix_in['Wqkv'], 'L1_mix_Wproj': _L1_mix_in['Wproj'], 'L1_mix_bproj': _L1_mix_in['bproj'], 'L1_mix_rand_matrix': _L1_mix_in['rand_matrix'], 'L1_ffn_g1': _L1_ffn_in['g1'], 'L1_ffn_b1': _L1_ffn_in['b1'], 'L1_ffn_g2': _L1_ffn_in['g2'], 'L1_ffn_b2': _L1_ffn_in['b2'], 'L1_ffn_Wr': _L1_ffn_in['Wr'], 'L1_ffn_br': _L1_ffn_in['br'], 'L1_ffn_Wq': _L1_ffn_in['Wq'], 'L1_ffn_bq': _L1_ffn_in['bq'], 'L1_ffn_Wk': _L1_ffn_in['Wk'], 'L1_ffn_bk': _L1_ffn_in['bk'], 'L1_ffn_Wv': _L1_ffn_in['Wv'], 'L1_ffn_bv': _L1_ffn_in['bv'], 'L1_ffn_Wo': _L1_ffn_in['Wo'], 'L1_ffn_bo': _L1_ffn_in['bo'], 'L1_ffn_Wm': _L1_ffn_in['Wm'], 'L1_ffn_bm': _L1_ffn_in['bm'], 'L1_ffn_W1': _L1_ffn_in['W1'], 'L1_ffn_bf1': _L1_ffn_in['bf1'], 'L1_ffn_W2': _L1_ffn_in['W2'], 'L1_ffn_bf2': _L1_ffn_in['bf2'], 'L2_gnn_W1': _L2_gnn_in['W1'], 'L2_gnn_att_src1': _L2_gnn_in['att_src1'], 'L2_gnn_att_dst1': _L2_gnn_in['att_dst1'], 'L2_gnn_b1': _L2_gnn_in['b1'], 'L2_gnn_W2': _L2_gnn_in['W2'], 'L2_gnn_att_src2': _L2_gnn_in['att_src2'], 'L2_gnn_att_dst2': _L2_gnn_in['att_dst2'], 'L2_gnn_b2': _L2_gnn_in['b2'], 'L2_mix_w_qkv': _L2_mix_in['w_qkv'], 'L2_mix_w_proj': _L2_mix_in['w_proj'], 'L2_mix_b_proj': _L2_mix_in['b_proj'], 'L2_ffn_qkv_w': _L2_ffn_in['qkv_w'], 'L2_ffn_qkv_b': _L2_ffn_in['qkv_b'], 'L2_ffn_q_norm_w': _L2_ffn_in['q_norm_w'], 'L2_ffn_q_norm_b': _L2_ffn_in['q_norm_b'], 'L2_ffn_k_norm_w': _L2_ffn_in['k_norm_w'], 'L2_ffn_k_norm_b': _L2_ffn_in['k_norm_b'], 'L2_ffn_wg_w': _L2_ffn_in['wg_w'], 'L2_ffn_wg0_w': _L2_ffn_in['wg0_w'], 'L2_ffn_wg1_w': _L2_ffn_in['wg1_w'], 'L2_ffn_proj_w': _L2_ffn_in['proj_w'], 'L2_ffn_proj_b': _L2_ffn_in['proj_b'], 'L3_gnn_W_fc': _L3_gnn_in['W_fc'], 'L3_gnn_attn_l': _L3_gnn_in['attn_l'], 'L3_gnn_attn_r': _L3_gnn_in['attn_r'], 'L3_gnn_W_res': _L3_gnn_in['W_res'], 'L3_mix_w_qkv': _L3_mix_in['w_qkv'], 'L3_mix_b_qkv': _L3_mix_in['b_qkv'], 'L3_mix_w_proj': _L3_mix_in['w_proj'], 'L3_mix_b_proj': _L3_mix_in['b_proj'], 'L3_ffn_Wg': _L3_ffn_in['Wg'], 'L3_ffn_bg': _L3_ffn_in['bg'], 'L3_ffn_Wqkv': _L3_ffn_in['Wqkv'], 'L3_ffn_bqkv': _L3_ffn_in['bqkv'], 'L3_ffn_Wproj': _L3_ffn_in['Wproj'], 'L3_ffn_bproj': _L3_ffn_in['bproj'], 'L3_ffn_A': _L3_ffn_in['A'], 'L3_ffn_ba': _L3_ffn_in['ba'], 'L3_ffn_Bm': _L3_ffn_in['Bm'], 'L3_ffn_bb': _L3_ffn_in['bb']}

def reference(x, src, dst, edge_type_3, L0_gnn_query_embs, L0_gnn_W_rel1, L0_gnn_W_root1, L0_gnn_b1, L0_gnn_W_rel2, L0_gnn_W_root2, L0_gnn_b2, L0_gnn_Wg, L0_gnn_bg, L0_gnn_Wq, L0_gnn_bq, L0_mix_qkv_w, L0_mix_qkv_b, L0_mix_proj_w, L0_mix_proj_b, L0_mix_fc1_w, L0_mix_fc1_b, L0_mix_fc2_w, L0_mix_fc2_b, L0_mix_ln1_w, L0_mix_ln1_b, L0_mix_ln2_w, L0_mix_ln2_b, L0_ffn_gate_w, L0_ffn_w1, L0_ffn_b1, L0_ffn_w2, L0_ffn_b2, L1_gnn_W, L1_gnn_b, L1_mix_Wqkv, L1_mix_Wproj, L1_mix_bproj, L1_mix_rand_matrix, L1_ffn_g1, L1_ffn_b1, L1_ffn_g2, L1_ffn_b2, L1_ffn_Wr, L1_ffn_br, L1_ffn_Wq, L1_ffn_bq, L1_ffn_Wk, L1_ffn_bk, L1_ffn_Wv, L1_ffn_bv, L1_ffn_Wo, L1_ffn_bo, L1_ffn_Wm, L1_ffn_bm, L1_ffn_W1, L1_ffn_bf1, L1_ffn_W2, L1_ffn_bf2, L2_gnn_W1, L2_gnn_att_src1, L2_gnn_att_dst1, L2_gnn_b1, L2_gnn_W2, L2_gnn_att_src2, L2_gnn_att_dst2, L2_gnn_b2, L2_mix_w_qkv, L2_mix_w_proj, L2_mix_b_proj, L2_ffn_qkv_w, L2_ffn_qkv_b, L2_ffn_q_norm_w, L2_ffn_q_norm_b, L2_ffn_k_norm_w, L2_ffn_k_norm_b, L2_ffn_wg_w, L2_ffn_wg0_w, L2_ffn_wg1_w, L2_ffn_proj_w, L2_ffn_proj_b, L3_gnn_W_fc, L3_gnn_attn_l, L3_gnn_attn_r, L3_gnn_W_res, L3_mix_w_qkv, L3_mix_b_qkv, L3_mix_w_proj, L3_mix_b_proj, L3_ffn_Wg, L3_ffn_bg, L3_ffn_Wqkv, L3_ffn_bqkv, L3_ffn_Wproj, L3_ffn_bproj, L3_ffn_A, L3_ffn_ba, L3_ffn_Bm, L3_ffn_bb):
    import jax
    import jax.numpy as jnp

    def _L0_gnn_ref(x, edge_index, edge_type, query_embs, W_rel1, W_root1, b1, W_rel2, W_root2, b2, Wg, bg, Wq, bq):
        import jax, jax.numpy as jnp
        import numpy as np
        NUM_RELATIONS = 3

        def _rgcn(x, W_rel, W_root, bias, src, dst, etype):
            n = x.shape[0]
            xr = jnp.einsum('ni,rio->rno', x, W_rel)
            msg = xr[etype, src]
            out = x @ W_root + bias
            for r in range(NUM_RELATIONS):
                m = etype == r
                s = jax.ops.segment_sum(jnp.where(m[:, None], msg, 0.0), dst, num_segments=n)
                c = jax.ops.segment_sum(m.astype(x.dtype), dst, num_segments=n)
                out = out + s / jnp.maximum(c, 1.0)[:, None]
            return out

        def _gate(h, q, Wg, bg, Wq, bq):
            B, L, F = q.shape
            N = h.shape[0] // B
            h3 = h.reshape(B, N, F)
            hg = jnp.einsum('bnf,gf->bng', h3, Wg[:, :F])
            qg = jnp.einsum('blf,gf->blg', q, Wg[:, F:]) + bg
            attn = jax.nn.sigmoid(hg[:, :, None, :] + qg[:, None, :, :])
            qi = jnp.einsum('bnlf,blf->bnf', attn, q)
            alpha = jax.nn.sigmoid(jnp.einsum('bnf,gf->bng', h3, Wq[:, :F]) + jnp.einsum('bnf,gf->bng', qi, Wq[:, F:]) + bq)
            hn = alpha * jnp.tanh(qi) + (1.0 - alpha) * h3
            return hn.reshape(B * N, F)
        src, dst = (edge_index[0], edge_index[1])
        h = jax.nn.relu(_rgcn(x, W_rel1, W_root1, b1, src, dst, edge_type))
        h = _gate(h, query_embs, Wg, bg, Wq, bq)
        h = jax.nn.relu(_rgcn(h, W_rel2, W_root2, b2, src, dst, edge_type))
        h = _gate(h, query_embs, Wg, bg, Wq, bq)
        return h

    def _L0_mix_ref(x, qkv_w, qkv_b, proj_w, proj_b, fc1_w, fc1_b, fc2_w, fc2_b, ln1_w, ln1_b, ln2_w, ln2_b):
        import jax, jax.numpy as jnp
        import numpy as np
        DIM = 768
        NUM_HEADS = 12
        HEAD_DIM = DIM // NUM_HEADS
        HIDDEN = int(DIM * 4.0)
        EPS = 1e-08

        def layer_norm(x, w, b):
            mu = jnp.mean(x, axis=-1, keepdims=True)
            var = jnp.mean(jnp.square(x - mu), axis=-1, keepdims=True)
            return (x - mu) * jax.lax.rsqrt(var + EPS) * w + b

        def linear_attention(x, qkv_w, qkv_b, proj_w, proj_b):
            B, N, C = x.shape
            qkv = (x @ qkv_w + qkv_b).reshape(B, N, 3, NUM_HEADS, HEAD_DIM)
            qkv = qkv.transpose(2, 0, 3, 1, 4)
            q, k, v = (qkv[0], qkv[1], qkv[2])
            q = jax.nn.elu(q) + 1.0
            k = jax.nn.elu(k) + 1.0
            kv = jnp.einsum('bhsd,bhse->bhde', k, v)
            z = 1.0 / jnp.einsum('bhsd,bhd->bhs', q, k.sum(axis=-2))
            out = jnp.einsum('bhde,bhsd,bhs->bhse', kv, q, z)
            out = out.transpose(0, 2, 1, 3).reshape(B, N, C)
            return out @ proj_w + proj_b
        y = linear_attention(layer_norm(x, ln1_w, ln1_b), qkv_w, qkv_b, proj_w, proj_b)
        x = x + y
        h = layer_norm(x, ln2_w, ln2_b)
        h = jax.nn.gelu(h @ fc1_w + fc1_b, approximate=False) @ fc2_w + fc2_b
        return x + h

    def _L0_ffn_ref(x, gate_w, w1, b1, w2, b2):
        import jax, jax.numpy as jnp
        import numpy as np
        D_MODEL = 768
        D_HID = 384
        NUM_EXPERTS = 8
        TOP_K = 2
        B, T = (1, 256)
        "MoE FFN: top-k router, per-expert GELU FFN, weighted combine.\n\n            Math identical to the torch sort/pad/bmm/scatter-add path: each token's\n            output is sum over its top-k experts of (normalized weight) * FFN_e(x).\n            Expressed here as a dense dispatch (combine matrix [N, E]) which is\n            jit-friendly (static shapes) and exactly equivalent since padded slots /\n            unrouted (token, expert) pairs carry zero combine weight.\n            "
        Bx, Tx, D = x.shape
        E = w1.shape[0]
        xf = x.reshape(-1, D)
        router_logits = xf @ gate_w
        scores = jax.nn.softmax(router_logits, axis=-1)
        topk_w, topk_idx = jax.lax.top_k(scores, TOP_K)
        topk_w = topk_w / jnp.sum(topk_w, axis=-1, keepdims=True)
        combine = jnp.einsum('nk,nke->ne', topk_w, jax.nn.one_hot(topk_idx, E, dtype=xf.dtype))
        h = jnp.einsum('nd,edh->enh', xf, w1) + b1
        h = jax.nn.gelu(h, approximate=False)
        y = jnp.einsum('enh,ehd->end', h, w2) + b2
        out = jnp.einsum('ne,end->nd', combine, y)
        return out.reshape(Bx, Tx, D)

    def _L1_gnn_ref(x, edge_index, W, b):
        import jax, jax.numpy as jnp
        import numpy as np
        N_NODES = 1250
        N_EDGES = 12500
        DIM = 768
        n = x.shape[0]
        loop = jnp.arange(n, dtype=edge_index.dtype)
        src = jnp.concatenate([edge_index[0], loop])
        dst = jnp.concatenate([edge_index[1], loop])
        deg = jax.ops.segment_sum(jnp.ones_like(dst, dtype=x.dtype), dst, num_segments=n)
        deg_inv_sqrt = jnp.where(deg > 0, jax.lax.rsqrt(deg), 0.0)
        norm = deg_inv_sqrt[src] * deg_inv_sqrt[dst]
        h = x @ W
        msg = h[src] * norm[:, None]
        out = jax.ops.segment_sum(msg, dst, num_segments=n)
        return out + b

    def _L1_mix_ref(x, Wqkv, Wproj, bproj, rand_matrix):
        import jax, jax.numpy as jnp
        import numpy as np
        B, N, C = (8, 512, 768)
        H, HD = (12, 64)
        M = HD * 2
        LAM = 0.3
        NUM_STEP = 5

        def _soft(z, t):
            return jnp.sign(z) * jax.nn.relu(jnp.abs(z) - t)
        Bn, Nn, Cn = x.shape
        Hh, hd, m = rand_matrix.shape
        scale = hd ** (-0.5)
        qkv = x @ Wqkv
        q = qkv[..., :Cn].reshape(Bn, Nn, Hh, hd).transpose(0, 2, 1, 3)
        v = qkv[..., Cn:].reshape(Bn, Nn, Hh, hd).transpose(0, 2, 1, 3)
        qs = q * scale ** 0.5
        rf = jnp.exp(jnp.einsum('bhnd,hdm->bhnm', qs, rand_matrix) - 0.5 * jnp.sum(qs * qs, axis=-1, keepdims=True)) / m ** 0.5
        qn = rf / jnp.maximum(jnp.linalg.norm(rf, axis=-2, keepdims=True), 1e-12)
        kk = jnp.einsum('bhnm,bhnp->bhmp', qn, qn)
        kv = jnp.einsum('bhnm,bhnd->bhmd', qn, v)
        L = jax.lax.stop_gradient(jnp.max(jnp.sum(jnp.abs(kk), axis=-1), axis=-1))[..., None, None] + 1.0
        s = _soft(kv, LAM)
        for _ in range(NUM_STEP):
            s = _soft(s - (kk @ s - kv) / L, LAM / L)
        out = jnp.einsum('bhnm,bhmd->bhnd', qn, s)
        out = out.transpose(0, 2, 1, 3).reshape(Bn, Nn, Cn)
        return out @ Wproj + bproj

    def _L1_ffn_ref(hidden_states, g1, b1, g2, b2, Wr, br, Wq, bq, Wk, bk, Wv, bv, Wo, bo, Wm, bm, W1, bf1, W2, bf2):
        import jax, jax.numpy as jnp
        import numpy as np
        B, L, D, H, F = (4, 256, 768, 12, 384)
        ROUTE_FRAC = 0.15
        LN_EPS = 1e-05

        def _ln(x, g, b):
            m = jnp.mean(x, axis=-1, keepdims=True)
            v = jnp.mean((x - m) ** 2, axis=-1, keepdims=True)
            return (x - m) * jax.lax.rsqrt(v + LN_EPS) * g + b
        b, l, d = hidden_states.shape
        dh = d // H
        normed = _ln(hidden_states, g1, b1)
        scores = jax.nn.sigmoid(jnp.einsum('bld,d->bl', normed, Wr) + br)
        k = max(1, int(round(ROUTE_FRAC * l)))
        _, idx = jax.lax.top_k(-scores, k)
        attn_mask = jnp.zeros((b, l), bool).at[jnp.arange(b)[:, None], idx].set(True)
        q = (normed @ Wq + bq).reshape(b, l, H, dh)
        kk = (normed @ Wk + bk).reshape(b, l, H, dh)
        v = (normed @ Wv + bv).reshape(b, l, H, dh)
        logits = jnp.einsum('blhd,bmhd->bhlm', q, kk) / jnp.sqrt(jnp.float32(dh))
        probs = jax.nn.softmax(logits, axis=-1)
        ctx = jnp.einsum('bhlm,bmhd->blhd', probs, v).reshape(b, l, d)
        attn_out = ctx @ Wo + bo
        w = scores / (jnp.sum(scores, axis=1, keepdims=True) + 1e-06)
        pooled = jnp.einsum('bl,bld->bd', w, normed)
        mix_out = (normed + scores[..., None] * pooled[:, None, :]) @ Wm + bm
        merged = jnp.where(attn_mask[..., None], attn_out, mix_out)
        h = hidden_states + merged
        n2 = _ln(h, g2, b2)
        ffn = jax.nn.gelu(n2 @ W1 + bf1, approximate=False) @ W2 + bf2
        return h + ffn

    def _L2_gnn_ref(x, edge_index, W1, att_src1, att_dst1, b1, W2, att_src2, att_dst2, b2):
        import jax, jax.numpy as jnp
        import numpy as np
        N_NODES = 1250
        N_EDGES = 12500
        DIM = 768
        NEG_SLOPE = 0.2

        def gat_conv(x, src, dst, W, att_src, att_dst, bias, num_nodes):
            h = x @ W
            a_s = h @ att_src
            a_d = h @ att_dst
            e = jax.nn.leaky_relu(a_s[src] + a_d[dst], NEG_SLOPE)
            m = jax.ops.segment_max(e, dst, num_segments=num_nodes)
            e = jnp.exp(e - m[dst])
            denom = jax.ops.segment_sum(e, dst, num_segments=num_nodes)
            alpha = e / denom[dst]
            msg = alpha[:, None] * h[src]
            out = jax.ops.segment_sum(msg, dst, num_segments=num_nodes)
            return out + bias
        n = x.shape[0]
        loops = jnp.arange(n, dtype=edge_index.dtype)
        src = jnp.concatenate([edge_index[0], loops])
        dst = jnp.concatenate([edge_index[1], loops])
        h = gat_conv(x, src, dst, W1, att_src1, att_dst1, b1, n)
        h = jax.nn.relu(h)
        out = gat_conv(h, src, dst, W2, att_src2, att_dst2, b2, n)
        return out

    def _L2_mix_ref(x, w_qkv, w_proj, b_proj):
        import jax, jax.numpy as jnp
        import numpy as np
        B, N, C = (16, 512, 768)
        H = 12
        D = C // H
        SCALE = D ** (-0.5)
        b, n, c = x.shape
        qkv = (x @ w_qkv).reshape(b, n, 3, H, D).transpose(2, 0, 3, 1, 4)
        q, k, v = (qkv[0], qkv[1], qkv[2])
        kv = jnp.einsum('bhnd,bhne->bhde', k, v) * SCALE
        gq = jax.nn.gelu(q, approximate=False)
        gkv = jax.nn.gelu(kv, approximate=False)
        out = jnp.einsum('bhtd,bhde->bhte', gq, gkv)
        out = out.transpose(0, 2, 1, 3).reshape(b, n, c)
        return out @ w_proj + b_proj

    def _L2_ffn_ref(x, qkv_w, qkv_b, q_norm_w, q_norm_b, k_norm_w, k_norm_b, wg_w, wg0_w, wg1_w, proj_w, proj_b):
        import jax, jax.numpy as jnp
        import numpy as np
        DIM = 768
        H = 12
        HD = 64
        SHARED = 2
        ROUTED = 2
        E_ROUTED = H - SHARED
        LN_EPS = 1e-05

        def _layernorm(x, w, b):
            m = x.mean(-1, keepdims=True)
            v = ((x - m) ** 2).mean(-1, keepdims=True)
            return (x - m) * jax.lax.rsqrt(v + LN_EPS) * w + b
        B, N, C = x.shape
        scale = HD ** (-0.5)
        gates = jax.nn.softmax(x @ wg_w, axis=-1)
        _, idx = jax.lax.top_k(gates, ROUTED)
        mask = jax.nn.one_hot(idx, E_ROUTED, dtype=gates.dtype).sum(-2)
        rg = gates * mask
        denom = jnp.clip(rg.sum(-1, keepdims=True), jnp.finfo(rg.dtype).eps, None)
        routed_gates = rg / denom * ROUTED
        qkv = (x @ qkv_w + qkv_b).reshape(B, N, 3, H, HD)
        qkv = jnp.transpose(qkv, (2, 0, 3, 1, 4))
        q, k, v = (qkv[0], qkv[1], qkv[2])
        q = _layernorm(q, q_norm_w, q_norm_b)
        k = _layernorm(k, k_norm_w, k_norm_b)
        attn = jax.nn.softmax(jnp.einsum('bhqd,bhkd->bhqk', q * scale, k), axis=-1)
        o = jnp.einsum('bhqk,bhkd->bhqd', attn, v)
        o = jnp.transpose(o, (0, 2, 1, 3))
        shared_gates = jax.nn.softmax(x @ wg1_w, axis=-1) * SHARED
        w0 = jax.nn.softmax(x @ wg0_w, axis=-1) * 2.0
        shared_gates = w0[..., 0:1] * shared_gates
        routed_gates = w0[..., 1:2] * routed_gates
        masked_gates = jnp.concatenate([shared_gates, routed_gates], axis=-1)
        o = (masked_gates[..., None] * o).reshape(B, N, H * HD)
        return o @ proj_w + proj_b

    def _L3_gnn_ref(h, W_fc, attn_l, attn_r, W_res, src, dst):
        import jax, jax.numpy as jnp
        import numpy as np
        N = 6250
        E = 31250
        H = 12
        D = 64
        NEG_SLOPE = 0.2
        n = h.shape[0]
        hh = h.reshape(n, H, D)
        ft = jnp.einsum('nhd,ed->nhe', hh, W_fc)
        a1 = jnp.einsum('nhd,hd->nh', ft, attn_l)
        a2 = jnp.einsum('nhd,hd->nh', ft, attn_r)
        e = jax.nn.leaky_relu(a1[src] + a2[dst], negative_slope=NEG_SLOPE)
        m = jax.ops.segment_max(e, dst, num_segments=n)
        ee = jnp.exp(e - m[dst])
        denom = jax.ops.segment_sum(ee, dst, num_segments=n)
        alpha = ee / denom[dst]
        agg = jax.ops.segment_sum(alpha[:, :, None] * ft[src], dst, num_segments=n)
        res = jnp.einsum('nhd,ed->nhe', hh, W_res)
        return jax.nn.relu((res + agg).reshape(n, H * D))

    def _L3_mix_ref(x, w_qkv, b_qkv, w_proj, b_proj):
        import jax, jax.numpy as jnp
        import numpy as np
        DIM = 768
        NUM_HEADS = 12
        HEAD_DIM = DIM // NUM_HEADS
        SCALE = HEAD_DIM ** (-0.5)
        B, N, C = x.shape
        H, D = (NUM_HEADS, HEAD_DIM)
        qkv = x @ w_qkv + b_qkv
        qkv = qkv.reshape(B, N, 3, H, D).transpose(2, 0, 3, 1, 4)
        q, k, v = (qkv[0] * SCALE, qkv[1], qkv[2])
        A = jnp.einsum('bhnd,bhmd->bhnm', q, k)
        numerator = 1.0 + A + 0.5 * A * A
        attn = numerator / numerator.sum(axis=-1, keepdims=True)
        out = jnp.einsum('bhnm,bhmd->bhnd', attn, v)
        out = out.transpose(0, 2, 1, 3).reshape(B, N, C)
        return out @ w_proj + b_proj

    def _L3_ffn_ref(x, Wg, bg, Wqkv, bqkv, Wproj, bproj, A, ba, Bm, bb):
        import jax, jax.numpy as jnp
        import numpy as np
        DIM = 768
        NUM_HEADS = 12
        HEAD_DIM = DIM // NUM_HEADS
        SCALE = HEAD_DIM ** (-0.5)
        NUM_EXPERTS = 8
        RANK = 16
        ALPHA = 32
        TOPK = 2
        SCALING = ALPHA / RANK
        B, S = (8, 1024)
        b, s, d = x.shape
        t = b * s
        xf = x.reshape(t, d)
        probs = jax.nn.softmax(xf @ Wg.T + bg, axis=-1)
        top_w, top_idx = jax.lax.top_k(probs, TOPK)
        combine = jnp.zeros((t, NUM_EXPERTS), x.dtype).at[jnp.arange(t)[:, None], top_idx].add(top_w)
        h = jnp.einsum('td,erd->ter', xf, A) + ba
        hw = h * combine[:, :, None]
        delta = jnp.einsum('ter,eor->to', hw, Bm) + combine @ bb
        delta = delta * SCALING
        qkv = xf @ Wqkv.T + bqkv + delta
        qkv = qkv.reshape(b, s, 3, NUM_HEADS, HEAD_DIM)
        qkv = jnp.transpose(qkv, (2, 0, 3, 1, 4))
        q, k, v = (qkv[0], qkv[1], qkv[2])
        attn = jax.nn.softmax(jnp.einsum('bhsd,bhtd->bhst', q, k) * SCALE, axis=-1)
        out = jnp.einsum('bhst,bhtd->bhsd', attn, v)
        out = jnp.transpose(out, (0, 2, 1, 3)).reshape(b, s, d)
        return out @ Wproj.T + bproj
    edge_index = jnp.stack([src, dst])
    xn = _layernorm(x, axis=-1)
    x = x + _L0_gnn_ref(xn, edge_index, edge_type_3, L0_gnn_query_embs, L0_gnn_W_rel1, L0_gnn_W_root1, L0_gnn_b1, L0_gnn_W_rel2, L0_gnn_W_root2, L0_gnn_b2, L0_gnn_Wg, L0_gnn_bg, L0_gnn_Wq, L0_gnn_bq) + _L0_mix_ref(xn[None], L0_mix_qkv_w, L0_mix_qkv_b, L0_mix_proj_w, L0_mix_proj_b, L0_mix_fc1_w, L0_mix_fc1_b, L0_mix_fc2_w, L0_mix_fc2_b, L0_mix_ln1_w, L0_mix_ln1_b, L0_mix_ln2_w, L0_mix_ln2_b)[0]
    x = x + _L0_ffn_ref(_layernorm(x, axis=-1)[None], L0_ffn_gate_w, L0_ffn_w1, L0_ffn_b1, L0_ffn_w2, L0_ffn_b2)[0]
    xn = _layernorm(x, axis=-1)
    x = x + _L1_gnn_ref(xn, edge_index, L1_gnn_W, L1_gnn_b) + _L1_mix_ref(xn[None], L1_mix_Wqkv, L1_mix_Wproj, L1_mix_bproj, L1_mix_rand_matrix)[0]
    x = x + _L1_ffn_ref(_layernorm(x, axis=-1)[None], L1_ffn_g1, L1_ffn_b1, L1_ffn_g2, L1_ffn_b2, L1_ffn_Wr, L1_ffn_br, L1_ffn_Wq, L1_ffn_bq, L1_ffn_Wk, L1_ffn_bk, L1_ffn_Wv, L1_ffn_bv, L1_ffn_Wo, L1_ffn_bo, L1_ffn_Wm, L1_ffn_bm, L1_ffn_W1, L1_ffn_bf1, L1_ffn_W2, L1_ffn_bf2)[0]
    xn = _layernorm(x, axis=-1)
    x = x + _L2_gnn_ref(xn, edge_index, L2_gnn_W1, L2_gnn_att_src1, L2_gnn_att_dst1, L2_gnn_b1, L2_gnn_W2, L2_gnn_att_src2, L2_gnn_att_dst2, L2_gnn_b2) + _L2_mix_ref(xn[None], L2_mix_w_qkv, L2_mix_w_proj, L2_mix_b_proj)[0]
    x = x + _L2_ffn_ref(_layernorm(x, axis=-1)[None], L2_ffn_qkv_w, L2_ffn_qkv_b, L2_ffn_q_norm_w, L2_ffn_q_norm_b, L2_ffn_k_norm_w, L2_ffn_k_norm_b, L2_ffn_wg_w, L2_ffn_wg0_w, L2_ffn_wg1_w, L2_ffn_proj_w, L2_ffn_proj_b)[0]
    xn = _layernorm(x, axis=-1)
    x = x + _L3_gnn_ref(xn, L3_gnn_W_fc, L3_gnn_attn_l, L3_gnn_attn_r, L3_gnn_W_res, src, dst) + _L3_mix_ref(xn[None], L3_mix_w_qkv, L3_mix_b_qkv, L3_mix_w_proj, L3_mix_b_proj)[0]
    x = x + _L3_ffn_ref(_layernorm(x, axis=-1)[None], L3_ffn_Wg, L3_ffn_bg, L3_ffn_Wqkv, L3_ffn_bqkv, L3_ffn_Wproj, L3_ffn_bproj, L3_ffn_A, L3_ffn_ba, L3_ffn_Bm, L3_ffn_bb)[0]
    return x

_drawn_inputs = setup_inputs


def setup_inputs(seed=0):
    import zlib

    import numpy as np

    out = dict(_drawn_inputs(seed))
    spreads = {'L0_gnn_b1': (0.0, 0.3),
     'L0_gnn_b2': (0.0, 0.1),
     'L0_gnn_bg': (0.0, 0.1),
     'L0_gnn_bq': (0.0, 0.1),
     'L0_mix_qkv_b': (0.0, 0.1),
     'L0_mix_proj_b': (0.0, 0.1),
     'L0_mix_fc1_b': (0.0, 0.1),
     'L0_mix_fc2_b': (0.0, 0.1),
     'L0_mix_ln1_w': (1.0, 0.6),
     'L0_mix_ln1_b': (0.0, 0.1),
     'L0_mix_ln2_w': (1.0, 0.2),
     'L0_mix_ln2_b': (0.0, 0.1),
     'L0_ffn_b1': (0.0, 0.1),
     'L0_ffn_b2': (0.0, 0.1),
     'L1_gnn_b': (0.0, 0.1),
     'L1_mix_bproj': (0.0, 0.1),
     'L1_ffn_g1': (1.0, 0.2),
     'L1_ffn_b1': (0.0, 0.1),
     'L1_ffn_g2': (1.0, 0.6),
     'L1_ffn_b2': (0.0, 0.8),
     'L1_ffn_bq': (0.0, 0.8),
     'L1_ffn_bk': (0.0, 2.0),
     'L1_ffn_bv': (0.0, 0.8),
     'L1_ffn_bo': (0.0, 0.701),
     'L1_ffn_bm': (0.0, 0.1),
     'L1_ffn_bf1': (0.0, 0.793),
     'L1_ffn_bf2': (0.0, 0.1),
     'L2_gnn_b1': (0.0, 0.532),
     'L2_gnn_b2': (0.0, 0.298),
     'L2_ffn_qkv_b': (0.0, 0.8),
     'L2_ffn_q_norm_w': (1.0, 0.6),
     'L2_ffn_q_norm_b': (0.0, 0.8),
     'L2_ffn_k_norm_w': (1.0, 0.6),
     'L2_ffn_k_norm_b': (0.0, 2.0),
     'L2_ffn_proj_b': (0.0, 0.277),
     'L3_mix_b_qkv': (0.0, 0.313),
     'L3_mix_b_proj': (0.0, 0.306)}
    factors = {'L1_ffn_Wq': 8.0,
     'L1_ffn_Wk': 8.0,
     'L1_ffn_Wv': 5.948,
     'L1_ffn_Wo': 5.018,
     'L2_gnn_att_src1': 3.983,
     'L2_gnn_att_dst1': 8.0,
     'L2_gnn_att_src2': 8.0,
     'L2_gnn_att_dst2': 8.0,
     'L2_mix_b_proj': 8.0,
     'L2_ffn_qkv_w': 3.101,
     'L2_ffn_wg_w': 4.685,
     'L2_ffn_wg0_w': 8.0,
     'L2_ffn_wg1_w': 8.0,
     'L2_ffn_proj_w': 2.68,
     'L3_ffn_Wg': 8.0,
     'L3_ffn_bg': 8.0,
     'L3_ffn_bqkv': 8.0,
     'L3_ffn_bproj': 60.912,
     'L3_ffn_A': 8.0,
     'L3_ffn_ba': 8.0,
     'L3_ffn_Bm': 8.0,
     'L3_ffn_bb': 8.0}
    for name, (base, spread) in spreads.items():
        noise = np.random.default_rng([zlib.crc32(name.encode()), seed]).standard_normal(out[name].shape)
        drawn = base * np.exp(spread * noise) if base else spread * noise
        out[name] = jnp.asarray(drawn.astype(out[name].dtype))
    for name, factor in factors.items():
        out[name] = (out[name] * factor).astype(out[name].dtype)
    return out
```

```python
from contextlib import ExitStack

import numpy as np

import concourse.bass as bass
from concourse import mybir

ALU = mybir.AluOpType
ACT = mybir.ActivationFunctionType
AX = mybir.AxisListType
F32 = mybir.dt.float32
BF16 = mybir.dt.bfloat16
I32 = mybir.dt.int32

P = 128
N = 256
NT = N // P
D = 768
KC = D // P
H = 12
DH = D // H
COLS = 384
E = 4096
EC = E // P
R = 3
B, L = 8, 64
NB = N // B
UNIT = NT * D

PANELS = {}


def _plan_panels():
    at = 0
    for name, n in (("qg_w", 2), ("rel1", 8), ("hg_w", 2), ("alpha_w", 4), ("rel2", 8),
                    ("l0_qkv", 6), ("l0_proj", 2), ("l0_fc1", 8), ("l0_fc2", 8), ("l0_w1", 8), ("l0_w2", 8),
                    ("l1_gcn", 2), ("l1_q", 2), ("l1_v", 2), ("l1_proj", 2), ("l1_wq", 2), ("l1_wk", 2),
                    ("l1_wv", 2), ("l1_wo", 2), ("l1_wm", 2), ("l1_f1", 1), ("l1_f2", 1),
                    ("l2_gat1", 2), ("l2_gat2", 2), ("l2_q", 2), ("l2_kv", 4), ("l2_proj", 2), ("l2_qkv", 6),
                    ("l2_wo", 2), ("l3_qk", 4), ("l3_v", 2), ("l3_proj", 2), ("l3_wq", 2), ("l3_wk", 2),
                    ("l3_wv", 2), ("l3_wo", 2)):
        PANELS[name] = at
        at += n
    return at


N_PANELS = _plan_panels()

COLUMNS = {}
_names = [("b1", 6), ("b2", 6), ("bg", 6), ("bq", 6), ("l0_qb", 6), ("l0_fc1b", 24), ("ln1w", 6), ("ln1b", 6),
          ("ln2w", 6), ("ln2b", 6), ("l0_b1", 24), ("g1", 6), ("gb1", 6), ("g2", 6), ("gb2", 6), ("l1_bq", 6),
          ("l1_bk", 6), ("l1_bf1", 3), ("gat_b1", 6), ("qnw", 1), ("qnb", 1), ("knw", 1), ("knb", 1),
          ("l3_qb", 6), ("l3_kb", 6), ("l3_bqk", 12)]
_at = 0
for _name, _n in _names:
    COLUMNS[_name] = (_at, _n)
    _at += _n
N_COLUMNS = _at

ROWS = {name: i for i, name in enumerate(
    ["l0_kb", "l0_vb", "l0_projb", "l0_fc2b", "gcn_b", "l1_projb", "l1_bv", "l1_bo", "l1_bm", "l1_bf2",
     "att_s1", "att_d1", "att_s2", "att_d2", "gat_b2", "l2_projb", "l2_qb", "l2_kb", "l2_vb", "l2_bo",
     "attn_l", "attn_r", "l3_vb", "l3_projb", "l3_bv", "l3_bo"])}
NARROW = {"gate": (0, 8), "wr": (8, 1), "gates": (9, 14), "l3_gate": (23, 8)}
N_NARROW = 31
SHORT = {"ba": (0, 128), "bg": (128, 8), "br": (136, 1)}
N_SHORT = 137


class Signal:

    def __init__(self, sem):
        self.sem, self.planned, self.raised = sem, 0, 0

    def mark(self):
        self.planned += 1
        return Mark(self, self.planned)


class Mark:

    def __init__(self, owner, count):
        self.owner, self.count = owner, count

    @property
    def at(self):
        return self.owner.sem, self.count

    @property
    def by(self):
        assert self.count == self.owner.raised + 1, (self.count, self.owner.raised)
        self.owner.raised += 1
        return self.owner.sem, 1


class Tile:

    def __init__(self, ps, before, filled, drained):
        self.ps, self.before, self.filled, self.drained = ps, before, filled, drained


class Load:

    def __init__(self, ap, src, sem, count, before):
        self.ap, self.src, self.sem, self.count, self.before, self.freed = ap, src, sem, count, before, None

    @property
    def at(self):
        return self.sem, 16 * self.count


class Slots:

    def __init__(self, aps, sems):
        self.aps, self.sems, self.last, self.counts = aps, sems, [None] * len(aps), [0] * len(aps)


class Lane:

    def __init__(self, sem, name, banks, users, panel_slots, panels, row_slots, rows):
        self.banks, self.users, self.nbank = banks, users, 0
        self.panel_slots, self.panels, self.npanel = panel_slots, panels, 0
        self.row_slots, self.rows, self.nrow = row_slots, rows, 0
        self.filled = Signal(sem(f"{name}_products_ready"))
        self.drained = {w: Signal(sem(f"{name}_{full}_drained")) for w, full in (("V", "vector"), ("A", "scalar"))}
        self.done = {w: Signal(sem(f"{name}_{full}_done")) for w, full in
                     (("V", "vector"), ("A", "scalar"), ("T", "tensor"), ("P", "pool"))}
        self.chain = {w: [sem(f"{name}_{full}_step"), 0] for w, full in
                      (("V", "vector"), ("A", "scalar"), ("P", "pool"))}
        self.stages = []

    def tile(self, who=None):
        bank = self.banks[self.nbank % len(self.banks)]
        self.nbank += 1
        tile = Tile(bank[0], self.users[bank[1]], self.filled.mark(), None)
        self.users[bank[1]] = tile
        if who:
            self.drained_by(tile, who)
        return tile

    def drained_by(self, tile, who):
        tile.drained = self.drained[who].mark()

    def mark(self, who):
        return self.done[who].mark()

    def load(self, slots, which, src, shape=None):
        ap = slots.aps[which]
        if shape:
            ap = ap[0:shape[0], 0:shape[1]]
        slots.counts[which] += 1
        new = Load(ap, src, slots.sems[which], slots.counts[which], slots.last[which])
        slots.last[which] = new
        return new

    def panel(self, src, freed=None):
        which = self.panels[self.npanel % len(self.panels)]
        self.npanel += 1
        new = self.load(self.panel_slots, which, src)
        new.freed = freed
        return new

    def row(self, src, shape=None):
        which = self.rows[self.nrow % len(self.rows)]
        self.nrow += 1
        return self.load(self.row_slots, which, src, shape)

    def step(self, who, eng, ins):
        self.chain[who][1] += 1
        ins.then_inc(self.chain[who][0], 1)
        eng.wait_ge(self.chain[who][0], self.chain[who][1])


def fill(pe, tile):
    if tile.before is not None:
        pe.wait_ge(*tile.before.drained.at)


def wait_all(eng, marks):
    for m in marks:
        eng.wait_ge(*m.at)


class Stage:
    time = 5.0
    loads = ()

    def __init__(self, lane):
        self.lane = lane
        lane.stages.append(self)

    def t(self, pe):
        yield self.time

    def v(self, dve):
        yield self.time

    def a(self, act):
        yield self.time

    def p(self, pool):
        yield self.time

    def s(self, sp):
        for load in self.loads:
            if load.before is not None:
                sp.wait_ge(*load.before.freed.at)
            sp.dma_start(load.ap, load.src).then_inc(load.sem, 16)
            yield self.time / len(self.loads) if load.ap.shape[1] > D else 0.0


def side_by_side(lanes, part, eng):
    work = []
    for lane in lanes:
        start, steps = 0.0, []
        for stage in lane:
            steps.append((start, program_of(stage, part)(eng)))
            start += stage.time
        work.append([0.0, steps, 0])
    while any(w[2] < len(w[1]) for w in work):
        w = min((w for w in work if w[2] < len(w[1])), key=lambda w: w[0])
        try:
            w[0] += next(w[1][w[2]][1])
        except StopIteration:
            w[2] += 1
            if w[2] < len(w[1]):
                w[0] = w[1][w[2]][0]


def program_of(stage, part):
    return {"t": stage.t, "v": stage.v, "a": stage.a, "p": stage.p, "s": stage.s}[part]


class LinearFeatures(Stage):

    def __init__(self, lane, k, inputs, chunks, drain, who, after=(), drain_after=(), cols=N, tail=None,
                 tail_after=(), rows=()):
        super().__init__(lane)
        self.inputs, self.drain, self.who, self.cols, self.tail = inputs, drain, who, cols, tail
        self.after, self.drain_after, self.tail_after = after, drain_after, tail_after
        self.groups, self.loads = [], list(rows)
        for g in range(chunks // 3):
            through = [lane.mark("T") for _ in inputs[:-1]]
            tiles = [lane.tile(who) for _ in range(3)]
            panels = [lane.panel(k.panel[i[0] + g]) for i in inputs]
            for p_, m in zip(panels, through + [tiles[-1].filled]):
                p_.freed = m
            self.groups.append((tiles, panels, through))
            self.loads += panels
        self.done = self.groups[-1][0][-1].drained
        self.time = 4 * 6 * self.cols / 2400 * len(inputs) * chunks + 0.5

    def t(self, pe):
        wait_all(pe, self.after)
        last = len(self.inputs) - 1
        for g, (tiles, panels, through) in enumerate(self.groups):
            for i, (_, x) in enumerate(self.inputs):
                pe.wait_ge(*panels[i].at)
                w = panels[i].ap.rearrange("p (k n) -> p k n", k=KC)
                for o, tile in enumerate(tiles):
                    if i == 0:
                        fill(pe, tile)
                    for c in range(KC):
                        mm = pe.matmul(tile.ps[:, 0:self.cols], w[:, c, o * P:(o + 1) * P], x[:, c, :],
                                       start=(i == 0 and c == 0),
                                       stop=(i == last and c == KC - 1 and self.tail is None))
                    if i == last:
                        if self.tail is not None:
                            if g == 0 and o == 0:
                                wait_all(pe, self.tail_after)
                            mm = self.tail(pe, 3 * g + o, tile.ps[:, 0:self.cols])
                        mm.then_inc(*tile.filled.by)
                    yield 4 * 6 * self.cols / 2400
                if i < last:
                    mm.then_inc(*through[i].by)

    def drains(self, eng):
        wait_all(eng, self.drain_after)
        for g, (tiles, _, _) in enumerate(self.groups):
            yield (len(self.inputs) - 1) * 3 * 4 * 6 * self.cols / 2400
            for o, tile in enumerate(tiles):
                eng.wait_ge(*tile.filled.at)
                self.drain(eng, 3 * g + o, tile.ps[:, 0:self.cols]).then_inc(*tile.drained.by)
                yield 4 * 6 * self.cols / 2400

    def v(self, dve):
        return self.drains(dve) if self.who == "V" else iter(())

    def a(self, act):
        return self.drains(act) if self.who == "A" else iter(())


class LinearTokens(Stage):

    def __init__(self, lane, k, inputs, panels, drain, who="V", after=(), drain_after=(), rows=(), tail=None,
                 tail_after=(), kc=KC, step=None):
        super().__init__(lane)
        self.inputs, self.drain, self.who, self.tail = inputs, drain, who, tail
        self.after, self.drain_after, self.tail_after = after, drain_after, tail_after
        self.groups, self.loads = [], list(rows)
        for g in range(panels):
            through = [lane.mark("T") for _ in inputs[:-1]]
            tiles = [lane.tile(who) for _ in range(NT)]
            loads = [lane.panel(k.panel[i[0] + g]) for i in inputs]
            for p_, m in zip(loads, through + [tiles[-1].filled]):
                p_.freed = m
            self.groups.append((tiles, loads, through))
            self.loads += loads
        self.done = self.groups[-1][0][-1].drained
        self.time = 4 * 6 * COLS / 2400 * len(inputs) * panels * NT + 0.5

    def t(self, pe):
        wait_all(pe, self.after)
        last = len(self.inputs) - 1
        for g, (tiles, panels, through) in enumerate(self.groups):
            for i, (_, x) in enumerate(self.inputs):
                pe.wait_ge(*panels[i].at)
                w = panels[i].ap.rearrange("p (k n) -> p k n", k=KC)
                for t, tile in enumerate(tiles):
                    if i == 0:
                        fill(pe, tile)
                    for c in range(KC):
                        mm = pe.matmul(tile.ps[:, 0:COLS], x[:, c, t * P:(t + 1) * P], w[:, c, :],
                                       start=(i == 0 and c == 0),
                                       stop=(i == last and c == KC - 1 and self.tail is None))
                    if i == last:
                        if self.tail is not None:
                            if g == 0 and t == 0:
                                wait_all(pe, self.tail_after)
                            mm = self.tail(pe, t, g, tile.ps[:, 0:COLS])
                        mm.then_inc(*tile.filled.by)
                    yield 4 * 6 * COLS / 2400
                if i < last:
                    mm.then_inc(*through[i].by)

    def drains(self, eng):
        wait_all(eng, self.drain_after)
        for g, (tiles, _, _) in enumerate(self.groups):
            yield (len(self.inputs) - 1) * NT * 4 * 6 * COLS / 2400
            for t, tile in enumerate(tiles):
                eng.wait_ge(*tile.filled.at)
                self.drain(eng, t, g, tile.ps[:, 0:COLS]).then_inc(*tile.drained.by)
                yield 4 * 6 * COLS / 2400

    def v(self, dve):
        return self.drains(dve) if self.who == "V" else iter(())

    def a(self, act):
        return self.drains(act) if self.who == "A" else iter(())


class ToFeatures(Stage):
    time = 4.0

    def __init__(self, lane, k, x, drain, who="V", after=(), drain_after=()):
        super().__init__(lane)
        self.k, self.x, self.drain, self.who, self.after, self.drain_after = k, x, drain, who, after, drain_after
        self.tiles = [lane.tile(who) for _ in range(KC)]
        self.done = self.tiles[-1].drained

    def t(self, pe):
        wait_all(pe, self.after)
        for c, tile in enumerate(self.tiles):
            fill(pe, tile)
            for t in range(NT):
                mm = pe.transpose(tile.ps[:, t * P:(t + 1) * P], self.x[:, t, c * P:(c + 1) * P], self.k.ident)
            mm.then_inc(*tile.filled.by)
            yield self.time / KC

    def drains(self, eng):
        wait_all(eng, self.drain_after)
        for c, tile in enumerate(self.tiles):
            eng.wait_ge(*tile.filled.at)
            self.drain(eng, c, tile.ps[:, 0:N]).then_inc(*tile.drained.by)
            yield self.time / KC

    def v(self, dve):
        return self.drains(dve) if self.who == "V" else iter(())

    def a(self, act):
        return self.drains(act) if self.who == "A" else iter(())


class ToTokens(Stage):
    time = 4.0

    def __init__(self, lane, k, xT, drain, who="V", after=(), drain_after=()):
        super().__init__(lane)
        self.k, self.xT, self.drain, self.who, self.after, self.drain_after = k, xT, drain, who, after, drain_after
        self.tiles = [lane.tile(who) for _ in range(2 * NT)]
        self.done = self.tiles[-1].drained

    def t(self, pe):
        wait_all(pe, self.after)
        for i, tile in enumerate(self.tiles):
            t, half = divmod(i, 2)
            fill(pe, tile)
            for c in range(3):
                mm = pe.transpose(tile.ps[:, c * P:(c + 1) * P], self.xT[:, 3 * half + c, t * P:(t + 1) * P],
                                  self.k.ident)
            mm.then_inc(*tile.filled.by)
            yield self.time / 4

    def drains(self, eng):
        wait_all(eng, self.drain_after)
        for i, tile in enumerate(self.tiles):
            t, half = divmod(i, 2)
            eng.wait_ge(*tile.filled.at)
            self.drain(eng, t, half, tile.ps[:, 0:COLS]).then_inc(*tile.drained.by)
            yield self.time / 4

    def v(self, dve):
        return self.drains(dve) if self.who == "V" else iter(())

    def a(self, act):
        return self.drains(act) if self.who == "A" else iter(())


def half(x, t, g):
    return x[:, t, g * COLS:(g + 1) * COLS]


class Power:

    def __init__(self, lane, k, x, exponent):
        self.x, self.exponent = x, k.exponents[:, exponent:exponent + 1]
        self.ready, self.done = lane.mark("V"), lane.mark("P")

    def p(self, pool):
        e = self.exponent
        for n in self.x.shape[2:]:
            e = e.unsqueeze(2)
        pool.wait_ge(*self.ready.at)
        pool.tensor_tensor(self.x, self.x, e.to_broadcast(list(self.x.shape)), ALU.pow).then_inc(*self.done.by)


INVERSE_ROOT, ROOT = 0, 1


class Setup(Stage):
    time = 3.0

    def __init__(self, lane, k):
        super().__init__(lane)
        self.k = k
        self.done = lane.mark("P")

    def p(self, pool):
        k = self.k
        pool.memset(k.exponents[:, 0:1], -0.5)
        pool.memset(k.exponents[:, 1:2], 0.5)
        pool.iota(k.iota_int, [[1, N]], base=0, channel_multiplier=0)
        pool.iota(k.rowid_int, [[P, NT]], base=0, channel_multiplier=1)
        self.lane.step("P", pool, pool.memset(k.ident, 0.0))
        self.lane.step("P", pool, pool.affine_select(out=k.ident, in_=k.ident, compare_op=ALU.not_equal, fill=1.0,
                                                     base=0, pattern=[[-1, P]], channel_multiplier=1))
        pool.memset(k.blocks, 0.0)
        pool.memset(k.ones, 1.0).then_inc(*self.done.by)
        pool.wait_ge(*self.done.at)
        yield self.time


class LayerNorm(Stage):
    time = 6.0

    def __init__(self, lane, k, x, out, eps, small, after=()):
        super().__init__(lane)
        self.x, self.out, self.eps, self.small, self.after = x, out, eps, small, after
        self.power = Power(lane, k, small[:, 24:28].rearrange("p (t n) -> p t n", t=NT)[:, :, 1], INVERSE_ROOT)
        self.done = lane.mark("V")

    def p(self, pool):
        self.power.p(pool)
        yield self.time

    def v(self, dve):
        wait_all(dve, self.after)
        step = lambda ins: self.lane.step("V", dve, ins)
        stats = self.small[:, 0:24].rearrange("p (t s n) -> p t s n", t=NT, s=2)
        mv = self.small[:, 24:28].rearrange("p (t n) -> p t n", t=NT)
        for t in range(NT):
            for s in range(2):
                ins = dve.bn_stats(stats[:, t, s, :], half(self.x, t, s))
        step(ins)
        for t in range(NT):
            ins = dve.bn_aggr(mv[:, t, :], stats[:, t, :, :].rearrange("p s n -> p (s n)"))
        step(ins)
        dve.tensor_scalar(mv[:, :, 1], mv[:, :, 1], self.eps, None, ALU.add).then_inc(*self.power.ready.by)
        dve.wait_ge(*self.power.done.at)
        for t in range(NT):
            ins = dve.tensor_scalar(self.out[:, t, :], self.x[:, t, :], mv[:, t, 0:1], mv[:, t, 1:2],
                                    ALU.subtract, ALU.mult)
        ins.then_inc(*self.done.by)
        dve.wait_ge(*self.done.at)
        yield self.time


class Graph(Stage):
    time = 60.0

    def __init__(self, lane, k, hot, counts, constants):
        super().__init__(lane)
        self.k, self.counts = k, counts
        self.hot = [h.bitcast(BF16)[:, 0:4 * 1024].rearrange("p (c n) -> p c n", c=4) for h in hot]
        self.constants = constants
        self.tiles = [lane.tile("V") for _ in range(4)]
        self.hot_ready = [lane.mark("V") for _ in range(EC // 4)]
        self.hot_used = [lane.mark("T") for _ in range(EC // 4 - 1)]
        self.sums = [lane.tile("V") for _ in range(2)]
        self.row_power = Power(lane, k, k.dis_row, INVERSE_ROOT)
        self.adj_ready = lane.mark("V")
        self.col_power = Power(lane, k, k.dis_col, INVERSE_ROOT)
        self.turned = lane.tile("V")
        self.done = lane.mark("V")

    def p(self, pool):
        self.row_power.p(pool)
        self.col_power.p(pool)
        yield self.time

    def v(self, dve):
        k, lane = self.k, self.lane
        step = lambda ins: lane.step("V", dve, ins)
        edges = k.edges
        dve.wait_ge(*self.constants.at)
        dve.wait_ge(*k.edges_at)
        dve.tensor_copy(k.iota_bf, k.iota_int)
        dve.tensor_copy(k.iota, k.iota_int)
        dve.tensor_copy(k.rowid, k.rowid_int)
        step(dve.tensor_copy(edges, k.edges_int))
        for r in range(R):
            ins = dve.tensor_scalar(k.dst_of[:, r, :], edges[:, 2, :], float(r), None, ALU.is_equal)
        step(ins)
        step(dve.tensor_scalar(edges[:, 1, :], edges[:, 1, :], 1.0, None, ALU.add))
        for r in range(R):
            ins = dve.tensor_tensor(k.dst_of[:, r, :], k.dst_of[:, r, :], edges[:, 1, :], ALU.mult)
        step(ins)
        step(dve.tensor_scalar(k.dst_of, k.dst_of, -1.0, None, ALU.add))
        for g in range(EC // 4):
            if g >= 2:
                dve.wait_ge(*self.hot_used[g - 2].at)
            for j in range(4):
                c = 4 * g + j
                dve.tensor_scalar(self.hot[g % 2][:, j, 0:N], k.iota_bf, edges[:, 0, c:c + 1], None, ALU.is_equal)
                for r in range(R):
                    ins = dve.tensor_scalar(self.hot[g % 2][:, j, (r + 1) * N:(r + 2) * N], k.iota_bf,
                                            k.dst_of[:, r, c:c + 1], None, ALU.is_equal)
            ins.then_inc(*self.hot_ready[g].by)
            yield 4.0
        counts = self.counts
        for i, tile in enumerate(self.tiles):
            t, b = divmod(i, 2)
            a, z = (0, 512) if b == 0 else (512, 768)
            dve.wait_ge(*tile.filled.at)
            dve.tensor_copy(counts[:, t, a:z], tile.ps[:, 0:z - a]).then_inc(*tile.drained.by)
        inv, deg = k.inv, k.dis_row
        dve.wait_ge(*self.tiles[-1].drained.at)
        for i, tile in enumerate(self.sums):
            a, z = (0, 512) if i == 0 else (512, 768)
            dve.wait_ge(*tile.filled.at)
            dve.tensor_copy(inv[:, a:z], tile.ps[:, 0:z - a]).then_inc(*tile.drained.by)
        dve.wait_ge(*self.sums[-1].drained.at)
        step(dve.tensor_tensor(deg, inv[:, 0:N], inv[:, N:2 * N], ALU.add))
        step(dve.tensor_tensor(deg, deg, inv[:, 2 * N:3 * N], ALU.add))
        dve.tensor_scalar(deg, deg, 1.0, None, ALU.add).then_inc(*self.row_power.ready.by)
        step(dve.tensor_scalar(inv, inv, 1.0, None, ALU.max))
        step(dve.reciprocal(inv, inv))
        cin = counts.rearrange("p t (r n) -> p t r n", r=R)
        step(dve.tensor_tensor(k.adjT, cin[:, :, 0, :], cin[:, :, 1, :], ALU.add))
        step(dve.tensor_tensor(k.adjT, k.adjT, cin[:, :, 2, :], ALU.add))
        for t in range(NT):
            blk = k.adjT[:, t, t * P:(t + 1) * P]
            ins = dve.tensor_tensor(blk, blk, k.ident, ALU.add)
        ins.then_inc(*self.adj_ready.by)
        dve.wait_ge(*self.adj_ready.at)
        for t in range(NT):
            ins = dve.tensor_tensor(counts[:, t, :], counts[:, t, :], inv, ALU.mult)
        step(ins)
        dve.wait_ge(*self.turned.filled.at)
        dve.tensor_copy(k.adj, self.turned.ps.rearrange("p (t n) -> p t n", t=NT)).then_inc(*self.turned.drained.by)
        dve.wait_ge(*self.turned.drained.at)
        dve.tensor_reduce(k.dis_col, k.adj, AX.X, ALU.add).then_inc(*self.col_power.ready.by)
        dve.wait_ge(*self.row_power.done.at)
        dve.wait_ge(*self.col_power.done.at)
        for t in range(NT):
            ins = dve.scalar_tensor_tensor(out=k.gcn[:, t, :], in0=k.adjT[:, t, :], scalar=k.dis_col[:, t:t + 1],
                                           in1=deg, op0=ALU.mult, op1=ALU.mult)
        for b in range(2):
            ins = dve.memset(k.blocks[b * DH:(b + 1) * DH, b * DH:(b + 1) * DH], 1.0)
        ins.then_inc(*self.done.by)
        dve.wait_ge(*self.done.at)
        yield 4.0

    def t(self, pe):
        k = self.k
        for tile in self.tiles:
            fill(pe, tile)
        for g in range(EC // 4):
            pe.wait_ge(*self.hot_ready[g].at)
            for j in range(4):
                first, last = g + j == 0, (g == EC // 4 - 1 and j == 3)
                hot = self.hot[g % 2][:, j, :]
                for i, tile in enumerate(self.tiles):
                    t, b = divmod(i, 2)
                    a, z = (256, 768) if b == 0 else (768, 1024)
                    mm = pe.matmul(tile.ps[:, 0:z - a], hot[:, t * P:(t + 1) * P], hot[:, a:z],
                                   start=first, stop=last)
                    if last:
                        if i < 3:
                            mm.then_inc(*tile.filled.by)
            if g < EC // 4 - 1:
                mm.then_inc(*self.hot_used[g].by)
            yield 4.0
        mm.then_inc(*self.tiles[3].filled.by)
        pe.wait_ge(*self.constants.at)
        pe.wait_ge(*self.tiles[-1].drained.at)
        for i, tile in enumerate(self.sums):
            a, z = (0, 512) if i == 0 else (512, 768)
            fill(pe, tile)
            for t in range(NT):
                mm = pe.matmul(tile.ps[:, 0:z - a], k.ones, self.counts[:, t, a:z], start=(t == 0), stop=(t == 1))
            mm.then_inc(*tile.filled.by)
        pe.wait_ge(*self.adj_ready.at)
        fill(pe, self.turned)
        for dt_ in range(NT):
            for st in range(NT):
                mm = pe.transpose(self.turned.ps[:, dt_ * N + st * P:dt_ * N + (st + 1) * P],
                                  k.adjT[:, st, dt_ * P:(dt_ + 1) * P], k.ident)
        mm.then_inc(*self.turned.filled.by)
        yield 4.0


class Aggregate(Stage):

    def __init__(self, lane, k, h, m, width, out, after=(), drain_after=()):
        super().__init__(lane)
        self.h, self.m, self.out, self.after, self.drain_after = h, m, out, after, drain_after
        self.cuts = [(0, 512), (512, 768)] if width == 768 else [(0, width)]
        self.tiles = [[lane.tile("V") for _ in self.cuts] for _ in range(KC)]
        self.done = self.tiles[-1][-1].drained
        self.time = KC * 2 * width * 4 / 2400

    def t(self, pe):
        wait_all(pe, self.after)
        for c, tiles in enumerate(self.tiles):
            for (a, z), tile in zip(self.cuts, tiles):
                fill(pe, tile)
                for t in range(NT):
                    mm = pe.matmul(tile.ps[:, 0:z - a], self.h[:, t, c * P:(c + 1) * P], self.m[:, t, a:z],
                                   start=(t == 0), stop=(t == NT - 1))
                mm.then_inc(*tile.filled.by)
            yield self.time / KC

    def v(self, dve):
        wait_all(dve, self.drain_after)
        for c, tiles in enumerate(self.tiles):
            for (a, z), tile in zip(self.cuts, tiles):
                dve.wait_ge(*tile.filled.at)
                dve.tensor_copy(self.out[:, c, a:z], tile.ps[:, 0:z - a]).then_inc(*tile.drained.by)
            yield self.time / KC


class GateSum(Stage):
    UNITS = [(c, b) for c in range(KC) for b in range(B)]
    time = len(UNITS) * 4.4

    def __init__(self, lane, k, hg, qg, q, out, z, after=()):
        super().__init__(lane)
        self.hg, self.qg, self.q, self.out, self.after = hg, qg, q, out, after
        self.z = [zz[:, 0:NB * L].rearrange("p (n l) -> p n l", n=NB) for zz in z]
        self.added = [lane.mark("P") for _ in self.UNITS]
        self.squashed = [lane.mark("A") for _ in self.UNITS]
        self.summed = [lane.mark("V") for _ in self.UNITS]
        self.done = self.summed[-1]

    def p(self, pool):
        wait_all(pool, self.after)
        for i, (c, b) in enumerate(self.UNITS):
            if i >= len(self.z):
                pool.wait_ge(*self.summed[i - len(self.z)].at)
            hg = self.hg[:, c, b * NB:(b + 1) * NB].unsqueeze(2).to_broadcast([P, NB, L])
            qg = self.qg[:, c, b * L:(b + 1) * L].unsqueeze(1).to_broadcast([P, NB, L])
            pool.tensor_tensor(self.z[i % len(self.z)], hg, qg, ALU.add).then_inc(*self.added[i].by)
            yield 4.4

    def a(self, act):
        for i in range(len(self.UNITS)):
            z = self.z[i % len(self.z)]
            act.wait_ge(*self.added[i].at)
            act.activation(z, z, ACT.Sigmoid).then_inc(*self.squashed[i].by)
            yield 4.4

    def v(self, dve):
        for i, (c, b) in enumerate(self.UNITS):
            z = self.z[i % len(self.z)]
            q = self.q[:, c, b * L:(b + 1) * L].unsqueeze(1).to_broadcast([P, NB, L])
            dve.wait_ge(*self.squashed[i].at)
            self.lane.step("V", dve, dve.tensor_tensor(z, z, q, ALU.mult))
            dve.tensor_reduce(self.out[:, c, b * NB:(b + 1) * NB], z, AX.X, ALU.add).then_inc(*self.summed[i].by)
            yield 4.4


class GateMix(Stage):
    time = 6.0

    def __init__(self, lane, alpha, qi, h, out, after=()):
        super().__init__(lane)
        self.alpha, self.qi, self.h, self.out, self.after = alpha, qi, h, out, after
        self.tanh = lane.mark("A")
        self.done = lane.mark("V")

    def a(self, act):
        wait_all(act, self.after)
        act.activation(self.qi, self.qi, ACT.Tanh).then_inc(*self.tanh.by)
        yield self.time

    def v(self, dve):
        step = lambda ins: self.lane.step("V", dve, ins)
        dve.wait_ge(*self.tanh.at)
        wait_all(dve, self.after)
        step(dve.tensor_tensor(self.qi, self.qi, self.alpha, ALU.mult))
        step(dve.tensor_scalar(self.alpha, self.alpha, -1.0, 1.0, ALU.mult, ALU.add))
        step(dve.tensor_tensor(self.alpha, self.alpha, self.h, ALU.mult))
        dve.tensor_tensor(self.out, self.qi, self.alpha, ALU.add).then_inc(*self.done.by)
        dve.wait_ge(*self.done.at)
        yield self.time


class Vector(Stage):

    def __init__(self, lane, body, time=2.0, after=(), rows=()):
        super().__init__(lane)
        self.body, self.time, self.after, self.loads = body, time, after, list(rows)
        self.done = lane.mark("V")
        for row in rows:
            row.freed = self.done

    def v(self, dve):
        wait_all(dve, self.after)
        for load in self.loads:
            dve.wait_ge(*load.at)
        self.body(dve, lambda ins: self.lane.step("V", dve, ins)).then_inc(*self.done.by)
        dve.wait_ge(*self.done.at)
        yield self.time


class EluPlusOne(Stage):
    time = 5.0

    def __init__(self, lane, x, tmp, after=()):
        super().__init__(lane)
        self.x, self.tmp, self.after = x, tmp, after
        self.exp = lane.mark("A")
        self.done = lane.mark("V")

    def a(self, act):
        wait_all(act, self.after)
        act.activation(self.tmp, self.x, ACT.Exp).then_inc(*self.exp.by)
        yield self.time

    def v(self, dve):
        dve.wait_ge(*self.exp.at)
        wait_all(dve, self.after)
        self.lane.step("V", dve, dve.tensor_scalar(self.x, self.x, 0.0, None, ALU.max))
        dve.scalar_tensor_tensor(out=self.x, in0=self.tmp, scalar=1.0, in1=self.x, op0=ALU.min,
                                 op1=ALU.add).then_inc(*self.done.by)
        dve.wait_ge(*self.done.at)
        yield self.time


class KeyValues(Stage):
    time = 6.0

    def __init__(self, lane, k, key, value, sums, drain, after=()):
        super().__init__(lane)
        self.k, self.key, self.value, self.sums, self.drain, self.after = k, key, value, sums, drain, after
        self.tiles = [lane.tile("V") for _ in range(KC)]
        self.done = self.tiles[-1].drained

    def t(self, pe):
        wait_all(pe, self.after)
        for c, tile in enumerate(self.tiles):
            fill(pe, tile)
            for t in range(NT):
                key = self.key[:, t, c * P:(c + 1) * P]
                mm = pe.matmul(tile.ps[:, 0:P], key, self.value[:, t, c * P:(c + 1) * P],
                               start=(t == 0), stop=(t == NT - 1))
            if self.sums:
                for t in range(NT):
                    mm = pe.matmul(tile.ps[:, P:P + 2], self.key[:, t, c * P:(c + 1) * P], self.k.ones[:, 0:2],
                                   start=(t == 0), stop=(t == NT - 1))
            mm.then_inc(*tile.filled.by)
            yield self.time / KC

    def v(self, dve):
        for c, tile in enumerate(self.tiles):
            dve.wait_ge(*tile.filled.at)
            self.drain(dve, c, tile.ps, lambda ins: self.lane.step("V", dve, ins)).then_inc(*tile.drained.by)
            yield self.time / KC


class QueryStates(Stage):
    time = 8.0

    def __init__(self, lane, k, states, norms, qT, outT, scratch, after=()):
        super().__init__(lane)
        self.states, self.norms, self.qT, self.outT, self.scratch, self.after = states, norms, qT, outT, scratch, after
        self.tiles = [lane.tile("V") for _ in range(KC)]
        self.done = self.tiles[-1].drained

    def t(self, pe):
        wait_all(pe, self.after)
        for c, tile in enumerate(self.tiles):
            fill(pe, tile)
            mm = pe.matmul(tile.ps[:, 0:N], self.states[:, c, :], self.qT[:, c, :], start=True, stop=True)
            if self.norms is not None:
                mm = pe.matmul(tile.ps[:, N:2 * N], self.norms[:, c, :], self.qT[:, c, :], start=True, stop=True)
            mm.then_inc(*tile.filled.by)
            yield self.time / KC

    def v(self, dve):
        for c, tile in enumerate(self.tiles):
            dve.wait_ge(*tile.filled.at)
            if self.norms is not None:
                if c:
                    dve.wait_ge(*self.tiles[c - 1].drained.at)
                self.lane.step("V", dve, dve.reciprocal(self.scratch, tile.ps[:, N:2 * N]))
                ins = dve.tensor_tensor(self.outT[:, c, :], tile.ps[:, 0:N], self.scratch, ALU.mult)
            else:
                ins = dve.tensor_copy(self.outT[:, c, :], tile.ps[:, 0:N])
            ins.then_inc(*tile.drained.by)
            yield self.time / KC


def top_two(dve, step, s, mask, best, rank, left, e):
    wide = lambda ap: ap.unsqueeze(2).to_broadcast([P, NT, e])
    rank_b = rank.unsqueeze(1).to_broadcast([P, NT, e])
    src = s
    for i in range(2):
        step(dve.tensor_reduce(best, src, AX.X, ALU.max))
        hit = left[i]
        step(dve.tensor_tensor(hit, src, wide(best), ALU.is_equal))
        step(dve.tensor_tensor(hit, hit, rank_b, ALU.mult))
        step(dve.tensor_reduce(best, hit, AX.X, ALU.max))
        step(dve.tensor_tensor(hit, hit, wide(best), ALU.is_equal))
        if i == 0:
            step(dve.scalar_tensor_tensor(out=left[2], in0=hit, scalar=-4.0, in1=s, op0=ALU.mult, op1=ALU.add))
            src = left[2]
    return dve.tensor_tensor(mask, left[0], left[1], ALU.add)


class Logits(Stage):
    time = 8.0

    def __init__(self, lane, k, xT, narrow, e, groups, out, small, bias=None, after=()):
        super().__init__(lane)
        self.xT, self.narrow, self.e, self.groups, self.out, self.bias = xT, narrow, e, groups, out, bias
        self.small, self.after = small, after
        self.tile = lane.tile("V")
        self.ready = lane.mark("V")
        self.exped = lane.mark("A")
        self.done = lane.mark("V")

    def t(self, pe):
        wait_all(pe, self.after)
        fill(pe, self.tile)
        for t in range(NT):
            for c in range(KC):
                mm = pe.matmul(self.tile.ps[:, t * self.e:(t + 1) * self.e], self.xT[:, c, t * P:(t + 1) * P],
                               self.narrow[:, c, :], start=(c == 0), stop=(c == KC - 1))
        mm.then_inc(*self.tile.filled.by)
        yield self.time

    def v(self, dve):
        step = lambda ins: self.lane.step("V", dve, ins)
        e, out, best = self.e, self.out, self.small
        dve.wait_ge(*self.tile.filled.at)
        dve.tensor_copy(out, self.tile.ps[:, 0:NT * e].rearrange("p (t e) -> p t e", t=NT)).then_inc(
            *self.tile.drained.by)
        dve.wait_ge(*self.tile.drained.at)
        if self.bias is not None:
            step(dve.tensor_tensor(out, out, self.bias.unsqueeze(1).to_broadcast([P, NT, e]), ALU.add))
        for a, z in self.groups:
            step(dve.tensor_reduce(best, out[:, :, a:z], AX.X, ALU.max))
            ins = dve.tensor_tensor(out[:, :, a:z], out[:, :, a:z], best.unsqueeze(2).to_broadcast([P, NT, z - a]),
                                    ALU.subtract)
            if z < e:
                step(ins)
        ins.then_inc(*self.ready.by)
        dve.wait_ge(*self.exped.at)
        for a, z in self.groups:
            step(dve.tensor_reduce(best, out[:, :, a:z], AX.X, ALU.add))
            step(dve.reciprocal(best, best))
            ins = dve.tensor_tensor(out[:, :, a:z], out[:, :, a:z], best.unsqueeze(2).to_broadcast([P, NT, z - a]),
                                    ALU.mult)
            if z < e:
                step(ins)
        ins.then_inc(*self.done.by)
        dve.wait_ge(*self.done.at)
        yield self.time

    def a(self, act):
        act.wait_ge(*self.ready.at)
        act.activation(self.out, self.out, ACT.Exp).then_inc(*self.exped.by)
        yield self.time


class TurnNarrow(Stage):
    time = 2.0

    def __init__(self, lane, k, x, e, out, scale=1.0, after=()):
        super().__init__(lane)
        self.k, self.x, self.e, self.out, self.scale, self.after = k, x, e, out, scale, after
        self.tile = lane.tile("V")
        self.done = self.tile.drained

    def t(self, pe):
        wait_all(pe, self.after)
        fill(pe, self.tile)
        for t in range(NT):
            mm = pe.transpose(self.tile.ps[0:self.e, t * P:(t + 1) * P], self.x[:, t, :], self.k.ident)
        mm.then_inc(*self.tile.filled.by)
        yield self.time

    def v(self, dve):
        dve.wait_ge(*self.tile.filled.at)
        dve.tensor_scalar(self.out, self.tile.ps[0:self.e, 0:N], self.scale, None, ALU.mult).then_inc(
            *self.tile.drained.by)
        yield self.time


class Experts(Stage):

    def __init__(self, lane, k, xT, x, combine, combineT, b2, hidden, after=()):
        super().__init__(lane)
        self.k, self.xT, self.x, self.combine, self.combineT, self.b2 = k, xT, x, combine, combineT, b2
        self.hidden, self.after = hidden, after
        self.bias_tiles = [lane.tile("V") for _ in range(2 * NT)]
        b2.freed = self.bias_tiles[-1].filled
        self.loads = [b2]
        self.up, self.down = {}, {}
        for kind, e in self.order():
            load = lane.panel(k.panel[PANELS["l0_w1" if kind == "up" else "l0_w2"] + e])
            tiles = [lane.tile("A" if kind == "up" else "V") for _ in range(3 if kind == "up" else 4)]
            load.freed = tiles[-1].filled
            (self.up if kind == "up" else self.down)[e] = (load, tiles)
            self.loads.append(load)
        self.done = self.down[7][1][-1].drained
        self.time = 16 * 7.7

    def order(self):
        yield "up", 0
        for e in range(8):
            if e < 7:
                yield "up", e + 1
            yield "down", e

    def t(self, pe):
        wait_all(pe, self.after)
        pe.wait_ge(*self.b2.at)
        for i, tile in enumerate(self.bias_tiles):
            t, g = divmod(i, 2)
            fill(pe, tile)
            pe.matmul(tile.ps[:, 0:COLS], self.combineT[:, t * P:(t + 1) * P], self.b2.ap[:, g * COLS:(g + 1) * COLS],
                      start=True, stop=True).then_inc(*tile.filled.by)
        for kind, e in self.order():
            load, tiles = (self.up if kind == "up" else self.down)[e]
            pe.wait_ge(*load.at)
            if kind == "up":
                w = load.ap.rearrange("p (k n) -> p k n", k=KC)
                for o, tile in enumerate(tiles):
                    fill(pe, tile)
                    for c in range(KC):
                        mm = pe.matmul(tile.ps[:, 0:N], w[:, c, o * P:(o + 1) * P], self.xT[:, c, :],
                                       start=(c == 0), stop=(c == KC - 1))
                    mm.then_inc(*tile.filled.by)
                    yield 2.56
            else:
                w = load.ap.rearrange("p (k n) -> p k n", k=3)
                pe.wait_ge(*self.up[e][1][-1].drained.at)
                for i, tile in enumerate(tiles):
                    t, g = divmod(i, 2)
                    fill(pe, tile)
                    for c in range(3):
                        mm = pe.matmul(tile.ps[:, 0:COLS], self.hidden[e % 2][:, c, t * P:(t + 1) * P],
                                       w[:, c, g * COLS:(g + 1) * COLS], start=(c == 0), stop=(c == 2))
                    mm.then_inc(*tile.filled.by)
                    yield 1.92

    def a(self, act):
        for e in range(8):
            for o, tile in enumerate(self.up[e][1]):
                act.wait_ge(*tile.filled.at)
                act.activation(self.hidden[e % 2][:, o, :], tile.ps[:, 0:N], ACT.Gelu,
                               bias=self.k.col("l0_b1", 3 * e + o)).then_inc(*tile.drained.by)
                yield 5.1

    def v(self, dve):
        for i, tile in enumerate(self.bias_tiles):
            x = half(self.x, *divmod(i, 2))
            dve.wait_ge(*tile.filled.at)
            dve.tensor_tensor(x, tile.ps[:, 0:COLS], x, ALU.add).then_inc(*tile.drained.by)
        before = self.bias_tiles
        for e in range(8):
            for i, tile in enumerate(self.down[e][1]):
                t, g = divmod(i, 2)
                x = half(self.x, t, g)
                dve.wait_ge(*before[i].drained.at)
                dve.wait_ge(*tile.filled.at)
                dve.scalar_tensor_tensor(out=x, in0=tile.ps[:, 0:COLS], scalar=self.combine[:, t, e:e + 1], in1=x,
                                         op0=ALU.mult, op1=ALU.add).then_inc(*tile.drained.by)
                yield 3.8
            before = self.down[e][1]


class SoftmaxAttention(Stage):

    def __init__(self, lane, k, qT, kT, v, outT, scale, probs, turned, small, gates=None, after=()):
        super().__init__(lane)
        self.k, self.qT, self.kT, self.value, self.outT, self.scale = k, qT, kT, v, outT, scale
        self.probs, self.turned, self.gates, self.after = probs, turned, gates, after
        self.nmax = small[:, 0:24].rearrange("p (h t) -> p h t", t=NT)
        self.rsum = small[:, 24:48].rearrange("p (h t) -> p h t", t=NT)
        self.maxed = {}
        self.exped, self.normed = {}, {}
        self.score, self.turn, self.out = {}, {}, {}
        for i in range(H + 3):
            if i < H:
                self.score[i] = lane.tile("A")
            if 0 <= i - 2 < H:
                self.turn[i - 2] = lane.tile("V")
            if 0 <= i - 3 < H:
                self.out[i - 3] = lane.tile("A")
            if i < H:
                self.maxed[i] = lane.mark("V")
            if 0 <= i - 1 < H:
                self.normed[i - 1] = lane.mark("V")
        self.done = self.out[H - 1].drained
        self.time = 4.0 * (H + 3)

    def t(self, pe):
        wait_all(pe, self.after)
        for i in range(H + 3):
            if i < H:
                c, r = i // 2, (i % 2) * DH
                tile = self.score[i]
                fill(pe, tile)
                for t in range(NT):
                    mm = pe.matmul(tile.ps[:, t * N:(t + 1) * N], self.qT[r:r + DH, c, t * P:(t + 1) * P],
                                   self.kT[r:r + DH, c, :], start=True, stop=True)
                mm.then_inc(*tile.filled.by)
            if 0 <= i - 2 < H:
                h = i - 2
                tile = self.turn[h]
                fill(pe, tile)
                pe.wait_ge(*self.normed[h].at)
                for m in range(NT):
                    for t in range(NT):
                        mm = pe.transpose(tile.ps[:, m * N + t * P:m * N + (t + 1) * P],
                                          self.probs[h % 3][:, t, m * P:(m + 1) * P], self.k.ident)
                mm.then_inc(*tile.filled.by)
            if 0 <= i - 3 < H:
                h = i - 3
                tile = self.out[h]
                fill(pe, tile)
                pe.wait_ge(*self.turn[h].drained.at)
                for m in range(NT):
                    mm = pe.matmul(tile.ps[:, 0:N], self.value[:, m, (h // 2) * P:(h // 2 + 1) * P],
                                   self.turned[h % 2][:, m, :], start=(m == 0), stop=(m == NT - 1))
                mm.then_inc(*tile.filled.by)
            yield 4.0

    def v(self, dve):
        step = lambda ins: self.lane.step("V", dve, ins)
        for i in range(H + 3):
            if i < H:
                dve.wait_ge(*self.score[i].filled.at)
                step(dve.tensor_reduce(self.nmax[:, i, :], self.score[i].ps.rearrange("p (t n) -> p t n", t=NT),
                                       AX.X, ALU.max))
                dve.tensor_scalar(self.nmax[:, i, :], self.nmax[:, i, :], -self.scale, None,
                                  ALU.mult).then_inc(*self.maxed[i].by)
            if 0 <= i - 1 < H:
                h = i - 1
                dve.wait_ge(*self.score[h].drained.at)
                step(dve.reciprocal(self.rsum[:, h, :], self.rsum[:, h, :]))
                if self.gates is not None:
                    step(dve.tensor_tensor(self.rsum[:, h, :], self.rsum[:, h, :], self.gates[:, :, h], ALU.mult))
                for t in range(NT):
                    p = self.probs[h % 3][:, t, :]
                    ins = dve.tensor_scalar(p, p, self.rsum[:, h, t:t + 1], None, ALU.mult)
                ins.then_inc(*self.normed[h].by)
            if 0 <= i - 2 < H:
                h = i - 2
                if h >= 2:
                    dve.wait_ge(*self.out[h - 2].filled.at)
                dve.wait_ge(*self.turn[h].filled.at)
                dve.tensor_copy(self.turned[h % 2], self.turn[h].ps.rearrange("p (m n) -> p m n", m=NT)).then_inc(
                    *self.turn[h].drained.by)
            yield 4.0

    def a(self, act):
        for i in range(H + 3):
            if i < H:
                if i >= 3:
                    act.wait_ge(*self.turn[i - 3].filled.at)
                act.wait_ge(*self.maxed[i].at)
                for t in range(NT):
                    ins = act.activation(self.probs[i % 3][:, t, :], self.score[i].ps[:, t * N:(t + 1) * N], ACT.Exp,
                                         bias=self.nmax[:, i, t:t + 1], scale=self.scale,
                                         accum_out=self.rsum[:, i, t:t + 1])
                ins.then_inc(*self.score[i].drained.by)
            if 0 <= i - 3 < H:
                h = i - 3
                r = (h % 2) * DH
                act.wait_ge(*self.out[h].filled.at)
                act.activation(self.outT[r:r + DH, h // 2, :], self.out[h].ps[r:r + DH, 0:N],
                               ACT.Copy).then_inc(*self.out[h].drained.by)
            yield 4.0


class RandomFeatures(Stage):
    time = 30.0

    def __init__(self, lane, k, qsT, sqT, rand, rf, tmp, small, after=()):
        super().__init__(lane)
        self.k, self.qsT, self.sqT, self.rand, self.rf, self.tmp = k, qsT, sqT, rand, rf, tmp
        self.ss, self.after = small[:, 0:H], after
        self.loads = [rand]
        self.squared = lane.mark("V")
        self.tiles = [lane.tile("A") for _ in range(H)]
        rand.freed = self.tiles[-1].filled
        self.power = Power(lane, k, self.ss, ROOT)
        self.done = lane.mark("V")

    def p(self, pool):
        self.power.p(pool)
        yield self.time

    def t(self, pe):
        pe.wait_ge(*self.squared.at)
        pe.wait_ge(*self.rand.at)
        rand = self.rand.ap.rearrange("p (c m) -> p c m", c=KC)
        for h, tile in enumerate(self.tiles):
            c, r = h // 2, (h % 2) * DH
            fill(pe, tile)
            pe.matmul(tile.ps[:, 0:N], rand[r:r + DH, c, :], self.qsT[r:r + DH, c, :], start=True, stop=False)
            pe.matmul(tile.ps[:, 0:N], self.k.minus_half[r:r + DH, :], self.sqT[r:r + DH, c, :],
                      start=False, stop=True).then_inc(*tile.filled.by)
            yield 1.0

    def a(self, act):
        for h, tile in enumerate(self.tiles):
            act.wait_ge(*tile.filled.at)
            act.activation(self.rf[:, h, :], tile.ps[:, 0:N], ACT.Exp).then_inc(*tile.drained.by)
            yield 1.0

    def v(self, dve):
        step = lambda ins: self.lane.step("V", dve, ins)
        wait_all(dve, self.after)
        dve.tensor_tensor(self.sqT, self.qsT, self.qsT, ALU.mult).then_inc(*self.squared.by)
        yield 12.0
        features = 2 * DH
        dve.wait_ge(*self.tiles[-1].drained.at)
        step(dve.tensor_tensor(self.tmp, self.rf, self.rf, ALU.mult))
        step(dve.tensor_reduce(self.ss, self.tmp, AX.X, ALU.add))
        dve.tensor_scalar(self.ss, self.ss, 1.0 / features, None, ALU.mult).then_inc(*self.power.ready.by)
        dve.wait_ge(*self.power.done.at)
        step(dve.tensor_scalar(self.ss, self.ss, 1e-12, None, ALU.max))
        step(dve.reciprocal(self.ss, self.ss))
        step(dve.tensor_scalar(self.ss, self.ss, float(features) ** -0.5, None, ALU.mult))
        dve.tensor_tensor(self.rf, self.rf, self.ss.unsqueeze(2).to_broadcast([P, H, N]), ALU.mult).then_inc(
            *self.done.by)
        dve.wait_ge(*self.done.at)
        yield 15.0


class SparseCodes(Stage):
    time = 90.0
    LAM, STEPS = 0.3, 5

    def __init__(self, lane, k, rf, v, qn, kk, kv, s, g, z, outT, small, after=()):
        super().__init__(lane)
        self.k, self.rf, self.value, self.qn, self.kk, self.kv, self.sparse, self.g, self.z = k, rf, v, qn, kk, kv, s, g, z
        self.outT, self.after = outT, after
        self.row = small[:, 0:H]
        self.diag = small[:, H:2 * H]
        self.inv = small[:, 2 * H:3 * H]
        self.lim = small[:, 3 * H:4 * H]
        self.neg = small[:, 4 * H:5 * H]
        self.turned = [lane.tile("V") for _ in range(H // 2)]
        self.gram = [lane.tile("V") for _ in range(3)]
        self.cross = [lane.tile("V") for _ in range(2)]
        self.summed = lane.mark("V")
        self.sums = lane.tile("V")
        self.diagonal = lane.mark("V")
        self.spread = lane.tile("V")
        self.code = [lane.mark("V") for _ in range(self.STEPS + 1)]
        self.grad = [[lane.tile("V") for _ in range(2)] for _ in range(self.STEPS)]
        self.out = [lane.tile("V") for _ in range(KC)]
        self.done = self.out[-1].drained

    HEADS = ((0, 8), (8, 12))

    def t(self, pe):
        k = self.k
        wait_all(pe, self.after)
        for i, tile in enumerate(self.turned):
            fill(pe, tile)
            for t in range(NT):
                for j in range(2):
                    mm = pe.transpose(tile.ps[:, (2 * t + j) * P:(2 * t + j + 1) * P],
                                      self.rf[:, 2 * i + j, t * P:(t + 1) * P], k.ident)
            mm.then_inc(*tile.filled.by)
        pe.wait_ge(*self.turned[-1].drained.at)
        for i, tile in enumerate(self.gram):
            fill(pe, tile)
            for j in range(4):
                for t in range(NT):
                    qn = self.qn[:, t, 4 * i + j, :]
                    mm = pe.matmul(tile.ps[:, j * P:(j + 1) * P], qn, qn, start=(t == 0), stop=(t == NT - 1))
            mm.then_inc(*tile.filled.by)
        for (a, z), tile in zip(self.HEADS, self.cross):
            fill(pe, tile)
            for h in range(a, z):
                for t in range(NT):
                    mm = pe.matmul(tile.ps[:, (h - a) * DH:(h - a + 1) * DH], self.qn[:, t, h, :],
                                   self.value[:, t, h * DH:(h + 1) * DH], start=(t == 0), stop=(t == NT - 1))
            mm.then_inc(*tile.filled.by)
        yield 25.0
        fill(pe, self.sums)
        pe.wait_ge(*self.summed.at)
        pe.transpose(self.sums.ps[0:H, 0:P], self.row, k.ident).then_inc(*self.sums.filled.by)
        fill(pe, self.spread)
        pe.wait_ge(*self.diagonal.at)
        pe.matmul(self.spread.ps[:, 0:H], k.ones[0:H, :], self.diag[0:H, :], start=True, stop=True).then_inc(
            *self.spread.filled.by)
        yield 5.0
        for n in range(self.STEPS):
            pe.wait_ge(*self.code[n].at)
            for (a, z), tile in zip(self.HEADS, self.grad[n]):
                fill(pe, tile)
                for h in range(a, z):
                    mm = pe.matmul(tile.ps[:, (h - a) * DH:(h - a + 1) * DH], self.kk[:, h, :],
                                   self.sparse[:, h * DH:(h + 1) * DH], start=True, stop=True)
                mm.then_inc(*tile.filled.by)
            yield 9.0
        pe.wait_ge(*self.code[self.STEPS].at)
        for c, tile in enumerate(self.out):
            fill(pe, tile)
            for j in range(2):
                mm = pe.matmul(tile.ps[:, j * N:(j + 1) * N], self.sparse[:, c * P:(c + 1) * P], self.rf[:, 2 * c + j, :],
                               start=True, stop=True)
            mm.then_inc(*tile.filled.by)
            yield 1.5

    def threshold(self, dve, step, z, lo, hi):
        step(dve.tensor_tensor(self.g, z, lo, ALU.max) if lo is not None else
             dve.tensor_scalar(self.g, z, -self.LAM, self.LAM, ALU.max, ALU.min))
        if lo is not None:
            step(dve.tensor_tensor(self.g, self.g, hi, ALU.min))
        return dve.tensor_tensor(self.sparse, z, self.g, ALU.subtract)

    def v(self, dve):
        step = lambda ins: self.lane.step("V", dve, ins)
        for i, tile in enumerate(self.turned):
            dve.wait_ge(*tile.filled.at)
            dve.tensor_copy(self.qn[:, :, 2 * i:2 * i + 2, :].rearrange("p t h m -> p t (h m)"),
                            tile.ps.rearrange("p (t x) -> p t x", t=NT)).then_inc(*tile.drained.by)
        for i, tile in enumerate(self.gram):
            dve.wait_ge(*tile.filled.at)
            dve.tensor_copy(self.kk[:, 4 * i:4 * i + 4, :].rearrange("p h m -> p (h m)"), tile.ps).then_inc(
                *tile.drained.by)
        for (a, z), tile in zip(self.HEADS, self.cross):
            dve.wait_ge(*tile.filled.at)
            dve.tensor_copy(self.kv[:, a * DH:z * DH], tile.ps[:, 0:(z - a) * DH]).then_inc(*tile.drained.by)
        dve.wait_ge(*self.cross[-1].drained.at)
        yield 25.0
        dve.tensor_reduce(self.row, self.kk, AX.X, ALU.add, apply_absolute_value=True).then_inc(*self.summed.by)
        dve.wait_ge(*self.sums.filled.at)
        dve.tensor_reduce(self.inv[0:H, 0:1], self.sums.ps[0:H, 0:P], AX.X, ALU.max).then_inc(*self.sums.drained.by)
        dve.wait_ge(*self.sums.drained.at)
        dve.tensor_scalar(self.diag[0:H, :], self.k.ident[0:H, 0:H], self.inv[0:H, 0:1], None, ALU.mult).then_inc(
            *self.diagonal.by)
        dve.wait_ge(*self.spread.filled.at)
        dve.wait_ge(*self.diagonal.at)
        dve.tensor_scalar(self.inv, self.spread.ps[:, 0:H], 1.0, None, ALU.add).then_inc(*self.spread.drained.by)
        dve.wait_ge(*self.spread.drained.at)
        step(dve.reciprocal(self.inv, self.inv))
        step(dve.tensor_scalar(self.lim, self.inv, self.LAM, None, ALU.mult))
        step(dve.tensor_scalar(self.neg, self.inv, -self.LAM, None, ALU.mult))
        self.threshold(dve, step, self.kv, None, None).then_inc(*self.code[0].by)
        dve.wait_ge(*self.code[0].at)
        yield 5.0
        wide = lambda ap: ap.unsqueeze(2).to_broadcast([P, H, DH])
        heads = lambda ap: ap.rearrange("p (h d) -> p h d", h=H)
        for n in range(self.STEPS):
            for (a, z), tile in zip(self.HEADS, self.grad[n]):
                dve.wait_ge(*tile.filled.at)
                dve.tensor_tensor(self.g[:, a * DH:z * DH], tile.ps[:, 0:(z - a) * DH],
                                  self.kv[:, a * DH:z * DH], ALU.subtract).then_inc(*tile.drained.by)
            dve.wait_ge(*self.grad[n][-1].drained.at)
            step(dve.tensor_tensor(heads(self.g), heads(self.g), wide(self.inv), ALU.mult))
            step(dve.tensor_tensor(self.z, self.sparse, self.g, ALU.subtract))
            step(dve.tensor_tensor(heads(self.g), heads(self.z), wide(self.neg), ALU.max))
            step(dve.tensor_tensor(heads(self.g), heads(self.g), wide(self.lim), ALU.min))
            dve.tensor_tensor(self.sparse, self.z, self.g, ALU.subtract).then_inc(*self.code[n + 1].by)
            dve.wait_ge(*self.code[n + 1].at)
            yield 9.0
        for c, tile in enumerate(self.out):
            dve.wait_ge(*tile.filled.at)
            for j in range(2):
                ins = dve.tensor_copy(self.outT[j * DH:(j + 1) * DH, c, :],
                                      tile.ps[j * DH:(j + 1) * DH, j * N:(j + 1) * N])
            ins.then_inc(*tile.drained.by)
            yield 1.5


class EdgeSoftmax(Stage):

    def __init__(self, lane, k, a_src, a_dst, heads, adj, mask, neg, diag, e, small, out, guard, after=()):
        super().__init__(lane)
        self.k, self.a_src, self.a_dst, self.heads, self.adj, self.mask, self.neg = k, a_src, a_dst, heads, adj, mask, neg
        self.diag, self.e, self.out, self.guard, self.after = diag, e, out, guard, after
        self.top = small[:, 0:NT]
        self.total = small[:, NT:2 * NT]
        self.diagonal, self.row, self.shifted, self.exped, self.normed, self.turn = [], [], [], [], [], []
        for i in range(heads + 2):
            if i < heads:
                self.diagonal.append(lane.mark("V"))
                self.row.append(lane.tile())
            if 0 <= i - 1 < heads:
                lane.drained_by(self.row[i - 1], "V")
                self.shifted.append(lane.mark("V"))
                self.exped.append(lane.mark("A"))
            if 0 <= i - 2 < heads:
                self.normed.append(lane.mark("V"))
                self.turn.append(lane.tile("V"))
        self.done = self.turn[-1].drained
        self.time = 8.0 * (heads + 2)

    def t(self, pe):
        k = self.k
        wait_all(pe, self.after)
        for i in range(self.heads + 2):
            if i < self.heads:
                fill(pe, self.row[i])
                pe.wait_ge(*self.diagonal[i].at)
                for t in range(NT):
                    mm = pe.matmul(self.row[i].ps[:, t * P:(t + 1) * P], k.ones, self.diag[i % 2][:, t, :],
                                   start=True, stop=True)
                mm.then_inc(*self.row[i].filled.by)
            if 0 <= i - 2 < self.heads:
                h = i - 2
                fill(pe, self.turn[h])
                pe.wait_ge(*self.normed[h].at)
                for s in range(NT):
                    for t in range(NT):
                        mm = pe.transpose(self.turn[h].ps[:, s * N + t * P:s * N + (t + 1) * P],
                                          self.e[h % 2][:, t, s * P:(s + 1) * P], k.ident)
                mm.then_inc(*self.turn[h].filled.by)
            yield 8.0

    def v(self, dve):
        step = lambda ins: self.lane.step("V", dve, ins)
        wide = lambda ap: ap.unsqueeze(2).to_broadcast([P, NT, N])
        wait_all(dve, self.after)
        for i in range(self.heads + 2):
            if i < self.heads:
                for t in range(NT):
                    ins = dve.tensor_scalar(self.diag[i % 2][:, t, :], self.k.ident, self.a_src[:, t, i:i + 1], None,
                                            ALU.mult)
                ins.then_inc(*self.diagonal[i].by)
            if 0 <= i - 1 < self.heads:
                h = i - 1
                e = self.e[h % 2]
                row = self.row[h]
                if h >= 1:
                    dve.wait_ge(*self.shifted[h - 1].at)
                if h >= 2:
                    dve.wait_ge(*self.turn[h - 2].filled.at)
                dve.wait_ge(*row.filled.at)
                for t in range(NT):
                    ins = dve.tensor_scalar(e[:, t, :], row.ps[:, 0:N], self.a_dst[:, t, h:h + 1], None, ALU.add)
                ins.then_inc(*row.drained.by)
                dve.wait_ge(*row.drained.at)
                step(dve.scalar_tensor_tensor(out=e, in0=e, scalar=0.2, in1=e, op0=ALU.mult, op1=ALU.max))
                step(dve.tensor_tensor(e, e, self.mask, ALU.mult))
                step(dve.tensor_tensor(e, e, self.neg, ALU.add))
                step(dve.tensor_reduce(self.top, e, AX.X, ALU.max))
                dve.tensor_tensor(e, e, wide(self.top), ALU.subtract).then_inc(*self.shifted[h].by)
            if 0 <= i - 2 < self.heads:
                h = i - 2
                e = self.e[h % 2]
                dve.wait_ge(*self.exped[h].at)
                if h >= 1:
                    dve.wait_ge(*self.normed[h - 1].at)
                step(dve.tensor_tensor(e, e, self.adj, ALU.mult))
                step(dve.tensor_reduce(self.total, e, AX.X, ALU.add))
                if self.guard:
                    step(dve.tensor_scalar(self.total, self.total, 0.5, None, ALU.max))
                step(dve.reciprocal(self.total, self.total))
                dve.tensor_tensor(e, e, wide(self.total), ALU.mult).then_inc(*self.normed[h].by)
                dve.wait_ge(*self.turn[h].filled.at)
                dve.tensor_copy(self.out[:, h, :, :], self.turn[h].ps.rearrange("p (s n) -> p s n", s=NT)).then_inc(
                    *self.turn[h].drained.by)
            yield 8.0

    def a(self, act):
        for i in range(self.heads + 2):
            if 0 <= i - 1 < self.heads:
                h = i - 1
                act.wait_ge(*self.shifted[h].at)
                act.activation(self.e[h % 2], self.e[h % 2], ACT.Exp).then_inc(*self.exped[h].by)
            yield 8.0


class AggregateTokens(Stage):
    time = 8.0

    def __init__(self, lane, k, probsT, heads, h, drain, after=(), drain_after=()):
        super().__init__(lane)
        self.probsT, self.heads, self.h, self.drain = probsT, heads, h, drain
        self.after, self.drain_after = after, drain_after
        self.tiles = [lane.tile("V") for _ in range(2 * NT)]
        self.done = self.tiles[-1].drained

    def t(self, pe):
        wait_all(pe, self.after)
        width = min(D // self.heads, COLS)
        for i, tile in enumerate(self.tiles):
            t, g = divmod(i, 2)
            fill(pe, tile)
            for a in range(0, COLS, width):
                head = (g * COLS + a) * self.heads // D
                for s in range(NT):
                    mm = pe.matmul(tile.ps[:, a:a + width], self.probsT[:, head, s, t * P:(t + 1) * P],
                                   self.h[:, s, g * COLS + a:g * COLS + a + width], start=(s == 0), stop=(s == NT - 1))
            mm.then_inc(*tile.filled.by)
            yield self.time / 4

    def v(self, dve):
        wait_all(dve, self.drain_after)
        for i, tile in enumerate(self.tiles):
            t, g = divmod(i, 2)
            dve.wait_ge(*tile.filled.at)
            self.drain(dve, t, g, tile.ps[:, 0:COLS]).then_inc(*tile.drained.by)
            yield self.time / 4


class HeadMatrices(Stage):
    time = 8.0

    def __init__(self, lane, k, xT, both, outs, after=()):
        super().__init__(lane)
        self.xT, self.both, self.outs, self.after = xT, both, outs, after
        self.loads = [both]
        self.tiles = [lane.tile("V") for _ in range(2 * 2 * NT)]
        both.freed = self.tiles[-1].filled
        self.done = self.tiles[-1].drained

    def t(self, pe):
        wait_all(pe, self.after)
        pe.wait_ge(*self.both.at)
        for i, tile in enumerate(self.tiles):
            o, t, g = i // 4, i // 2 % 2, i % 2
            fill(pe, tile)
            for c in range(3):
                mm = pe.matmul(tile.ps[:, c * P:(c + 1) * P], self.xT[:, 3 * g + c, t * P:(t + 1) * P],
                               self.both.ap[:, o * P:(o + 1) * P], start=True, stop=True)
            mm.then_inc(*tile.filled.by)
            yield 1.0

    def v(self, dve):
        for i, tile in enumerate(self.tiles):
            o, t, g = i // 4, i // 2 % 2, i % 2
            dve.wait_ge(*tile.filled.at)
            dve.tensor_copy(half(self.outs[o], t, g), tile.ps[:, 0:COLS]).then_inc(*tile.drained.by)
            yield 1.0


class PolynomialAttention(Stage):

    def __init__(self, lane, k, qT, kT, v, outT, num, inv, scale, after=()):
        super().__init__(lane)
        self.k, self.qT, self.kT, self.value, self.outT, self.num, self.inv = k, qT, kT, v, outT, num, inv
        self.scale, self.after = scale, after
        self.score, self.out, self.raised = [], [], []
        for i in range(H + 1):
            if i < H:
                self.score.append(lane.tile("A"))
                self.raised.append(lane.mark("V"))
            if i >= 1:
                self.out.append(lane.tile("V"))
        self.done = self.out[-1].drained
        self.time = 4.5 * (H + 1)

    def t(self, pe):
        wait_all(pe, self.after)
        for i in range(H + 1):
            if i < H:
                c, r = i // 2, (i % 2) * DH
                fill(pe, self.score[i])
                for m in range(NT):
                    mm = pe.matmul(self.score[i].ps[:, m * N:(m + 1) * N], self.kT[r:r + DH, c, m * P:(m + 1) * P],
                                   self.qT[r:r + DH, c, :], start=True, stop=True)
                mm.then_inc(*self.score[i].filled.by)
            if i >= 1:
                h = i - 1
                fill(pe, self.out[h])
                pe.wait_ge(*self.raised[h].at)
                num = self.num[h % 2]
                for m in range(NT):
                    pe.matmul(self.out[h].ps[:, 0:N], self.value[:, m, (h // 2) * P:(h // 2 + 1) * P], num[:, m, :],
                              start=(m == 0), stop=(m == NT - 1))
                for m in range(NT):
                    mm = pe.matmul(self.out[h].ps[:, N:2 * N], self.k.ones, num[:, m, :],
                                   start=(m == 0), stop=(m == NT - 1))
                mm.then_inc(*self.out[h].filled.by)
            yield 4.5

    def a(self, act):
        for i in range(H + 1):
            if i < H:
                act.wait_ge(*self.score[i].filled.at)
                if i >= 2:
                    act.wait_ge(*self.out[i - 2].filled.at)
                act.activation(self.num[i % 2], self.score[i].ps.rearrange("p (m n) -> p m n", m=NT), ACT.Square,
                               bias=self.k.ones[:, 0:1], scale=self.scale).then_inc(*self.score[i].drained.by)
            yield 4.5

    def v(self, dve):
        for i in range(H + 1):
            if i < H:
                dve.wait_ge(*self.score[i].drained.at)
                dve.tensor_scalar(self.num[i % 2], self.num[i % 2], 1.0, None, ALU.add).then_inc(*self.raised[i].by)
            if i >= 1:
                h = i - 1
                c, r = h // 2, (h % 2) * DH
                dve.wait_ge(*self.out[h].filled.at)
                if h:
                    dve.wait_ge(*self.out[h - 1].drained.at)
                self.lane.step("V", dve, dve.reciprocal(self.inv[r:r + DH, :], self.out[h].ps[r:r + DH, N:2 * N]))
                dve.tensor_tensor(self.outT[r:r + DH, c, :], self.out[h].ps[r:r + DH, 0:N], self.inv[r:r + DH, :],
                                  ALU.mult).then_inc(*self.out[h].drained.by)
            yield 4.5


class RouteScores(Stage):
    time = 25.0

    def __init__(self, lane, k, xT, wr_rep, scores, tmp, mixT, mask, small, take, after=()):
        super().__init__(lane)
        self.k, self.xT, self.wr_rep, self.scores, self.tmp, self.mixT = k, xT, wr_rep, scores, tmp, mixT
        self.mask, self.small, self.take, self.after = mask, small, take, after
        self.spread = lane.mark("V")
        self.tile = lane.tile("A")
        self.done = lane.mark("V")

    def t(self, pe):
        wait_all(pe, self.after)
        pe.wait_ge(*self.spread.at)
        fill(pe, self.tile)
        for c in range(KC):
            mm = pe.matmul(self.tile.ps[:, 0:N], self.wr_rep[:, c, :], self.xT[:, c, :], start=(c == 0),
                           stop=(c == KC - 1))
        mm.then_inc(*self.tile.filled.by)
        yield self.time

    def a(self, act):
        act.wait_ge(*self.tile.filled.at)
        act.activation(self.scores, self.tile.ps[:, 0:N], ACT.Sigmoid, bias=self.k.short("br")).then_inc(
            *self.tile.drained.by)
        yield self.time

    def v(self, dve):
        k = self.k
        step = lambda ins: self.lane.step("V", dve, ins)
        wait_all(dve, self.after)
        a, z = NARROW["wr"][0], NARROW["wr"][0] + 1
        dve.tensor_copy(self.wr_rep, k.narrow[:, :, a:z].to_broadcast([P, KC, P])).then_inc(*self.spread.by)
        dve.wait_ge(*self.tile.drained.at)
        own, rank, total = self.small[:, 0:2], self.small[:, 2:4], self.small[:, 4:5]
        pooled = self.small[:, 8:8 + KC]
        two = self.tmp[:, 0, :].rearrange("p (t j) -> p t j", t=NT)
        step(dve.tensor_tensor(two, self.scores.rearrange("p (t j) -> p t j", t=NT),
                               k.ident.unsqueeze(1).to_broadcast([P, NT, P]), ALU.mult))
        step(dve.tensor_reduce(own, two, AX.X, ALU.add))
        for t in range(NT):
            step(dve.tensor_scalar(self.tmp[:, 0, :], self.scores, own[:, t:t + 1], None, ALU.is_equal))
            step(dve.tensor_scalar(self.tmp[:, 1, :], k.iota, k.rowid[:, t:t + 1], None, ALU.is_lt))
            step(dve.tensor_tensor(self.tmp[:, 0, :], self.tmp[:, 0, :], self.tmp[:, 1, :], ALU.mult))
            step(dve.tensor_scalar(self.tmp[:, 1, :], self.scores, own[:, t:t + 1], None, ALU.is_lt))
            step(dve.tensor_tensor(self.tmp[:, 0, :], self.tmp[:, 0, :], self.tmp[:, 1, :], ALU.add))
            step(dve.tensor_reduce(rank[:, t:t + 1], self.tmp[:, 0, :], AX.X, ALU.add))
        step(dve.tensor_scalar(self.mask, rank, float(self.take), None, ALU.is_lt))
        step(dve.tensor_tensor(self.tmp, self.xT, self.scores.unsqueeze(1).to_broadcast([P, KC, N]), ALU.mult))
        step(dve.tensor_reduce(pooled, self.tmp, AX.X, ALU.add))
        step(dve.tensor_reduce(total, self.scores, AX.X, ALU.add))
        step(dve.tensor_scalar(total, total, 1e-6, None, ALU.add))
        step(dve.reciprocal(total, total))
        step(dve.tensor_scalar(pooled, pooled, total, None, ALU.mult))
        for c in range(KC):
            ins = dve.scalar_tensor_tensor(out=self.mixT[:, c, :], in0=self.scores, scalar=pooled[:, c:c + 1],
                                           in1=self.xT[:, c, :], op0=ALU.mult, op1=ALU.add)
        ins.then_inc(*self.done.by)
        dve.wait_ge(*self.done.at)
        yield self.time


class HeadNorm(Stage):
    time = 10.0

    def __init__(self, lane, k, x, tmp, small, after=()):
        super().__init__(lane)
        self.x, self.tmp, self.small, self.after = x, tmp, small[:, 0:NT * H], after
        self.power = Power(lane, k, self.small, INVERSE_ROOT)
        self.done = lane.mark("V")

    def p(self, pool):
        self.power.p(pool)
        yield self.time

    def v(self, dve):
        step = lambda ins: self.lane.step("V", dve, ins)
        heads = lambda ap: ap.rearrange("p t (h d) -> p (t h) d", d=DH)
        x, tmp, m = heads(self.x), heads(self.tmp), self.small
        wide = m.unsqueeze(2).to_broadcast([P, NT * H, DH])
        wait_all(dve, self.after)
        step(dve.tensor_reduce(m, x, AX.X, ALU.add))
        step(dve.tensor_scalar(m, m, 1.0 / DH, None, ALU.mult))
        step(dve.tensor_tensor(x, x, wide, ALU.subtract))
        step(dve.tensor_tensor(tmp, x, x, ALU.mult))
        step(dve.tensor_reduce(m, tmp, AX.X, ALU.add))
        dve.tensor_scalar(m, m, 1.0 / DH, 1e-5, ALU.mult, ALU.add).then_inc(*self.power.ready.by)
        dve.wait_ge(*self.power.done.at)
        dve.tensor_tensor(x, x, wide, ALU.mult).then_inc(*self.done.by)
        dve.wait_ge(*self.done.at)
        yield self.time


class Adapters(Stage):
    time = 6.0

    def __init__(self, lane, k, xT, a_t, combine2, hw, experts, rank, after=()):
        super().__init__(lane)
        self.k, self.xT, self.a_t, self.combine2, self.hw, self.after = k, xT, a_t, combine2, hw, after
        self.experts, self.rank = experts, rank
        self.loads = [a_t]
        self.tile = lane.tile("V")
        a_t.freed = self.tile.filled
        self.done = lane.mark("V")

    def t(self, pe):
        wait_all(pe, self.after)
        pe.wait_ge(*self.a_t.at)
        fill(pe, self.tile)
        w = self.a_t.ap.rearrange("p (c n) -> p c n", c=KC)
        for t in range(NT):
            for c in range(KC):
                mm = pe.matmul(self.tile.ps[:, t * P:(t + 1) * P], self.xT[:, c, t * P:(t + 1) * P], w[:, c, :],
                               start=(c == 0), stop=(c == KC - 1))
        mm.then_inc(*self.tile.filled.by)
        yield self.time

    def v(self, dve):
        dve.wait_ge(*self.tile.filled.at)
        dve.tensor_tensor(self.hw, self.tile.ps[:, 0:N].rearrange("p (t n) -> p t n", t=NT),
                          self.k.short("ba").unsqueeze(1).to_broadcast([P, NT, P]), ALU.add).then_inc(
            *self.tile.drained.by)
        dve.wait_ge(*self.tile.drained.at)
        for t in range(NT):
            grouped = self.hw[:, t, :].rearrange("p (e r) -> p e r", e=self.experts)
            ins = dve.tensor_tensor(grouped, grouped,
                                    self.combine2[:, t, :].unsqueeze(2).to_broadcast([P, self.experts, self.rank]),
                                    ALU.mult)
        ins.then_inc(*self.done.by)
        dve.wait_ge(*self.done.at)
        yield self.time


class Activation(Stage):
    time = 1.5

    def __init__(self, lane, body, after=()):
        super().__init__(lane)
        self.body, self.after = body, after
        self.done = lane.mark("A")

    def a(self, act):
        wait_all(act, self.after)
        self.body(act).then_inc(*self.done.by)
        yield self.time


class AggregateRelu(Stage):
    time = 6.0

    def __init__(self, lane, k, h, probsT, out, bias, after=()):
        super().__init__(lane)
        self.k, self.h, self.probsT, self.out, self.bias, self.after = k, h, probsT, out, bias, after
        self.tiles = [lane.tile("A") for _ in range(KC)]
        self.done = self.tiles[-1].drained

    def t(self, pe):
        wait_all(pe, self.after)
        for c, tile in enumerate(self.tiles):
            fill(pe, tile)
            for s in range(NT):
                mm = pe.matmul(tile.ps[:, 0:N], self.h[:, s, c * P:(c + 1) * P], self.probsT[:, s, :],
                               start=(s == 0), stop=(s == NT - 1))
            mm.then_inc(*tile.filled.by)
            yield 1.0

    def a(self, act):
        for c, tile in enumerate(self.tiles):
            act.wait_ge(*tile.filled.at)
            act.activation(self.out[:, c, :], tile.ps[:, 0:N], ACT.Relu, bias=self.k.col(self.bias, c)).then_inc(
                *tile.drained.by)
            yield 1.0


class HalfDown(Stage):
    time = 8.0

    def __init__(self, lane, k, panel, xT, drain, after=()):
        super().__init__(lane)
        self.xT, self.drain, self.after = xT, drain, after
        self.panel = lane.panel(k.panel[panel])
        self.tiles = [lane.tile("V") for _ in range(2 * NT)]
        self.panel.freed = self.tiles[-1].filled
        self.loads = [self.panel]
        self.done = self.tiles[-1].drained

    def t(self, pe):
        wait_all(pe, self.after)
        pe.wait_ge(*self.panel.at)
        w = self.panel.ap.rearrange("p (k n) -> p k n", k=3)
        for i, tile in enumerate(self.tiles):
            t, g = divmod(i, 2)
            fill(pe, tile)
            for c in range(3):
                mm = pe.matmul(tile.ps[:, 0:COLS], self.xT[:, c, t * P:(t + 1) * P], w[:, c, g * COLS:(g + 1) * COLS],
                               start=(c == 0), stop=(c == 2))
            mm.then_inc(*tile.filled.by)
            yield 2.0

    def v(self, dve):
        for i, tile in enumerate(self.tiles):
            dve.wait_ge(*tile.filled.at)
            self.drain(dve, *divmod(i, 2), tile.ps[:, 0:COLS]).then_inc(*tile.drained.by)
            yield 2.0


class Fetch(Stage):
    time = 1.0

    def __init__(self, lane, sem, pairs, after=()):
        super().__init__(lane)
        self.sem, self.pairs, self.after = sem, pairs, after
        self.at = (sem, 16 * len(pairs))

    def s(self, sp):
        wait_all(sp, self.after)
        for ap, src in self.pairs:
            sp.dma_start(ap, src).then_inc(self.sem, 16)
        yield self.time


class Constants:

    def __init__(self, panel, ident, ones, blocks, minus_half, iota, rowid, adjT, adj, gcn, cols, narrow, shorts,
                 exponents, iota_int, rowid_int, edges_int, iota_bf, edges, dst_of, dis_row, dis_col, inv):
        self.panel, self.ident, self.ones, self.blocks, self.minus_half = panel, ident, ones, blocks, minus_half
        self.iota, self.rowid, self.adjT, self.adj, self.gcn = iota, rowid, adjT, adj, gcn
        self.cols, self.narrow, self.shorts, self.exponents = cols, narrow, shorts, exponents
        self.iota_int, self.rowid_int, self.edges_int, self.iota_bf = iota_int, rowid_int, edges_int, iota_bf
        self.edges, self.dst_of, self.dis_row, self.dis_col, self.inv = edges, dst_of, dis_row, dis_col, inv

    def col(self, name, c=0):
        a, n = COLUMNS[name]
        return self.cols[:, a + c:a + c + 1]

    def short(self, name):
        a, n = SHORT[name]
        return self.shorts[:, a:a + n]

    def narrow_of(self, name):
        a, n = NARROW[name]
        return self.narrow[:, :, a:a + n]


def copy(dst):
    return lambda eng, i, ps: eng.tensor_copy(dst[:, i, :], ps)


def copy_half(dst):
    return lambda eng, t, g, ps: eng.tensor_copy(half(dst, t, g), ps)


def scaled(dst, factor):
    return lambda eng, i, ps: eng.tensor_scalar(dst[:, i, :], ps, factor, None, ALU.mult)


def plus_col(k, dst, name, first=0):
    return lambda eng, i, ps: eng.tensor_scalar(dst[:, i, :], ps, k.col(name, first + i), None, ALU.add)


def affine(k, dst, weight, bias):
    return lambda eng, i, ps: eng.tensor_scalar(dst[:, i, :], ps, k.col(weight, i), k.col(bias, i), ALU.mult, ALU.add)


def head_affine(k, dst, weight, bias):
    return lambda eng, i, ps: eng.tensor_scalar(dst[:, i, :], ps, k.col(weight), k.col(bias), ALU.mult, ALU.add)


def plus_row(dst, row):
    return lambda eng, t, g, ps: eng.tensor_tensor(half(dst, t, g), ps, row.ap[:, g * COLS:(g + 1) * COLS], ALU.add)


def onto(dst):
    return lambda eng, t, g, ps: eng.tensor_tensor(half(dst, t, g), ps, half(dst, t, g), ALU.add)


def act_col(k, dst, func, name=None, first=0):
    def drain(eng, i, ps):
        if name is None:
            return eng.activation(dst[:, i, :], ps, func)
        return eng.activation(dst[:, i, :], ps, func, bias=k.col(name, first + i))
    return drain


def build(nc, x_in, src, dst, edge_type, panels, cols, rows, narrow, shorts, query_t, b2, rand, head_mats,
          a_t, bm, bb, out, last_layer=3):
    with ExitStack() as ctx:
        sb = lambda name, shape, dt=F32: ctx.enter_context(nc.sbuf_tensor(name, shape, dt))
        sem = lambda name: ctx.enter_context(nc.semaphore(name))
        arena = sb("arena", [P, 21 * UNIT])
        panel_ring = [sb(f"panel{i}", [P, 6 * COLS]) for i in range(7)]
        row_ring = [sb(f"row{i}", [P, D]) for i in range(3)]
        u = lambda i, n=1: arena[:, i * UNIT:(i + n) * UNIT]
        tok = lambda i: u(i).rearrange("p (t d) -> p t d", t=NT)
        fea = lambda i: u(i).rearrange("p (c n) -> p c n", c=KC)

        small_g, small_m = sb("small_g", [P, 188]), sb("small_m", [P, 104])
        shared_ints = u(15)[:, 0:512 + 96].bitcast(I32)
        graph_f = u(16)
        k = Constants(
            panel=[panels[i] for i in range(N_PANELS)],
            ident=sb("ident", [P, P])[:, :], ones=sb("ones", [P, P])[:, :], blocks=sb("blocks", [P, P])[:, :],
            minus_half=u(12)[:, 0:P], iota=sb("iota", [P, N])[:, :], rowid=sb("rowid", [P, NT])[:, :],
            adjT=u(17)[:, 0:512].rearrange("p (t n) -> p t n", t=NT), adj=sb("adj", [P, NT, N])[:, :, :],
            gcn=sb("gcn", [P, NT, N])[:, :, :],
            cols=sb("cols", [P, N_COLUMNS])[:, :], narrow=sb("narrow", [P, KC, N_NARROW])[:, :, :],
            shorts=sb("shorts", [P, N_SHORT])[:, :], exponents=sb("exponents", [P, 2])[:, :],
            iota_int=shared_ints[:, 0:256], rowid_int=shared_ints[:, 256:258],
            edges_int=shared_ints[:, 512:608].rearrange("p (i c) -> p i c", i=3),
            iota_bf=graph_f[:, 0:128].bitcast(BF16), edges=graph_f[:, 128:224].rearrange("p (i c) -> p i c", i=3),
            dst_of=graph_f[:, 224:320].rearrange("p (r c) -> p r c", r=R), dis_row=graph_f[:, 320:576],
            dis_col=graph_f[:, 576:578], inv=graph_f[:, 640:1408])

        banks = [ctx.enter_context(nc.psum_tensor(f"bank{i}", [P, 512], F32))[:, :] for i in range(8)]
        users = [None] * 8
        slots = Slots([r[:, :] for r in panel_ring], [sem(f"panel{i}_arrived") for i in range(7)])
        row_slots = Slots([r[:, :] for r in row_ring], [sem(f"row{i}_arrived") for i in range(3)])
        x_arrived, edges_arrived, small_arrived, query_arrived = (
            sem("x_arrived"), sem("edges_arrived"), sem("small_arrived"), sem("query_arrived"))
        adapters_arrived, out_written = sem("adapters_arrived"), sem("out_written")

        class At:
            def __init__(self, s, v):
                self.at = (s, v)

        def lane(name, which, pslots, rslots):
            return Lane(sem, name, [(banks[i], i) for i in which], users, slots, pslots, row_slots, rslots)

        def row(lane_, name):
            return lane_.row(rows[ROWS[name]:ROWS[name] + 1, :].to_broadcast([P, D]))

        k.edges_at = (edges_arrived, 48)
        cols_at = At(small_arrived, 48)
        X, XN, XNT = tok(0), tok(1), fea(2)
        segments = []

        S = lane("start", range(8), range(7), range(3))
        segments.append((S,))
        averages = tok(3)
        agg = u(4, 3).rearrange("p (c n) -> p c n", c=KC)
        zs = [arena[:, 4 * UNIT + i * 2048:4 * UNIT + (i + 1) * 2048] for i in range(3)]
        QG, QT = (u(i, 2).rearrange("p (c n) -> p c n", c=KC) for i in (8, 10))
        H1, H2, H3 = fea(12), fea(13), fea(14)

        consts = Setup(S, k)
        norm = LayerNorm(S, k, X, XN, 1e-5, small_g, after=[At(x_arrived, 16)])
        graph = Graph(S, k, (u(4, 2), u(6, 2)), averages, consts.done)
        turn = ToFeatures(S, k, XN, copy(XNT), after=[norm.done])

        G = lane("graph", (0, 1, 2, 3), (0, 1, 2, 3), (0, 1))
        M = lane("mix", (4, 5, 6, 7), (4, 5, 6), (2,))
        segments.append((G, M))
        qg = LinearFeatures(G, k, [(PANELS["qg_w"], QT)], KC, plus_col(k, QG, "bg"), "V", cols=B * L,
                            after=[At(query_arrived, 16)], drain_after=[cols_at])

        def rgcn(h, hT, panels_at, bias, after):
            a = Aggregate(G, k, h, averages, 768, agg, after=after)
            inputs = [(panels_at + 2 * r, agg[:, :, r * N:(r + 1) * N]) for r in range(R)]
            inputs.append((panels_at + 2 * R, hT))
            lin = LinearFeatures(G, k, inputs, KC, act_col(k, H1, ACT.Relu, bias), "A", after=[a.done])
            hg = LinearFeatures(G, k, [(PANELS["hg_w"], H1)], KC, copy(H2), "V", after=[lin.done])
            gate = GateSum(G, k, H2, QG, QT, H3, zs, after=[hg.done])
            alpha = LinearFeatures(G, k, [(PANELS["alpha_w"], H1), (PANELS["alpha_w"] + 2, H3)], KC,
                                   act_col(k, H2, ACT.Sigmoid, "bq"), "A", after=[gate.done])
            return GateMix(G, u(13), u(14), u(12), u(13), after=[alpha.done])

        first = rgcn(XN, XNT, PANELS["rel1"], "b1", [graph.done, turn.done])
        h_tok = tok(14)
        back = ToTokens(G, k, H2, copy_half(h_tok), after=[first.done])
        second = rgcn(h_tok, H2, PANELS["rel2"], "b2", [back.done])
        gnn_out = ToTokens(G, k, H2, onto(X), after=[second.done])

        a_, b_, c_, d_, e_, f_ = 15, 16, 17, 18, 19, 20
        m_after = [graph.done, turn.done, cols_at]
        m_norm = LayerNorm(M, k, XN, tok(e_), 1e-8, small_m, after=m_after)
        m_turn = ToFeatures(M, k, tok(e_), affine(k, fea(a_), "ln1w", "ln1b"), after=[m_norm.done])
        q = LinearFeatures(M, k, [(PANELS["l0_qkv"], fea(a_))], KC, plus_col(k, fea(b_), "l0_qb"), "V",
                           after=[m_turn.done])
        kb, vb = row(M, "l0_kb"), row(M, "l0_vb")
        key = LinearTokens(M, k, [(PANELS["l0_qkv"] + 2, fea(a_))], 2, plus_row(tok(c_), kb), drain_after=[kb],
                           rows=[kb])
        kb.freed = key.done
        val = LinearTokens(M, k, [(PANELS["l0_qkv"] + 4, fea(a_))], 2, plus_row(tok(d_), vb), drain_after=[vb],
                           rows=[vb])
        vb.freed = val.done
        elu_q = EluPlusOne(M, u(b_), u(e_), after=[q.done])
        elu_k = EluPlusOne(M, u(c_), u(f_), after=[key.done])
        states = u(a_)[:, 0:KC * P].rearrange("p (c e) -> p c e", c=KC)
        norms = u(a_)[:, KC * P:2 * KC * P].rearrange("p (c e) -> p c e", c=KC)

        def keep_states(eng, c, ps, step):
            eng.tensor_scalar(norms[:, c, :], k.blocks, ps[:, P:P + 1], None, ALU.mult)
            return eng.tensor_tensor(states[:, c, :], ps[:, 0:P], k.blocks, ALU.mult)

        kv = KeyValues(M, k, tok(c_), tok(d_), True, keep_states, after=[elu_k.done, val.done, elu_q.done])
        att = QueryStates(M, k, states, norms, fea(b_), fea(f_), u(e_)[:, 0:N], after=[kv.done])
        pb = row(M, "l0_projb")
        pre = Vector(M, lambda dve, step: dve.tensor_tensor(
            tok(e_), XN, pb.ap.unsqueeze(1).to_broadcast([P, NT, D]), ALU.add), rows=[pb], after=[att.done])
        proj = LinearTokens(M, k, [(PANELS["l0_proj"], fea(f_))], 2, onto(tok(e_)), after=[att.done])
        m_norm2 = LayerNorm(M, k, tok(e_), tok(b_), 1e-8, small_m, after=[proj.done])
        m_turn2 = ToFeatures(M, k, tok(b_), affine(k, fea(a_), "ln2w", "ln2b"), after=[m_norm2.done])
        hidden = [fea(b_), fea(c_), fea(d_), fea(f_)]
        for i in range(4):
            fc1 = LinearFeatures(M, k, [(PANELS["l0_fc1"] + 2 * i, fea(a_))], KC,
                                 act_col(k, hidden[i], ACT.Gelu, "l0_fc1b", 6 * i), "A", after=[m_turn2.done])
        fb = row(M, "l0_fc2b")
        pre2 = Vector(M, lambda dve, step: dve.tensor_tensor(
            tok(e_), tok(e_), fb.ap.unsqueeze(1).to_broadcast([P, NT, D]), ALU.add), rows=[fb])
        fc2 = LinearTokens(M, k, [(PANELS["l0_fc2"] + 2 * i, hidden[i]) for i in range(4)], 2, onto(tok(e_)),
                           after=[fc1.done])

        S = lane("main", range(8), range(7), range(3))
        segments.append((S,))

        def join(other, after, eps=1e-5):
            both = Vector(S, lambda dve, step: dve.tensor_tensor(X, X, other, ALU.add), after=after)
            n = LayerNorm(S, k, X, XN, eps, small_g, after=[both.done])
            return ToFeatures(S, k, XN, copy(XNT), after=[n.done])

        t0 = join(tok(e_), [gnn_out.done, fc2.done])
        rank = sb("rank", [P, 16])[:, :]
        Vector(S, lambda dve, step: dve.tensor_scalar(rank, k.iota[:, 0:16], -1.0, 16.0, ALU.mult, ALU.add))

        def narrow_place(i, e, at=0):
            return u(i)[:, at:at + NT * e].rearrange("p (t e) -> p t e", t=NT)

        comb0, picked0 = narrow_place(12, 8), narrow_place(12, 8, 32)
        left = [narrow_place(12, 10, 64 + 32 * i) for i in range(3)]
        left8 = [narrow_place(12, 8, 64 + 32 * i) for i in range(3)]
        gates0 = Logits(S, k, XNT, k.narrow_of("gate"), 8, [(0, 8)], comb0, small_g[:, 0:2], after=[t0.done])

        def combine0(dve, step):
            step(top_two(dve, step, comb0, picked0, small_g[:, 0:2], rank[:, 0:8], left8, 8))
            step(dve.tensor_tensor(comb0, comb0, picked0, ALU.mult))
            step(dve.tensor_reduce(small_g[:, 0:2], comb0, AX.X, ALU.add))
            step(dve.reciprocal(small_g[:, 0:2], small_g[:, 0:2]))
            return dve.tensor_tensor(comb0, comb0, small_g[:, 0:2].unsqueeze(2).to_broadcast([P, NT, 8]), ALU.mult)

        picked = Vector(S, combine0, time=4.0, after=[gates0.done])
        comb0T = u(13)[0:8, 0:N]
        turned0 = TurnNarrow(S, k, comb0, 8, comb0T, after=[picked.done])
        b2_row = S.row(b2, (8, D))
        ffn0 = Experts(S, k, XNT, X, comb0, comb0T, b2_row,
                       [u(14)[:, i * 768:(i + 1) * 768].rearrange("p (c n) -> p c n", c=3) for i in range(2)],
                       after=[turned0.done, t0.done])
        end = ffn0.done

        def next_norm(after):
            n = LayerNorm(S, k, X, XN, 1e-5, small_g, after=after)
            return ToFeatures(S, k, XN, copy(XNT), after=[n.done])

        if last_layer >= 1:
            t1 = next_norm([end])
            G = lane("graph1", (0, 1, 2, 3), (0, 1, 2), (0, 1))
            M = lane("mix1", (4, 5, 6, 7), (3, 4, 5, 6), (2,))
            segments.append((G, M))
            a = Aggregate(G, k, XN, k.gcn, N, fea(3), after=[t1.done])
            gb = row(G, "gcn_b")
            pre = Vector(G, lambda dve, step: dve.tensor_tensor(
                X, X, gb.ap.unsqueeze(1).to_broadcast([P, NT, D]), ALU.add), rows=[gb], after=[t1.done])
            gcn = LinearTokens(G, k, [(PANELS["l1_gcn"], fea(3))], 2, onto(X), after=[a.done])

            qs = LinearFeatures(M, k, [(PANELS["l1_q"], XNT)], KC, scaled(fea(15), float(DH) ** -0.25), "V",
                                after=[t1.done])
            v1 = LinearTokens(M, k, [(PANELS["l1_v"], XNT)], 2, copy_half(tok(16)))
            Vector(M, lambda dve, step: dve.memset(k.minus_half, -0.5))
            rf = u(4, 2).rearrange("p (h n) -> p h n", h=H)
            features = RandomFeatures(M, k, fea(15), fea(17), M.row(rand), rf,
                                      u(6, 2).rearrange("p (h n) -> p h n", h=H), small_m, after=[qs.done])
            codes = SparseCodes(M, k, rf, tok(16), u(8, 2).rearrange("p (t h m) -> p t h m", t=NT, h=H),
                                u(10).rearrange("p (h m) -> p h m", h=H), u(18)[:, 0:D], u(18)[:, D:2 * D],
                                u(11)[:, 0:D], u(11)[:, D:2 * D], fea(17), small_m, after=[features.done, v1.done])
            pb1 = row(M, "l1_projb")
            mix1 = LinearTokens(M, k, [(PANELS["l1_proj"], fea(17))], 2, plus_row(tok(19), pb1), after=[codes.done],
                                drain_after=[pb1], rows=[pb1])
            pb1.freed = mix1.done

            S = lane("main1", range(8), range(7), range(3))
            segments.append((S,))
            both = Vector(S, lambda dve, step: dve.tensor_tensor(X, X, tok(19), ALU.add), after=[gcn.done, mix1.done])
            hid = LayerNorm(S, k, X, tok(3), 1e-5, small_g, after=[both.done])
            nrm = LayerNorm(S, k, tok(3), tok(4), 1e-5, small_g, after=[hid.done])
            nT = ToFeatures(S, k, tok(4), affine(k, fea(5), "g1", "gb1"), after=[nrm.done])
            q1 = LinearFeatures(S, k, [(PANELS["l1_wq"], fea(5))], KC, plus_col(k, fea(6), "l1_bq"), "V",
                                after=[nT.done])
            k1 = LinearFeatures(S, k, [(PANELS["l1_wk"], fea(5))], KC, plus_col(k, fea(7), "l1_bk"), "V")
            vb1 = row(S, "l1_bv")
            v1b = LinearTokens(S, k, [(PANELS["l1_wv"], fea(5))], 2, plus_row(tok(8), vb1), drain_after=[vb1],
                               rows=[vb1])
            vb1.freed = v1b.done
            mask = small_g[:, 180:182]
            route = RouteScores(S, k, fea(5), u(17)[:, 0:D].rearrange("p (c n) -> p c n", c=KC), u(18)[:, 0:N],
                                fea(19), fea(10), mask, small_g, int(round(0.15 * N)), after=[nT.done])
            att1 = SoftmaxAttention(S, k, fea(6), fea(7), tok(8), fea(9), DH ** -0.5,
                                    [u(15)[:, i * 512:(i + 1) * 512].rearrange("p (t n) -> p t n", t=NT)
                                     for i in range(3)],
                                    [u(16)[:, i * 512:(i + 1) * 512].rearrange("p (t n) -> p t n", t=NT)
                                     for i in range(2)], small_m, after=[q1.done, k1.done, v1b.done, route.done])
            bo, bmr = row(S, "l1_bo"), row(S, "l1_bm")
            ao = LinearTokens(S, k, [(PANELS["l1_wo"], fea(9))], 2, plus_row(tok(11), bo), after=[att1.done],
                              drain_after=[bo], rows=[bo])
            bo.freed = ao.done
            mo = LinearTokens(S, k, [(PANELS["l1_wm"], fea(10))], 2, plus_row(tok(12), bmr), after=[route.done],
                              drain_after=[bmr], rows=[bmr])
            bmr.freed = mo.done

            def merge(dve, step):
                step(dve.tensor_scalar(small_g[:, 184:186], mask, -1.0, 1.0, ALU.mult, ALU.add))
                for t in range(NT):
                    ins = dve.tensor_scalar(tok(11)[:, t, :], tok(11)[:, t, :], mask[:, t:t + 1], None, ALU.mult)
                step(ins)
                for t in range(NT):
                    ins = dve.scalar_tensor_tensor(out=tok(12)[:, t, :], in0=tok(12)[:, t, :],
                                                   scalar=small_g[:, 184 + t:185 + t], in1=tok(11)[:, t, :],
                                                   op0=ALU.mult, op1=ALU.add)
                step(ins)
                step(dve.tensor_tensor(tok(12), tok(12), tok(3), ALU.add))
                return dve.tensor_tensor(X, X, tok(12), ALU.add)

            merged = Vector(S, merge, time=6.0, after=[ao.done, mo.done])
            n2 = LayerNorm(S, k, tok(12), tok(13), 1e-5, small_g, after=[merged.done])
            n2T = ToFeatures(S, k, tok(13), affine(k, fea(14), "g2", "gb2"), after=[n2.done])
            f1T = u(15)[:, 0:768].rearrange("p (c n) -> p c n", c=3)
            f1 = LinearFeatures(S, k, [(PANELS["l1_f1"], fea(14))], 3, act_col(k, f1T, ACT.Gelu, "l1_bf1"), "A",
                                after=[n2T.done])
            bf2 = row(S, "l1_bf2")
            pre = Vector(S, lambda dve, step: dve.tensor_tensor(
                X, X, bf2.ap.unsqueeze(1).to_broadcast([P, NT, D]), ALU.add), rows=[bf2], after=[merged.done])
            down = HalfDown(S, k, PANELS["l1_f2"], f1T, onto(X), after=[f1.done])
            end = down.done

        if last_layer >= 2:
            t2 = next_norm([end])
            G = lane("graph2", (0, 1, 2, 3), (0, 1, 2), (0, 1))
            M = lane("mix2", (4, 5, 6, 7), (3, 4, 5, 6), (2,))
            segments.append((G, M))
            view = lambda i, at: u(i)[:, at:at + 512].rearrange("p (t n) -> p t n", t=NT)
            edge_mask, edge_neg = view(6, 0), view(6, 512)

            def masks(adj):
                def body(dve, step):
                    step(dve.tensor_scalar(edge_mask, adj, 0.5, None, ALU.is_gt))
                    return dve.tensor_scalar(edge_neg, edge_mask, -1.0, 1e30, ALU.add, ALU.mult)
                return body

            Vector(G, masks(k.adj), after=[t2.done])

            def gat(h, weights, inT, s_row, d_row, after):
                rs, rd = row(G, s_row), row(G, d_row)
                lin = LinearTokens(G, k, [(weights, inT)], 2, copy_half(h), after=after)

                def scores(dve, step):
                    for r_, at in ((rs, 32), (rd, 34)):
                        step(dve.tensor_tensor(tok(4), h, r_.ap.unsqueeze(1).to_broadcast([P, NT, D]), ALU.mult))
                        ins = dve.tensor_reduce(small_g[:, at:at + 2], tok(4), AX.X, ALU.add)
                        if at == 32:
                            step(ins)
                    return ins

                s_ = Vector(G, scores, time=7.0, after=[lin.done], rows=[rs, rd])
                return EdgeSoftmax(G, k, small_g[:, 32:34].unsqueeze(2), small_g[:, 34:36].unsqueeze(2), 1, k.adj,
                                   edge_mask, edge_neg,
                                   [u(5)[:, 512 + 256 * i:768 + 256 * i].rearrange("p (t n) -> p t n", t=NT)
                                    for i in range(2)], [view(5, 0)] * 2, small_g,
                                   u(5)[:, 1024:1536].rearrange("p (h s n) -> p h s n", h=1, s=NT), False,
                                   after=[s_.done])

            e1 = gat(tok(3), PANELS["l2_gat1"], XNT, "att_s1", "att_d1", [t2.done])
            g1 = AggregateRelu(G, k, tok(3), u(5)[:, 1024:1536].rearrange("p (s n) -> p s n", s=NT), fea(7),
                               "gat_b1", after=[e1.done])
            e2 = gat(tok(8), PANELS["l2_gat2"], fea(7), "att_s2", "att_d2", [g1.done])
            gb2 = row(G, "gat_b2")
            pre = Vector(G, lambda dve, step: dve.tensor_tensor(
                X, X, gb2.ap.unsqueeze(1).to_broadcast([P, NT, D]), ALU.add), rows=[gb2], after=[e2.done])
            g2 = AggregateTokens(G, k, u(5)[:, 1024:1536].rearrange("p (h s n) -> p h s n", h=1, s=NT), 1, tok(8),
                                 onto(X), after=[e2.done], drain_after=[pre.done])

            key = LinearTokens(M, k, [(PANELS["l2_kv"], XNT)], 2, copy_half(tok(15)), after=[t2.done])
            val = LinearTokens(M, k, [(PANELS["l2_kv"] + 2, XNT)], 2, copy_half(tok(16)))
            q = LinearFeatures(M, k, [(PANELS["l2_q"], XNT)], KC, act_col(k, fea(17), ACT.Gelu), "A")
            gstates = u(18)[:, 0:KC * P].rearrange("p (c e) -> p c e", c=KC)

            def keep2(eng, c, ps, step):
                return eng.scalar_tensor_tensor(out=gstates[:, c, :], in0=ps[:, 0:P], scalar=float(DH) ** -0.5,
                                                in1=k.blocks, op0=ALU.mult, op1=ALU.mult)

            kv = KeyValues(M, k, tok(15), tok(16), False, keep2, after=[key.done, val.done])
            kvg = Activation(M, lambda act: act.activation(gstates, gstates, ACT.Gelu), after=[kv.done])
            att = QueryStates(M, k, gstates, None, fea(17), fea(19), None, after=[kvg.done, q.done])
            pb2 = row(M, "l2_projb")
            mix2 = LinearTokens(M, k, [(PANELS["l2_proj"], fea(19))], 2, plus_row(tok(20), pb2), after=[att.done],
                                drain_after=[pb2], rows=[pb2])
            pb2.freed = mix2.done

            S = lane("main2", range(8), range(7), range(3))
            segments.append((S,))
            t2b = join(tok(20), [g2.done, mix2.done])
            E2 = 14
            probs2 = narrow_place(12, E2)
            picked2 = narrow_place(12, 10, 32)
            gates2 = narrow_place(12, H, 192)
            lg = Logits(S, k, XNT, k.narrow_of("gates"), E2, [(0, 10), (10, 12), (12, 14)], probs2, small_g[:, 0:2],
                        after=[t2b.done])

            def head_gates(dve, step):
                routed = probs2[:, :, 0:10]
                best = small_g[:, 0:2]
                step(top_two(dve, step, routed, picked2, best, rank[:, 0:10], left, 10))
                step(dve.tensor_tensor(routed, routed, picked2, ALU.mult))
                step(dve.tensor_reduce(best, routed, AX.X, ALU.add))
                step(dve.tensor_scalar(best, best, float(np.finfo(np.float32).eps), None, ALU.max))
                step(dve.reciprocal(best, best))
                step(dve.tensor_scalar(best, best, 4.0, None, ALU.mult))
                step(dve.tensor_tensor(best, best, probs2[:, :, 11], ALU.mult))
                step(dve.tensor_tensor(gates2[:, :, 2:H], routed, best.unsqueeze(2).to_broadcast([P, NT, 10]),
                                       ALU.mult))
                step(dve.tensor_scalar(best, probs2[:, :, 10], 4.0, None, ALU.mult))
                return dve.tensor_tensor(gates2[:, :, 0:2], probs2[:, :, 12:14],
                                         best.unsqueeze(2).to_broadcast([P, NT, 2]), ALU.mult)

            hg2 = Vector(S, head_gates, time=5.0, after=[lg.done])
            for dst_, name, at in ((3, "l2_qb", 0), (4, "l2_kb", 2), (5, "l2_vb", 4)):
                r_ = row(S, name)
                lin = LinearTokens(S, k, [(PANELS["l2_qkv"] + at, XNT)], 2, plus_row(tok(dst_), r_),
                                   after=[t2b.done], drain_after=[r_], rows=[r_])
                r_.freed = lin.done
            qn = HeadNorm(S, k, tok(3), tok(6), small_g, after=[lin.done])
            kn = HeadNorm(S, k, tok(4), tok(6), small_g, after=[qn.done])
            qT = ToFeatures(S, k, tok(3), head_affine(k, fea(7), "qnw", "qnb"), after=[qn.done])
            kT = ToFeatures(S, k, tok(4), head_affine(k, fea(8), "knw", "knb"), after=[kn.done])
            att2 = SoftmaxAttention(S, k, fea(7), fea(8), tok(5), fea(9), DH ** -0.5,
                                    [view(15, i * 512) for i in range(3)], [view(16, i * 512) for i in range(2)],
                                    small_m, gates=gates2, after=[qT.done, kT.done, lin.done, hg2.done])
            bo2 = row(S, "l2_bo")
            pre = Vector(S, lambda dve, step: dve.tensor_tensor(
                X, X, bo2.ap.unsqueeze(1).to_broadcast([P, NT, D]), ALU.add), rows=[bo2])
            wo2 = LinearTokens(S, k, [(PANELS["l2_wo"], fea(9))], 2, onto(X), after=[att2.done])
            end = wo2.done

        if last_layer >= 3:
            t3 = next_norm([end])
            G = lane("graph3", (0, 1, 2, 3), (0, 1, 2), (0, 1))
            M = lane("mix3", (4, 5, 6, 7), (3, 4, 5, 6), (2,))
            segments.append((G, M))
            edge_mask3, edge_neg3 = view(7, 0), view(7, 512)

            def masks3(dve, step):
                for t in range(NT):
                    blk = k.adj[:, t, t * P:(t + 1) * P]
                    ins = dve.tensor_tensor(blk, blk, k.ident, ALU.subtract)
                step(ins)
                step(dve.tensor_scalar(edge_mask3, k.adj, 0.5, None, ALU.is_gt))
                return dve.tensor_scalar(edge_neg3, edge_mask3, -1.0, 1e30, ALU.add, ALU.mult)

            Vector(G, masks3, after=[t3.done])
            mats = G.load(row_slots, 0, head_mats, (P, 2 * P))
            ft = HeadMatrices(G, k, XNT, mats, (tok(3), tok(4)), after=[t3.done])
            G.nrow = 1
            al = row(G, "attn_l")
            ar = row(G, "attn_r")

            def head_scores(dve, step):
                for r_, at in ((al, 64), (ar, 96)):
                    step(dve.tensor_tensor(tok(5), tok(3), r_.ap.unsqueeze(1).to_broadcast([P, NT, D]), ALU.mult))
                    ins = dve.tensor_reduce(small_g[:, at:at + NT * H],
                                            tok(5).rearrange("p t (h d) -> p (t h) d", h=H), AX.X, ALU.add)
                    if at == 64:
                        step(ins)
                return ins

            hs = Vector(G, head_scores, time=7.0, after=[ft.done], rows=[al, ar])
            columns = lambda at: small_g[:, at:at + NT * H].rearrange("p (t h) -> p t h", t=NT)
            pT = u(8, 4).rearrange("p (h s n) -> p h s n", h=H, s=NT)
            es = EdgeSoftmax(G, k, columns(64), columns(96), H, k.adj, edge_mask3, edge_neg3,
                             [u(7)[:, 1024 + 256 * i:1280 + 256 * i].rearrange("p (t n) -> p t n", t=NT)
                              for i in range(2)], [view(6, 0), view(6, 512)], small_g, pT, True, after=[hs.done])
            res = tok(4)
            ag = AggregateTokens(G, k, pT, H, tok(3), onto(res), after=[es.done])

            def add_relu(dve, step):
                step(dve.tensor_scalar(res, res, 0.0, None, ALU.max))
                return dve.tensor_tensor(X, X, res, ALU.add)

            g3 = Vector(G, add_relu, after=[ag.done])

            q = LinearFeatures(M, k, [(PANELS["l3_qk"], XNT)], KC, plus_col(k, fea(15), "l3_qb"), "V",
                               after=[t3.done])
            key = LinearFeatures(M, k, [(PANELS["l3_qk"] + 2, XNT)], KC, plus_col(k, fea(16), "l3_kb"), "V")
            vb3 = row(M, "l3_vb")
            val = LinearTokens(M, k, [(PANELS["l3_v"], XNT)], 2, plus_row(tok(17), vb3), drain_after=[vb3],
                               rows=[vb3])
            vb3.freed = val.done
            poly = PolynomialAttention(M, k, fea(15), fea(16), tok(17), fea(18),
                                       [view(19, 0), view(19, 512)], u(19)[:, 1024:1280], DH ** -0.5,
                                       after=[q.done, key.done, val.done])
            pb3 = row(M, "l3_projb")
            mix3 = LinearTokens(M, k, [(PANELS["l3_proj"], fea(18))], 2, plus_row(tok(20), pb3), after=[poly.done],
                                drain_after=[pb3], rows=[pb3])
            pb3.freed = mix3.done

            S = lane("main3", range(8), range(7), range(3))
            segments.append((S,))
            t3b = join(tok(20), [g3.done, mix3.done])
            EX, RK = 8, 16
            bm_place, bb_place = u(7, 2)[:, 0:3 * D], u(9, 2)[0:EX, 0:3 * D]
            fetch = Fetch(S, adapters_arrived, [(bm_place, bm), (bb_place, bb)], after=[g3.done, mix3.done])
            comb3 = narrow_place(12, EX)
            picked3 = narrow_place(12, EX, 32)
            lg3 = Logits(S, k, XNT, k.narrow_of("l3_gate"), EX, [(0, EX)], comb3, small_g[:, 0:2],
                         bias=k.short("bg"), after=[t3b.done])

            def combine3(dve, step):
                step(top_two(dve, step, comb3, picked3, small_g[:, 0:2], rank[:, 0:EX], left8, EX))
                return dve.scalar_tensor_tensor(out=comb3, in0=comb3, scalar=2.0, in1=picked3, op0=ALU.mult,
                                                op1=ALU.mult)

            cb3 = Vector(S, combine3, time=4.0, after=[lg3.done])
            comb3T = u(13)[0:EX, 0:N]
            c3T = TurnNarrow(S, k, comb3, EX, comb3T, after=[cb3.done])
            hw = u(14)[:, 0:N].rearrange("p (t n) -> p t n", t=NT)
            hwT = u(14)[:, N:2 * N]
            ad = Adapters(S, k, XNT, S.row(a_t), comb3, hw, EX, RK, after=[cb3.done])
            hT = TurnNarrow(S, k, hw, P, hwT, after=[ad.done])

            def feature_tail(at):
                def tail(pe, o, ps):
                    c0 = at + o * P
                    pe.matmul(ps, bm_place[:, c0:c0 + P], hwT, start=False, stop=False)
                    return pe.matmul(ps, bb_place[:, c0:c0 + P], comb3T, start=False, stop=True)
                return tail

            def token_tail(pe, t, g, ps):
                c0 = 2 * D + g * COLS
                pe.matmul(ps, hwT[:, t * P:(t + 1) * P], bm_place[:, c0:c0 + COLS], start=False, stop=False)
                return pe.matmul(ps, comb3T[:, t * P:(t + 1) * P], bb_place[:, c0:c0 + COLS], start=False, stop=True)

            tail_after = [fetch, hT.done, c3T.done]
            q3 = LinearFeatures(S, k, [(PANELS["l3_wq"], XNT)], KC, plus_col(k, fea(3), "l3_bqk"), "V",
                                after=[t3b.done], tail=feature_tail(0), tail_after=tail_after)
            k3 = LinearFeatures(S, k, [(PANELS["l3_wk"], XNT)], KC, plus_col(k, fea(4), "l3_bqk", KC), "V",
                                tail=feature_tail(D))
            vb4 = row(S, "l3_bv")
            v3 = LinearTokens(S, k, [(PANELS["l3_wv"], XNT)], 2, plus_row(tok(5), vb4), drain_after=[vb4],
                              rows=[vb4], tail=token_tail)
            vb4.freed = v3.done
            att3 = SoftmaxAttention(S, k, fea(3), fea(4), tok(5), fea(6), DH ** -0.5,
                                    [view(15, i * 512) for i in range(3)], [view(16, i * 512) for i in range(2)],
                                    small_m, after=[q3.done, k3.done, v3.done])
            bo3 = row(S, "l3_bo")
            pre = Vector(S, lambda dve, step: dve.tensor_tensor(
                X, X, bo3.ap.unsqueeze(1).to_broadcast([P, NT, D]), ALU.add), rows=[bo3])
            wo3 = LinearTokens(S, k, [(PANELS["l3_wo"], fea(6))], 2, onto(X), after=[att3.done])
            end = wo3.done

        def run(part, eng):
            for lanes in segments:
                side_by_side([lane_.stages for lane_ in lanes], part, eng)

        block = ctx.enter_context(nc.Block())

        @block.sync
        def _(sp):
            sp.dma_start(X, x_in.rearrange("(t p) d -> p t d", p=P)).then_inc(x_arrived, 16)
            for i, v_ in enumerate((src, dst, edge_type)):
                sp.dma_start(k.edges_int[:, i, :], v_.rearrange("(p c) -> p c", p=P)).then_inc(edges_arrived, 16)
            sp.dma_start(k.cols, cols).then_inc(small_arrived, 16)
            sp.dma_start(k.narrow, narrow).then_inc(small_arrived, 16)
            sp.dma_start(k.shorts, shorts.to_broadcast([P, N_SHORT])).then_inc(small_arrived, 16)
            sp.dma_start(QT, query_t).then_inc(query_arrived, 16)
            run("s", sp)
            sp.wait_ge(*end.at)
            sp.dma_start(out.rearrange("(t p) d -> p t d", p=P), X).then_inc(out_written, 16)
            sp.wait_ge(out_written, 16)

        @block.tensor
        def _(pe):
            run("t", pe)

        @block.vector
        def _(dve):
            run("v", dve)

        @block.scalar
        def _(act):
            run("a", act)

        @block.gpsimd
        def _(pool):
            run("p", pool)


def kernel(**inputs):
    import concourse.bacc as bacc
    from concourse.bass_utils import run_bass_kernel_spmd

    w = {name: np.asarray(a) for name, a in inputs.items()}

    def cut(m, k=KC, n=COLS):
        parts = []
        for c in range(0, m.shape[1], n):
            parts.append(np.ascontiguousarray(
                m[:, c:c + n].reshape(k, P, n).transpose(1, 0, 2)).reshape(P, k * n))
        return parts

    def stack(mats):
        return [p for m in mats for p in cut(m)]

    rel1, rel2 = w["L0_gnn_W_rel1"], w["L0_gnn_W_rel2"]
    wg, wq = w["L0_gnn_Wg"], w["L0_gnn_Wq"]
    fc2 = w["L0_mix_fc2_w"]
    l3_w = w["L3_ffn_Wqkv"]
    panel_groups = {
        "qg_w": stack([wg[:, D:].T]), "rel1": stack([*rel1, w["L0_gnn_W_root1"]]),
        "hg_w": stack([wg[:, :D].T]), "alpha_w": stack([wq[:, :D].T, wq[:, D:].T]),
        "rel2": stack([*rel2, w["L0_gnn_W_root2"]]),
        "l0_qkv": cut(w["L0_mix_qkv_w"]), "l0_proj": cut(w["L0_mix_proj_w"]), "l0_fc1": cut(w["L0_mix_fc1_w"]),
        "l0_fc2": stack([fc2[i * D:(i + 1) * D] for i in range(4)]),
        "l0_w1": stack(list(w["L0_ffn_w1"])), "l0_w2": [cut(m, 3, D)[0] for m in w["L0_ffn_w2"]],
        "l1_gcn": cut(w["L1_gnn_W"]), "l1_q": cut(w["L1_mix_Wqkv"][:, :D]), "l1_v": cut(w["L1_mix_Wqkv"][:, D:]),
        "l1_proj": cut(w["L1_mix_Wproj"]), "l1_wq": cut(w["L1_ffn_Wq"]), "l1_wk": cut(w["L1_ffn_Wk"]),
        "l1_wv": cut(w["L1_ffn_Wv"]), "l1_wo": cut(w["L1_ffn_Wo"]), "l1_wm": cut(w["L1_ffn_Wm"]),
        "l1_f1": cut(w["L1_ffn_W1"]), "l1_f2": cut(w["L1_ffn_W2"], 3, D),
        "l2_gat1": cut(w["L2_gnn_W1"]), "l2_gat2": cut(w["L2_gnn_W2"]),
        "l2_q": cut(w["L2_mix_w_qkv"][:, :D]), "l2_kv": cut(w["L2_mix_w_qkv"][:, D:]),
        "l2_proj": cut(w["L2_mix_w_proj"]), "l2_qkv": cut(w["L2_ffn_qkv_w"]), "l2_wo": cut(w["L2_ffn_proj_w"]),
        "l3_qk": cut(w["L3_mix_w_qkv"][:, :2 * D]), "l3_v": cut(w["L3_mix_w_qkv"][:, 2 * D:]),
        "l3_proj": cut(w["L3_mix_w_proj"]), "l3_wq": cut(l3_w[:D].T), "l3_wk": cut(l3_w[D:2 * D].T),
        "l3_wv": cut(l3_w[2 * D:].T), "l3_wo": cut(w["L3_ffn_Wproj"].T)}
    panels = np.stack([p for name in PANELS for p in panel_groups[name]])
    assert len(panels) == N_PANELS

    def col(v):
        return np.ascontiguousarray(v.reshape(-1, P).T)

    twice = lambda v: np.concatenate([v, v]).reshape(P, 1)
    qkv_b, mix3_b, ffn3_b = w["L0_mix_qkv_b"], w["L3_mix_b_qkv"], w["L3_ffn_bqkv"]
    columns = {"b1": col(w["L0_gnn_b1"]), "b2": col(w["L0_gnn_b2"]), "bg": col(w["L0_gnn_bg"]),
               "bq": col(w["L0_gnn_bq"]), "l0_qb": col(qkv_b[:D]), "l0_fc1b": col(w["L0_mix_fc1_b"]),
               "ln1w": col(w["L0_mix_ln1_w"]), "ln1b": col(w["L0_mix_ln1_b"]), "ln2w": col(w["L0_mix_ln2_w"]),
               "ln2b": col(w["L0_mix_ln2_b"]), "l0_b1": col(w["L0_ffn_b1"]), "g1": col(w["L1_ffn_g1"]),
               "gb1": col(w["L1_ffn_b1"]), "g2": col(w["L1_ffn_g2"]), "gb2": col(w["L1_ffn_b2"]),
               "l1_bq": col(w["L1_ffn_bq"]), "l1_bk": col(w["L1_ffn_bk"]), "l1_bf1": col(w["L1_ffn_bf1"]),
               "gat_b1": col(w["L2_gnn_b1"]), "qnw": twice(w["L2_ffn_q_norm_w"]), "qnb": twice(w["L2_ffn_q_norm_b"]),
               "knw": twice(w["L2_ffn_k_norm_w"]), "knb": twice(w["L2_ffn_k_norm_b"]), "l3_qb": col(mix3_b[:D]),
               "l3_kb": col(mix3_b[D:2 * D]), "l3_bqk": col(ffn3_b[:2 * D])}
    cols = np.concatenate([columns[name] for name in COLUMNS], axis=1)
    l2b = w["L2_ffn_qkv_b"]
    row_of = {"l0_kb": qkv_b[D:2 * D], "l0_vb": qkv_b[2 * D:], "l0_projb": w["L0_mix_proj_b"],
              "l0_fc2b": w["L0_mix_fc2_b"], "gcn_b": w["L1_gnn_b"], "l1_projb": w["L1_mix_bproj"],
              "l1_bv": w["L1_ffn_bv"], "l1_bo": w["L1_ffn_bo"], "l1_bm": w["L1_ffn_bm"], "l1_bf2": w["L1_ffn_bf2"],
              "att_s1": w["L2_gnn_att_src1"], "att_d1": w["L2_gnn_att_dst1"], "att_s2": w["L2_gnn_att_src2"],
              "att_d2": w["L2_gnn_att_dst2"], "gat_b2": w["L2_gnn_b2"], "l2_projb": w["L2_mix_b_proj"],
              "l2_qb": l2b[:D], "l2_kb": l2b[D:2 * D], "l2_vb": l2b[2 * D:], "l2_bo": w["L2_ffn_proj_b"],
              "attn_l": w["L3_gnn_attn_l"].reshape(-1), "attn_r": w["L3_gnn_attn_r"].reshape(-1),
              "l3_vb": mix3_b[2 * D:], "l3_projb": w["L3_mix_b_proj"], "l3_bv": ffn3_b[2 * D:],
              "l3_bo": w["L3_ffn_bproj"]}
    rows = np.stack([row_of[name] for name in ROWS])
    narrow = np.concatenate([w["L0_ffn_gate_w"], w["L1_ffn_Wr"].reshape(D, 1), w["L2_ffn_wg_w"], w["L2_ffn_wg0_w"],
                             w["L2_ffn_wg1_w"], w["L3_ffn_Wg"].T], axis=1)
    narrow = np.ascontiguousarray(narrow.reshape(KC, P, N_NARROW).transpose(1, 0, 2))
    shorts = np.concatenate([w["L3_ffn_ba"].reshape(-1), w["L3_ffn_bg"], w["L1_ffn_br"].reshape(-1)]).reshape(1, -1)
    query_t = np.ascontiguousarray(w["L0_gnn_query_embs"].reshape(B * L, KC, P).transpose(2, 1, 0))
    rand = np.ascontiguousarray(w["L1_mix_rand_matrix"].reshape(KC, P, P).transpose(1, 0, 2)).reshape(P, D)
    head_mats = np.zeros((P, 2 * P), np.float32)
    for i, m in enumerate((w["L3_gnn_W_fc"], w["L3_gnn_W_res"])):
        for b in range(2):
            head_mats[b * DH:(b + 1) * DH, i * P + b * DH:i * P + (b + 1) * DH] = m.T
    a_t = cut(w["L3_ffn_A"].reshape(P, D).T, KC, P)[0]
    bm = np.ascontiguousarray(w["L3_ffn_Bm"].transpose(0, 2, 1)).reshape(P, 3 * D)

    arrays = {"x": w["x"], "src": w["src"], "dst": w["dst"], "edge_type": w["edge_type_3"], "panels": panels,
              "cols": cols, "rows": rows, "narrow": narrow, "shorts": shorts, "query_t": query_t,
              "b2": w["L0_ffn_b2"].reshape(8, D), "rand": rand, "head_mats": head_mats, "a_t": a_t, "bm": bm,
              "bb": w["L3_ffn_bb"]}
    nc = bacc.Bacc("TRN2", target_bir_lowering=False, num_devices=1)
    arrays = {f"in_{name}": np.ascontiguousarray(a) for name, a in arrays.items()}
    args = [nc.dram_tensor(name, a.shape, mybir.dt.from_np(a.dtype), kind="ExternalInput").ap()
            for name, a in arrays.items()]
    out = nc.dram_tensor("out", (N, D), F32, kind="ExternalOutput").ap()
    build(nc, *args, out)
    return run_bass_kernel_spmd(nc, [arrays], core_ids=[0]).results[0]["out"]
```

```python
from contextlib import ExitStack

import numpy as np

import concourse.bass as bass
from concourse import mybir

ALU = mybir.AluOpType
ACT = mybir.ActivationFunctionType
AX = mybir.AxisListType
F32 = mybir.dt.float32
BF16 = mybir.dt.bfloat16
I32 = mybir.dt.int32
F32R = mybir.dt.float32r

P = 128
N = 256
NT = N // P
D = 768
KC = D // P
H = 12
DH = D // H
COLS = 384
E = 4096
EC = E // P
R = 3
B, L = 8, 64
NB = N // B
UNIT = NT * D

PANELS = {}


def _plan_panels():
    at = 0
    for name, n in (("qg_w", 2), ("rel1", 8), ("hg_w", 2), ("alpha_w", 4), ("rel2", 8),
                    ("l0_qkv", 6), ("l0_proj", 2), ("l0_fc1", 8), ("l0_fc2", 8), ("l0_w1", 8), ("l0_w2", 8),
                    ("l1_gcn", 2), ("l1_q", 2), ("l1_v", 2), ("l1_proj", 2), ("l1_wq", 2), ("l1_wk", 2),
                    ("l1_wv", 2), ("l1_wo", 2), ("l1_wm", 2), ("l1_f1", 1), ("l1_f2", 1),
                    ("l2_gat1", 2), ("l2_gat2", 2), ("l2_q", 2), ("l2_kv", 4), ("l2_proj", 2), ("l2_qkv", 6),
                    ("l2_wo", 2), ("l3_qk", 4), ("l3_v", 2), ("l3_proj", 2), ("l3_wq", 2), ("l3_wk", 2),
                    ("l3_wv", 2), ("l3_wo", 2)):
        PANELS[name] = at
        at += n
    return at


N_PANELS = _plan_panels()

COLUMNS = {}
_names = [("b1", 6), ("b2", 6), ("bq", 6), ("l0_qb", 6), ("l0_fc1b", 24), ("ln1w", 6), ("ln1b", 6),
          ("ln2w", 6), ("ln2b", 6), ("l0_b1", 24), ("g1", 6), ("gb1", 6), ("g2", 6), ("gb2", 6), ("l1_bq", 6),
          ("l1_bk", 6), ("l1_bf1", 3), ("gat_b1", 6), ("qnw", 1), ("qnb", 1), ("knw", 1), ("knb", 1),
          ("l3_qb", 6), ("l3_kb", 6), ("l3_bqk", 12)]
_at = 0
for _name, _n in _names:
    COLUMNS[_name] = (_at, _n)
    _at += _n
N_COLUMNS = _at

ROWS = {name: i for i, name in enumerate(
    ["l0_kb", "l0_vb", "l0_projb", "l0_fc2b", "gcn_b", "l1_projb", "l1_bv", "l1_bo", "l1_bm", "l1_bf2",
     "att_s1", "att_d1", "att_s2", "att_d2", "gat_b2", "l2_projb", "l2_qb", "l2_kb", "l2_vb", "l2_bo",
     "attn_l", "attn_r", "l3_vb", "l3_projb", "l3_bv", "l3_bo", "bg"])}
NARROW = {"gate": (0, 8), "wr": (8, 1), "gates": (9, 14), "l3_gate": (23, 8)}
N_NARROW = 31
SHORT = {"ba": (0, 128), "bg": (128, 8), "br": (136, 1)}
N_SHORT = 137


class Signal:

    def __init__(self, sem):
        self.sem, self.planned, self.raised = sem, 0, 0

    def mark(self):
        self.planned += 1
        return Mark(self, self.planned)


class Mark:

    def __init__(self, owner, count):
        self.owner, self.count = owner, count

    @property
    def at(self):
        return self.owner.sem, self.count

    @property
    def by(self):
        assert self.count == self.owner.raised + 1, (self.count, self.owner.raised)
        self.owner.raised += 1
        return self.owner.sem, 1


class Tile:

    def __init__(self, ps, before, filled, drained):
        self.ps, self.before, self.filled, self.drained = ps, before, filled, drained


class Load:

    def __init__(self, ap, src, sem, count, before):
        self.ap, self.src, self.sem, self.count, self.before, self.freed = ap, src, sem, count, before, None

    @property
    def at(self):
        return self.sem, 16 * self.count


class Slots:

    def __init__(self, aps, sems):
        self.aps, self.sems, self.last, self.counts = aps, sems, [None] * len(aps), [0] * len(aps)


class Lane:

    def __init__(self, sem, name, banks, users, panel_slots, panels, row_slots, rows):
        self.banks, self.users, self.nbank = banks, users, 0
        self.panel_slots, self.panels, self.npanel = panel_slots, panels, 0
        self.row_slots, self.rows, self.nrow = row_slots, rows, 0
        self.filled = Signal(sem(f"{name}_products_ready"))
        self.drained = {w: Signal(sem(f"{name}_{full}_drained")) for w, full in (("V", "vector"), ("A", "scalar"))}
        self.done = {w: Signal(sem(f"{name}_{full}_done")) for w, full in
                     (("V", "vector"), ("A", "scalar"), ("T", "tensor"), ("P", "pool"))}
        self.chain = {w: [sem(f"{name}_{full}_step"), 0] for w, full in
                      (("V", "vector"), ("A", "scalar"), ("P", "pool"))}
        self.stages = []
        self.pace = 1.0

    def tile(self, who=None):
        bank = self.banks[self.nbank % len(self.banks)]
        self.nbank += 1
        tile = Tile(bank[0], self.users[bank[1]], self.filled.mark(), None)
        self.users[bank[1]] = tile
        if who:
            self.drained_by(tile, who)
        return tile

    def drained_by(self, tile, who):
        tile.drained = self.drained[who].mark()

    def time(self):
        return sum(stage.time * stage.pace for stage in self.stages)

    def mark(self, who):
        return self.done[who].mark()

    def load(self, slots, which, src, shape=None):
        ap = slots.aps[which]
        if shape:
            ap = ap[0:shape[0], 0:shape[1]]
        slots.counts[which] += 1
        new = Load(ap, src, slots.sems[which], slots.counts[which], slots.last[which])
        slots.last[which] = new
        return new

    def panel(self, src, freed=None):
        which = self.panels[self.npanel % len(self.panels)]
        self.npanel += 1
        new = self.load(self.panel_slots, which, src)
        new.freed = freed
        return new

    def row(self, src, shape=None):
        which = self.rows[self.nrow % len(self.rows)]
        self.nrow += 1
        return self.load(self.row_slots, which, src, shape)

    def step(self, who, eng, ins):
        self.chain[who][1] += 1
        ins.then_inc(self.chain[who][0], 1)
        eng.wait_ge(self.chain[who][0], self.chain[who][1])


def fill(pe, tile):
    if tile.before is not None:
        pe.wait_ge(*tile.before.drained.at)


def wait_all(eng, marks):
    for m in marks:
        eng.wait_ge(*m.at)


class Stage:
    time = 5.0
    loads = ()

    def __init__(self, lane):
        self.lane, self.pace = lane, lane.pace
        lane.stages.append(self)

    def t(self, pe):
        yield self.time

    def v(self, dve):
        yield self.time

    def a(self, act):
        yield self.time

    def p(self, pool):
        yield self.time

    def s(self, sp):
        for load in self.loads:
            if load.before is not None:
                sp.wait_ge(*load.before.freed.at)
            sp.dma_start(load.ap, load.src).then_inc(load.sem, 16)
            yield self.time / len(self.loads) if load.ap.shape[1] > D else 0.0


def side_by_side(lanes, part, eng):
    work = []
    for lane in lanes:
        start, steps = 0.0, []
        for stage in lane:
            steps.append((start, program_of(stage, part)(eng), stage.pace))
            start += stage.time * stage.pace
        work.append([0.0, steps, 0])
    while any(w[2] < len(w[1]) for w in work):
        w = min((w for w in work if w[2] < len(w[1])), key=lambda w: w[0])
        try:
            w[0] += next(w[1][w[2]][1]) * w[1][w[2]][2]
        except StopIteration:
            w[2] += 1
            if w[2] < len(w[1]):
                w[0] = w[1][w[2]][0]


def program_of(stage, part):
    return {"t": stage.t, "v": stage.v, "a": stage.a, "p": stage.p, "s": stage.s}[part]


class SplitPanel:

    def __init__(self, lane, k, panel, buffers):
        self.load = lane.panel(k.panel[panel])
        self.high, self.low, self.before = buffers.take(self)
        self.high_ready, self.ready, self.used = lane.mark("A"), lane.mark("P"), None
        self.load.freed = self.ready

    def round(self, act):
        act.wait_ge(*self.load.at)
        if self.before is not None:
            act.wait_ge(*self.before.used.at)
        act.activation(self.high, self.load.ap, ACT.Copy).then_inc(*self.high_ready.by)

    def subtract(self, pool):
        pool.wait_ge(*self.high_ready.at)
        pool.tensor_tensor(self.low, self.load.ap, self.high, ALU.subtract).then_inc(*self.ready.by)


class SplitBuffers:

    def __init__(self, pairs):
        self.pairs, self.last, self.n = pairs, [None] * len(pairs), 0

    def take(self, user):
        i = self.n % len(self.pairs)
        self.n += 1
        before, self.last[i] = self.last[i], user
        return self.pairs[i][0], self.pairs[i][1], before


class SplitActivation(Stage):
    time = 3.0

    def __init__(self, lane, x, high, low, after=()):
        super().__init__(lane)
        self.x, self.high, self.low, self.after = x, high, low, after
        self.rounded = [lane.mark("A") for _ in range(2)]
        self.done = lane.mark("V")
        n = x.shape[1] // 2
        self.cuts = [(0, n), (n, 2 * n)]

    def a(self, act):
        wait_all(act, self.after)
        for (a, z), mark in zip(self.cuts, self.rounded):
            act.activation(self.high[:, a:z], self.x[:, a:z], ACT.Copy).then_inc(*mark.by)
        yield self.time

    def v(self, dve):
        wait_all(dve, self.after)
        for (a, z), mark in zip(self.cuts, self.rounded):
            dve.wait_ge(*mark.at)
            ins = dve.tensor_tensor(self.low[:, a:z], self.x[:, a:z], self.high[:, a:z], ALU.subtract)
        ins.then_inc(*self.done.by)
        yield self.time


def three_passes(pe, ps, still, moving, start, stop):
    pe.matmul(ps, still[0], moving[0], start=start, stop=False)
    pe.matmul(ps, still[0], moving[1], start=False, stop=False)
    return pe.matmul(ps, still[1], moving[0], start=False, stop=stop)


class PanelParts(Stage):
    time = 0.0

    def __init__(self, lane, k, panels, buffers, after=()):
        super().__init__(lane)
        self.after = after
        self.parts = [SplitPanel(lane, k, panel, buffers) for panel in panels]
        self.loads = [part.load for part in self.parts]

    def a(self, act):
        wait_all(act, self.after)
        for part in self.parts:
            part.round(act)
        yield 0.0

    def p(self, pool):
        wait_all(pool, self.after)
        for part in self.parts:
            part.subtract(pool)
        yield 0.0


def weights(pe, panel):
    if isinstance(panel, SplitPanel):
        pe.wait_ge(*panel.ready.at)
        return [ap.rearrange("p (k n) -> p k n", k=KC) for ap in (panel.high, panel.low)]
    pe.wait_ge(*panel.at)
    return panel.ap.rearrange("p (k n) -> p k n", k=KC)


class LinearFeatures(Stage):

    def __init__(self, lane, k, inputs, chunks, drain, who, after=(), drain_after=(), cols=N, tail=None,
                 tail_after=(), rows=(), together=False, parts=None):
        super().__init__(lane)
        self.parts = parts
        self.together = together
        self.inputs, self.drain, self.who, self.cols, self.tail = inputs, drain, who, cols, tail
        self.after, self.drain_after, self.tail_after = after, drain_after, tail_after
        self.groups, self.loads = [], list(rows)
        for g in range(chunks // 3):
            through = [lane.mark("T") for _ in inputs[:-1]]
            tiles = [lane.tile(who) for _ in range(3)]
            if parts:
                panels = [parts[g]]
                parts[g].used = tiles[-1].filled
            else:
                panels = [lane.panel(k.panel[i[0] + g]) for i in inputs]
                for p_, m in zip(panels, through + [tiles[-1].filled]):
                    p_.freed = m
                self.loads += panels
            self.groups.append((tiles, panels, through))
        self.done = self.groups[-1][0][-1].drained
        self.time = 4 * 6 * self.cols / 2400 * len(inputs) * chunks + 0.5

    def t(self, pe):
        wait_all(pe, self.after)
        last = len(self.inputs) - 1
        for g, (tiles, panels, through) in enumerate(self.groups):
            for i, (_, x) in enumerate(self.inputs):
                w = weights(pe, panels[i])
                for o, tile in enumerate(tiles):
                    if i == 0:
                        fill(pe, tile)
                    for c in range(KC):
                        ps, start = tile.ps[:, 0:self.cols], i == 0 and c == 0
                        stop = i == last and c == KC - 1 and self.tail is None
                        if self.parts:
                            mm = three_passes(pe, ps, [part[:, c, o * P:(o + 1) * P] for part in w],
                                              [part[:, c, :] for part in x], start, stop)
                        else:
                            mm = pe.matmul(ps, w[:, c, o * P:(o + 1) * P], x[:, c, :], start=start, stop=stop)
                    if i == last:
                        if self.tail is not None:
                            if g == 0 and o == 0:
                                wait_all(pe, self.tail_after)
                            mm = self.tail(pe, 3 * g + o, tile.ps[:, 0:self.cols])
                        mm.then_inc(*tile.filled.by)
                    yield 4 * 6 * self.cols / 2400
                if i < last:
                    mm.then_inc(*through[i].by)

    def drains(self, eng):
        wait_all(eng, self.drain_after)
        for g, (tiles, _, _) in enumerate(self.groups):
            yield (len(self.inputs) - 1) * 3 * 4 * 6 * self.cols / 2400
            if self.together:
                yield 3 * 4 * 6 * self.cols / 2400
            for o, tile in enumerate(tiles):
                if not self.together:
                    yield 4 * 6 * self.cols / 2400
                eng.wait_ge(*tile.filled.at)
                self.drain(eng, 3 * g + o, tile.ps[:, 0:self.cols]).then_inc(*tile.drained.by)

    def v(self, dve):
        return self.drains(dve) if self.who == "V" else iter(())

    def a(self, act):
        return self.drains(act) if self.who == "A" else iter(())


class LinearTokens(Stage):

    def __init__(self, lane, k, inputs, panels, drain, who="V", after=(), drain_after=(), rows=(), tail=None,
                 tail_after=(), tokens=N, parts=None):
        super().__init__(lane)
        self.parts = parts
        self.inputs, self.drain, self.who, self.tail = inputs, drain, who, tail
        self.after, self.drain_after, self.tail_after = after, drain_after, tail_after
        self.nt = tokens // P
        self.groups, self.loads = [], list(rows)
        for g in range(panels):
            through = [lane.mark("T") for _ in inputs[:-1]]
            tiles = [lane.tile(who) for _ in range(self.nt)]
            if parts:
                loads = [parts[g]]
                parts[g].used = tiles[-1].filled
            else:
                loads = [lane.panel(k.panel[i[0] + g]) for i in inputs]
                for p_, m in zip(loads, through + [tiles[-1].filled]):
                    p_.freed = m
                self.loads += loads
            self.groups.append((tiles, loads, through))
        self.done = self.groups[-1][0][-1].drained
        self.time = 4 * 6 * COLS / 2400 * len(inputs) * panels * self.nt + 0.5

    def t(self, pe):
        wait_all(pe, self.after)
        last = len(self.inputs) - 1
        for g, (tiles, panels, through) in enumerate(self.groups):
            for i, (_, x) in enumerate(self.inputs):
                w = weights(pe, panels[i])
                for t, tile in enumerate(tiles):
                    if i == 0:
                        fill(pe, tile)
                    for c in range(KC):
                        ps, start = tile.ps[:, 0:COLS], i == 0 and c == 0
                        stop = i == last and c == KC - 1 and self.tail is None
                        if self.parts:
                            mm = three_passes(pe, ps, [part[:, c, t * P:(t + 1) * P] for part in x],
                                              [part[:, c, :] for part in w], start, stop)
                        else:
                            mm = pe.matmul(ps, x[:, c, t * P:(t + 1) * P], w[:, c, :], start=start, stop=stop)
                    if i == last:
                        if self.tail is not None:
                            if g == 0 and t == 0:
                                wait_all(pe, self.tail_after)
                            mm = self.tail(pe, t, g, tile.ps[:, 0:COLS])
                        mm.then_inc(*tile.filled.by)
                    yield 4 * 6 * COLS / 2400
                if i < last:
                    mm.then_inc(*through[i].by)

    def drains(self, eng):
        wait_all(eng, self.drain_after)
        for g, (tiles, _, _) in enumerate(self.groups):
            yield (len(self.inputs) - 1) * self.nt * 4 * 6 * COLS / 2400
            for t, tile in enumerate(tiles):
                yield 4 * 6 * COLS / 2400
                eng.wait_ge(*tile.filled.at)
                self.drain(eng, t, g, tile.ps[:, 0:COLS]).then_inc(*tile.drained.by)

    def v(self, dve):
        return self.drains(dve) if self.who == "V" else iter(())

    def a(self, act):
        return self.drains(act) if self.who == "A" else iter(())


class ToFeatures(Stage):
    time = 4.0

    def __init__(self, lane, k, x, drain, who="V", after=(), drain_after=()):
        super().__init__(lane)
        self.k, self.x, self.drain, self.who, self.after, self.drain_after = k, x, drain, who, after, drain_after
        self.tiles = [lane.tile(who) for _ in range(KC)]
        self.done = self.tiles[-1].drained

    def t(self, pe):
        wait_all(pe, self.after)
        for c, tile in enumerate(self.tiles):
            fill(pe, tile)
            for t in range(NT):
                mm = pe.transpose(tile.ps[:, t * P:(t + 1) * P], self.x[:, t, c * P:(c + 1) * P], self.k.ident)
            mm.then_inc(*tile.filled.by)
            yield self.time / KC

    def drains(self, eng):
        wait_all(eng, self.drain_after)
        for c, tile in enumerate(self.tiles):
            yield self.time / KC
            eng.wait_ge(*tile.filled.at)
            self.drain(eng, c, tile.ps[:, 0:N]).then_inc(*tile.drained.by)

    def v(self, dve):
        return self.drains(dve) if self.who == "V" else iter(())

    def a(self, act):
        return self.drains(act) if self.who == "A" else iter(())


class ToTokens(Stage):
    time = 4.0

    def __init__(self, lane, k, xT, drain, who="V", after=(), drain_after=()):
        super().__init__(lane)
        self.k, self.xT, self.drain, self.who, self.after, self.drain_after = k, xT, drain, who, after, drain_after
        self.tiles = [lane.tile(who) for _ in range(2 * NT)]
        self.done = self.tiles[-1].drained

    def t(self, pe):
        wait_all(pe, self.after)
        for i, tile in enumerate(self.tiles):
            t, half = divmod(i, 2)
            fill(pe, tile)
            for c in range(3):
                mm = pe.transpose(tile.ps[:, c * P:(c + 1) * P], self.xT[:, 3 * half + c, t * P:(t + 1) * P],
                                  self.k.ident)
            mm.then_inc(*tile.filled.by)
            yield self.time / 4

    def drains(self, eng):
        wait_all(eng, self.drain_after)
        for i, tile in enumerate(self.tiles):
            t, half = divmod(i, 2)
            yield self.time / 4
            eng.wait_ge(*tile.filled.at)
            self.drain(eng, t, half, tile.ps[:, 0:COLS]).then_inc(*tile.drained.by)

    def v(self, dve):
        return self.drains(dve) if self.who == "V" else iter(())

    def a(self, act):
        return self.drains(act) if self.who == "A" else iter(())


def half(x, t, g):
    return x[:, t, g * COLS:(g + 1) * COLS]


class Power:

    def __init__(self, lane, k, x, exponent):
        self.x, self.exponent = x, k.exponents[:, exponent:exponent + 1]
        self.ready, self.done = lane.mark("V"), lane.mark("P")

    def p(self, pool):
        e = self.exponent
        for n in self.x.shape[2:]:
            e = e.unsqueeze(2)
        pool.wait_ge(*self.ready.at)
        pool.tensor_tensor(self.x, self.x, e.to_broadcast(list(self.x.shape)), ALU.pow).then_inc(*self.done.by)


INVERSE_ROOT, ROOT = 0, 1


class Setup(Stage):
    time = 3.0

    def __init__(self, lane, k):
        super().__init__(lane)
        self.k = k
        self.done = lane.mark("P")

    def p(self, pool):
        k = self.k
        pool.memset(k.exponents[:, 0:1], -0.5)
        pool.memset(k.exponents[:, 1:2], 0.5)
        pool.iota(k.iota_int, [[1, N]], base=0, channel_multiplier=0)
        pool.iota(k.rowid_int, [[P, NT]], base=0, channel_multiplier=1)
        self.lane.step("P", pool, pool.memset(k.ident, 0.0))
        self.lane.step("P", pool, pool.affine_select(out=k.ident, in_=k.ident, compare_op=ALU.not_equal, fill=1.0,
                                                     base=0, pattern=[[-1, P]], channel_multiplier=1))
        pool.memset(k.blocks, 0.0)
        pool.memset(k.ones, 1.0).then_inc(*self.done.by)
        pool.wait_ge(*self.done.at)
        yield self.time


class LayerNorm(Stage):
    time = 8.0

    def __init__(self, lane, k, x, out, eps, small, after=()):
        super().__init__(lane)
        self.x, self.out, self.eps, self.small, self.after = x, out, eps, small, after
        self.power = Power(lane, k, small[:, 24:28].rearrange("p (t n) -> p t n", t=NT)[:, :, 1], INVERSE_ROOT)
        self.done = lane.mark("V")

    def p(self, pool):
        self.power.p(pool)
        yield self.time

    def v(self, dve):
        wait_all(dve, self.after)
        step = lambda ins: self.lane.step("V", dve, ins)
        stats = self.small[:, 0:24].rearrange("p (t s n) -> p t s n", t=NT, s=2)
        mv = self.small[:, 24:28].rearrange("p (t n) -> p t n", t=NT)
        for t in range(NT):
            for s in range(2):
                ins = dve.bn_stats(stats[:, t, s, :], half(self.x, t, s))
        step(ins)
        for t in range(NT):
            ins = dve.bn_aggr(mv[:, t, :], stats[:, t, :, :].rearrange("p s n -> p (s n)"))
        step(ins)
        dve.tensor_scalar(mv[:, :, 1], mv[:, :, 1], self.eps, None, ALU.add).then_inc(*self.power.ready.by)
        yield 5.0
        dve.wait_ge(*self.power.done.at)
        for t in range(NT):
            ins = dve.tensor_scalar(self.out[:, t, :], self.x[:, t, :], mv[:, t, 0:1], mv[:, t, 1:2],
                                    ALU.subtract, ALU.mult)
        ins.then_inc(*self.done.by)
        dve.wait_ge(*self.done.at)
        yield self.time - 5.0


class Graph(Stage):
    time = 65.0

    def __init__(self, lane, k, hot, counts, constants):
        super().__init__(lane)
        self.k, self.counts = k, counts
        self.hot = [h.bitcast(BF16)[:, 0:4 * 1024].rearrange("p (c n) -> p c n", c=4) for h in hot]
        self.constants = constants
        self.tiles = [lane.tile("V") for _ in range(4)]
        self.hot_ready = [lane.mark("V") for _ in range(EC // 4)]
        self.hot_used = [lane.mark("T") for _ in range(EC // 4 - 1)]
        self.sums = [lane.tile("V") for _ in range(2)]
        self.adj_ready = lane.mark("V")
        self.averaged = lane.mark("V")
        self.col_power = Power(lane, k, k.dis_col, INVERSE_ROOT)
        self.turned = lane.tile("V")
        self.diagonal = lane.mark("V")
        self.spread = lane.tile("V")
        self.done = lane.mark("V")

    def p(self, pool):
        yield 56.0
        self.col_power.p(pool)
        yield self.time

    def v(self, dve):
        k, lane = self.k, self.lane
        step = lambda ins: lane.step("V", dve, ins)
        edges = k.edges
        dve.wait_ge(*self.constants.at)
        dve.wait_ge(*k.edges_at)
        dve.tensor_copy(k.iota_bf, k.iota_int)
        dve.tensor_copy(k.iota, k.iota_int)
        dve.tensor_copy(k.rowid, k.rowid_int)
        step(dve.tensor_copy(edges, k.edges_int))
        for r in range(R):
            ins = dve.tensor_scalar(k.dst_of[:, r, :], edges[:, 2, :], float(r), None, ALU.is_equal)
        step(ins)
        step(dve.tensor_scalar(edges[:, 1, :], edges[:, 1, :], 1.0, None, ALU.add))
        for r in range(R):
            ins = dve.tensor_tensor(k.dst_of[:, r, :], k.dst_of[:, r, :], edges[:, 1, :], ALU.mult)
        step(ins)
        step(dve.tensor_scalar(k.dst_of, k.dst_of, -1.0, None, ALU.add))
        for g in range(EC // 4):
            if g >= 2:
                dve.wait_ge(*self.hot_used[g - 2].at)
            for j in range(4):
                c = 4 * g + j
                dve.tensor_scalar(self.hot[g % 2][:, j, 0:N], k.iota_bf, edges[:, 0, c:c + 1], None, ALU.is_equal)
                for r in range(R):
                    ins = dve.tensor_scalar(self.hot[g % 2][:, j, (r + 1) * N:(r + 2) * N], k.iota_bf,
                                            k.dst_of[:, r, c:c + 1], None, ALU.is_equal)
            ins.then_inc(*self.hot_ready[g].by)
            yield 5.5
        counts = self.counts
        for i, tile in enumerate(self.tiles):
            t, b = divmod(i, 2)
            a, z = (0, 512) if b == 0 else (512, 768)
            dve.wait_ge(*tile.filled.at)
            dve.tensor_copy(counts[:, t, a:z], tile.ps[:, 0:z - a]).then_inc(*tile.drained.by)
        yield 3.0
        inv = k.inv
        dve.wait_ge(*self.tiles[-1].drained.at)
        for i, tile in enumerate(self.sums):
            a, z = (0, 512) if i == 0 else (512, 768)
            dve.wait_ge(*tile.filled.at)
            dve.tensor_copy(inv[:, a:z], tile.ps[:, 0:z - a]).then_inc(*tile.drained.by)
        dve.wait_ge(*self.sums[-1].drained.at)
        step(dve.tensor_scalar(inv, inv, 1.0, None, ALU.max))
        step(dve.reciprocal(inv, inv))
        cin = counts.rearrange("p t (r n) -> p t r n", r=R)
        step(dve.tensor_tensor(k.adjT, cin[:, :, 0, :], cin[:, :, 1, :], ALU.add))
        step(dve.tensor_tensor(k.adjT, k.adjT, cin[:, :, 2, :], ALU.add))
        for t in range(NT):
            blk = k.adjT[:, t, t * P:(t + 1) * P]
            ins = dve.tensor_tensor(blk, blk, k.ident, ALU.add)
        ins.then_inc(*self.adj_ready.by)
        dve.wait_ge(*self.adj_ready.at)
        for t in range(NT):
            ins = dve.tensor_tensor(counts[:, t, :], counts[:, t, :], inv, ALU.mult)
        ins.then_inc(*self.averaged.by)
        yield 9.0
        dve.wait_ge(*self.turned.filled.at)
        dve.tensor_copy(k.adj, self.turned.ps.rearrange("p (t n) -> p t n", t=NT)).then_inc(*self.turned.drained.by)
        dve.wait_ge(*self.turned.drained.at)
        dve.tensor_reduce(k.dis_col, k.adj, AX.X, ALU.add).then_inc(*self.col_power.ready.by)
        yield 3.0
        dve.wait_ge(*self.col_power.done.at)
        for t in range(NT):
            ins = dve.tensor_scalar(k.dis_diag[:, t * P:(t + 1) * P], k.ident, k.dis_col[:, t:t + 1], None, ALU.mult)
        ins.then_inc(*self.diagonal.by)
        yield 2.0
        dve.wait_ge(*self.spread.filled.at)
        for t in range(NT):
            ins = dve.scalar_tensor_tensor(out=k.gcn[:, t, :], in0=k.adjT[:, t, :], scalar=k.dis_col[:, t:t + 1],
                                           in1=self.spread.ps[:, 0:N], op0=ALU.mult, op1=ALU.mult)
        ins.then_inc(*self.spread.drained.by)
        for b in range(2):
            ins = dve.memset(k.blocks[b * DH:(b + 1) * DH, b * DH:(b + 1) * DH], 1.0)
        ins.then_inc(*self.done.by)
        dve.wait_ge(*self.done.at)
        yield 4.0

    def t(self, pe):
        k = self.k
        for tile in self.tiles:
            fill(pe, tile)
        for g in range(EC // 4):
            yield 5.5
            pe.wait_ge(*self.hot_ready[g].at)
            for j in range(4):
                first, last = g + j == 0, (g == EC // 4 - 1 and j == 3)
                hot = self.hot[g % 2][:, j, :]
                for i, tile in enumerate(self.tiles):
                    t, b = divmod(i, 2)
                    a, z = (256, 768) if b == 0 else (768, 1024)
                    mm = pe.matmul(tile.ps[:, 0:z - a], hot[:, t * P:(t + 1) * P], hot[:, a:z],
                                   start=first, stop=last)
                    if last:
                        if i < 3:
                            mm.then_inc(*tile.filled.by)
            if g < EC // 4 - 1:
                mm.then_inc(*self.hot_used[g].by)
        mm.then_inc(*self.tiles[3].filled.by)
        yield 3.0
        pe.wait_ge(*self.constants.at)
        pe.wait_ge(*self.tiles[-1].drained.at)
        for i, tile in enumerate(self.sums):
            a, z = (0, 512) if i == 0 else (512, 768)
            fill(pe, tile)
            for t in range(NT):
                mm = pe.matmul(tile.ps[:, 0:z - a], k.ones, self.counts[:, t, a:z], start=(t == 0), stop=(t == 1))
            mm.then_inc(*tile.filled.by)
        yield 9.0
        pe.wait_ge(*self.adj_ready.at)
        fill(pe, self.turned)
        for dt_ in range(NT):
            for st in range(NT):
                mm = pe.transpose(self.turned.ps[:, dt_ * N + st * P:dt_ * N + (st + 1) * P],
                                  k.adjT[:, st, dt_ * P:(dt_ + 1) * P], k.ident)
        mm.then_inc(*self.turned.filled.by)
        yield 4.0
        pe.wait_ge(*self.diagonal.at)
        fill(pe, self.spread)
        pe.matmul(self.spread.ps[:, 0:N], k.ones, k.dis_diag, start=True, stop=True).then_inc(*self.spread.filled.by)
        yield 2.0


class Aggregate(Stage):

    def __init__(self, lane, k, h, m, width, out, after=(), drain_after=()):
        super().__init__(lane)
        self.h, self.m, self.out, self.after, self.drain_after = h, m, out, after, drain_after
        self.cuts = [(0, 512), (512, 768)] if width == 768 else [(0, width)]
        self.tiles = [[lane.tile("V") for _ in self.cuts] for _ in range(KC)]
        self.done = self.tiles[-1][-1].drained
        self.time = KC * 2 * width * 4 / 2400

    def t(self, pe):
        wait_all(pe, self.after)
        for c, tiles in enumerate(self.tiles):
            for (a, z), tile in zip(self.cuts, tiles):
                fill(pe, tile)
                for t in range(NT):
                    mm = pe.matmul(tile.ps[:, 0:z - a], self.h[:, t, c * P:(c + 1) * P], self.m[:, t, a:z],
                                   start=(t == 0), stop=(t == NT - 1))
                mm.then_inc(*tile.filled.by)
            yield self.time / KC

    def v(self, dve):
        wait_all(dve, self.drain_after)
        for c, tiles in enumerate(self.tiles):
            yield self.time / KC
            for (a, z), tile in zip(self.cuts, tiles):
                dve.wait_ge(*tile.filled.at)
                dve.tensor_copy(self.out[:, c, a:z], tile.ps[:, 0:z - a]).then_inc(*tile.drained.by)


class PairCode(Stage):
    time = 5.0

    def __init__(self, lane, k, pairs, after=()):
        super().__init__(lane)
        self.k, self.pairs, self.after = k, pairs, after
        self.done = lane.mark("A")

    def a(self, act):
        wait_all(act, self.after)
        view = self.pairs.rearrange("p (n l) -> p n l", n=NB)
        act.activation(view[0:L], self.k.ident[0:L, 0:L].unsqueeze(1).to_broadcast([L, NB, L]), ACT.Copy)
        act.activation(view[L:L + NB], self.k.ident[L:L + NB, L:L + NB].unsqueeze(2).to_broadcast([NB, NB, L]),
                       ACT.Copy).then_inc(*self.done.by)
        yield self.time


class GateSum(Stage):
    UNITS = [(b, c) for b in range(B) for c in range(KC)]
    ROWS = L + NB
    START = 7.0

    def __init__(self, lane, hg, qg, q, out, z, pairs, rows, high, low, arrived, unit_time, pool_nodes,
                 after=()):
        super().__init__(lane)
        self.hg, self.qg, self.q, self.out, self.after = hg, qg, q, out, after
        self.z = [zz[:, 0:NB * L] for zz in z]
        self.pairs, self.rows, self.high, self.low = pairs, rows, high, low
        self.arrived, self.unit_time, self.pool_nodes = arrived, unit_time, pool_nodes
        self.tiles = [[lane.tile("A") for _ in range(4)] for _ in self.UNITS]
        self.high_ready = [lane.mark("A") for _ in range(B)]
        self.multiplied = [lane.mark("P") for _ in self.UNITS]
        self.low_ready, self.summed = [lane.mark("V")], []
        for i, (b, c) in enumerate(self.UNITS):
            if c == 3 and b + 1 < B:
                self.low_ready.append(lane.mark("V"))
            if i >= 1:
                self.summed.append(lane.mark("V"))
        self.summed.append(lane.mark("V"))
        self.used = [self.tiles[b * KC + KC - 1][3].filled for b in range(B)]
        self.done = self.summed[-1]
        self.time = self.START + len(self.UNITS) * unit_time + 6.5

    def arrival(self, b):
        sem, before = self.arrived[b % 2]
        return sem, before + 32 * (b // 2 + 1)

    def s(self, sp):
        wait_all(sp, self.after)
        for b in range(B):
            if b >= 2:
                yield self.START + KC * self.unit_time if b == 2 else KC * self.unit_time
                sp.wait_ge(*self.used[b - 2].at)
            sem = self.arrived[b % 2][0]
            sp.dma_start(self.rows[b % 2][0:L, :], self.qg[(b % 2) * L:(b % 2 + 1) * L, b // 2, :]).then_inc(sem, 16)
            sp.dma_start(self.rows[b % 2][L:self.ROWS, :],
                         self.hg[(b % 4) * NB:(b % 4 + 1) * NB, b // 4, :]).then_inc(sem, 16)

    def t(self, pe):
        yield self.START
        wait_all(pe, self.after)
        for i, (b, c) in enumerate(self.UNITS):
            if c == 0:
                pe.wait_ge(*self.low_ready[b].at)
            for q, tile in enumerate(self.tiles[i]):
                fill(pe, tile)
                code = self.pairs[0:self.ROWS, q * 512:(q + 1) * 512]
                pe.matmul(tile.ps, self.high[b % 2][0:self.ROWS, c * P:(c + 1) * P], code,
                          start=True, stop=False)
                pe.matmul(tile.ps, self.low[b % 2][0:self.ROWS, c * P:(c + 1) * P], code,
                          start=False, stop=True).then_inc(*tile.filled.by)
            yield self.unit_time

    def split_high(self, act, b):
        act.wait_ge(*self.arrival(b))
        if b >= 2:
            act.wait_ge(*self.used[b - 2].at)
        act.activation(self.high[b % 2][0:self.ROWS, :], self.rows[b % 2][0:self.ROWS, :], ACT.Copy).then_inc(*self.high_ready[b].by)

    def a(self, act):
        yield 3.0
        wait_all(act, self.after)
        self.split_high(act, 0)
        yield self.START - 2.0
        for i, (b, c) in enumerate(self.UNITS):
            if c == 2 and b + 1 < B:
                self.split_high(act, b + 1)
            z = self.z[i % len(self.z)]
            if i >= len(self.z):
                act.wait_ge(*self.summed[i - len(self.z)].at)
            for q, tile in enumerate(self.tiles[i]):
                act.wait_ge(*tile.filled.at)
                act.activation(z[:, q * 512:(q + 1) * 512], tile.ps, ACT.Sigmoid).then_inc(*tile.drained.by)
            yield self.unit_time

    def nodes(self, i, a, e):
        b, c = self.UNITS[i]
        z = self.z[i % len(self.z)].rearrange("p (n l) -> p n l", n=NB)[:, a:e, :]
        return z, self.q[:, c, b * L:(b + 1) * L].unsqueeze(1).to_broadcast([P, e - a, L])

    def p(self, pool):
        yield self.START + 3.0
        for i in range(len(self.UNITS)):
            z, q = self.nodes(i, 0, self.pool_nodes)
            pool.wait_ge(*self.tiles[i][3].drained.at)
            pool.tensor_tensor(z, z, q, ALU.mult).then_inc(*self.multiplied[i].by)
            yield self.unit_time

    def split_low(self, dve, b):
        dve.wait_ge(*self.high_ready[b].at)
        dve.tensor_tensor(self.low[b % 2][0:self.ROWS, :], self.rows[b % 2][0:self.ROWS, :],
                          self.high[b % 2][0:self.ROWS, :], ALU.subtract).then_inc(
            *self.low_ready[b].by)

    def sum_up(self, dve, i):
        b, c = self.UNITS[i]
        dve.wait_ge(*self.multiplied[i].at)
        z, _ = self.nodes(i, 0, NB)
        dve.tensor_reduce(self.out[:, c, b * NB:(b + 1) * NB], z, AX.X, ALU.add).then_inc(*self.summed[i].by)

    def v(self, dve):
        yield 3.0
        self.split_low(dve, 0)
        yield self.START + 0.3
        for i, (b, c) in enumerate(self.UNITS):
            if c == 3 and b + 1 < B:
                self.split_low(dve, b + 1)
            z, q = self.nodes(i, self.pool_nodes, NB)
            dve.wait_ge(*self.tiles[i][3].drained.at)
            self.lane.step("V", dve, dve.tensor_tensor(z, z, q, ALU.mult))
            if i >= 1:
                self.sum_up(dve, i - 1)
            yield self.unit_time
        self.sum_up(dve, len(self.UNITS) - 1)


class GateMix(Stage):
    time = 6.0

    def __init__(self, lane, alpha, qi, h, out, after=()):
        super().__init__(lane)
        self.alpha, self.qi, self.h, self.out, self.after = alpha, qi, h, out, after
        self.tanh = lane.mark("A")
        self.done = lane.mark("V")

    def a(self, act):
        wait_all(act, self.after)
        act.activation(self.qi, self.qi, ACT.Tanh).then_inc(*self.tanh.by)
        yield self.time

    def v(self, dve):
        step = lambda ins: self.lane.step("V", dve, ins)
        dve.wait_ge(*self.tanh.at)
        wait_all(dve, self.after)
        step(dve.tensor_tensor(self.qi, self.qi, self.alpha, ALU.mult))
        step(dve.tensor_scalar(self.alpha, self.alpha, -1.0, 1.0, ALU.mult, ALU.add))
        step(dve.tensor_tensor(self.alpha, self.alpha, self.h, ALU.mult))
        dve.tensor_tensor(self.out, self.qi, self.alpha, ALU.add).then_inc(*self.done.by)
        dve.wait_ge(*self.done.at)
        yield self.time


class Vector(Stage):

    def __init__(self, lane, body, time=2.0, after=(), rows=()):
        super().__init__(lane)
        self.body, self.time, self.after, self.loads = body, time, after, list(rows)
        self.done = lane.mark("V")
        for row in rows:
            row.freed = self.done

    def v(self, dve):
        wait_all(dve, self.after)
        for load in self.loads:
            dve.wait_ge(*load.at)
        self.body(dve, lambda ins: self.lane.step("V", dve, ins)).then_inc(*self.done.by)
        dve.wait_ge(*self.done.at)
        yield self.time


class EluPlusOne(Stage):
    time = 5.0

    def __init__(self, lane, x, tmp, after=()):
        super().__init__(lane)
        self.x, self.tmp, self.after = x, tmp, after
        self.exp = lane.mark("A")
        self.done = lane.mark("V")

    def a(self, act):
        wait_all(act, self.after)
        act.activation(self.tmp, self.x, ACT.Exp).then_inc(*self.exp.by)
        yield self.time

    def v(self, dve):
        dve.wait_ge(*self.exp.at)
        wait_all(dve, self.after)
        self.lane.step("V", dve, dve.tensor_scalar(self.x, self.x, 0.0, None, ALU.max))
        dve.scalar_tensor_tensor(out=self.x, in0=self.tmp, scalar=1.0, in1=self.x, op0=ALU.min,
                                 op1=ALU.add).then_inc(*self.done.by)
        dve.wait_ge(*self.done.at)
        yield self.time


class KeyValues(Stage):
    time = 6.0

    def __init__(self, lane, k, key, value, sums, drain, after=()):
        super().__init__(lane)
        self.k, self.key, self.value, self.sums, self.drain, self.after = k, key, value, sums, drain, after
        self.tiles = [lane.tile("V") for _ in range(KC)]
        self.done = self.tiles[-1].drained

    def t(self, pe):
        wait_all(pe, self.after)
        for c, tile in enumerate(self.tiles):
            fill(pe, tile)
            for t in range(NT):
                key = self.key[:, t, c * P:(c + 1) * P]
                mm = pe.matmul(tile.ps[:, 0:P], key, self.value[:, t, c * P:(c + 1) * P],
                               start=(t == 0), stop=(t == NT - 1))
            if self.sums:
                for t in range(NT):
                    mm = pe.matmul(tile.ps[:, P:P + 2], self.key[:, t, c * P:(c + 1) * P], self.k.ones[:, 0:2],
                                   start=(t == 0), stop=(t == NT - 1))
            mm.then_inc(*tile.filled.by)
            yield self.time / KC

    def v(self, dve):
        for c, tile in enumerate(self.tiles):
            yield self.time / KC
            dve.wait_ge(*tile.filled.at)
            self.drain(dve, c, tile.ps, lambda ins: self.lane.step("V", dve, ins)).then_inc(*tile.drained.by)


class QueryStates(Stage):
    time = 8.0

    def __init__(self, lane, k, states, norms, qT, outT, scratch, after=()):
        super().__init__(lane)
        self.states, self.norms, self.qT, self.outT, self.scratch, self.after = states, norms, qT, outT, scratch, after
        self.tiles = [lane.tile("V") for _ in range(KC)]
        self.done = self.tiles[-1].drained

    def t(self, pe):
        wait_all(pe, self.after)
        for c, tile in enumerate(self.tiles):
            fill(pe, tile)
            mm = pe.matmul(tile.ps[:, 0:N], self.states[:, c, :], self.qT[:, c, :], start=True, stop=True)
            if self.norms is not None:
                mm = pe.matmul(tile.ps[:, N:2 * N], self.norms[:, c, :], self.qT[:, c, :], start=True, stop=True)
            mm.then_inc(*tile.filled.by)
            yield self.time / KC

    def v(self, dve):
        for c, tile in enumerate(self.tiles):
            yield self.time / KC
            dve.wait_ge(*tile.filled.at)
            if self.norms is not None:
                if c:
                    dve.wait_ge(*self.tiles[c - 1].drained.at)
                self.lane.step("V", dve, dve.reciprocal(self.scratch, tile.ps[:, N:2 * N]))
                ins = dve.tensor_tensor(self.outT[:, c, :], tile.ps[:, 0:N], self.scratch, ALU.mult)
            else:
                ins = dve.tensor_copy(self.outT[:, c, :], tile.ps[:, 0:N])
            ins.then_inc(*tile.drained.by)


def top_two(dve, step, s, mask, best, rank, left, e):
    wide = lambda ap: ap.unsqueeze(2).to_broadcast([P, NT, e])
    rank_b = rank.unsqueeze(1).to_broadcast([P, NT, e])
    src = s
    for i in range(2):
        step(dve.tensor_reduce(best, src, AX.X, ALU.max))
        hit = left[i]
        step(dve.tensor_tensor(hit, src, wide(best), ALU.is_equal))
        step(dve.tensor_tensor(hit, hit, rank_b, ALU.mult))
        step(dve.tensor_reduce(best, hit, AX.X, ALU.max))
        step(dve.tensor_tensor(hit, hit, wide(best), ALU.is_equal))
        if i == 0:
            step(dve.scalar_tensor_tensor(out=left[2], in0=hit, scalar=-4.0, in1=s, op0=ALU.mult, op1=ALU.add))
            src = left[2]
    return dve.tensor_tensor(mask, left[0], left[1], ALU.add)


class Logits(Stage):
    time = 8.0

    def __init__(self, lane, k, xT, narrow, e, groups, out, small, bias=None, after=()):
        super().__init__(lane)
        self.xT, self.narrow, self.e, self.groups, self.out, self.bias = xT, narrow, e, groups, out, bias
        self.small, self.after = small, after
        self.tile = lane.tile("V")
        self.ready = lane.mark("V")
        self.exped = lane.mark("A")
        self.done = lane.mark("V")

    def t(self, pe):
        wait_all(pe, self.after)
        fill(pe, self.tile)
        for t in range(NT):
            for c in range(KC):
                mm = pe.matmul(self.tile.ps[:, t * self.e:(t + 1) * self.e], self.xT[:, c, t * P:(t + 1) * P],
                               self.narrow[:, c, :], start=(c == 0), stop=(c == KC - 1))
        mm.then_inc(*self.tile.filled.by)
        yield self.time

    def v(self, dve):
        step = lambda ins: self.lane.step("V", dve, ins)
        e, out, best = self.e, self.out, self.small
        dve.wait_ge(*self.tile.filled.at)
        dve.tensor_copy(out, self.tile.ps[:, 0:NT * e].rearrange("p (t e) -> p t e", t=NT)).then_inc(
            *self.tile.drained.by)
        dve.wait_ge(*self.tile.drained.at)
        if self.bias is not None:
            step(dve.tensor_tensor(out, out, self.bias.unsqueeze(1).to_broadcast([P, NT, e]), ALU.add))
        for a, z in self.groups:
            step(dve.tensor_reduce(best, out[:, :, a:z], AX.X, ALU.max))
            ins = dve.tensor_tensor(out[:, :, a:z], out[:, :, a:z], best.unsqueeze(2).to_broadcast([P, NT, z - a]),
                                    ALU.subtract)
            if z < e:
                step(ins)
        ins.then_inc(*self.ready.by)
        dve.wait_ge(*self.exped.at)
        for a, z in self.groups:
            step(dve.tensor_reduce(best, out[:, :, a:z], AX.X, ALU.add))
            step(dve.reciprocal(best, best))
            ins = dve.tensor_tensor(out[:, :, a:z], out[:, :, a:z], best.unsqueeze(2).to_broadcast([P, NT, z - a]),
                                    ALU.mult)
            if z < e:
                step(ins)
        ins.then_inc(*self.done.by)
        dve.wait_ge(*self.done.at)
        yield self.time

    def a(self, act):
        act.wait_ge(*self.ready.at)
        act.activation(self.out, self.out, ACT.Exp).then_inc(*self.exped.by)
        yield self.time


class TurnNarrow(Stage):
    time = 2.0

    def __init__(self, lane, k, x, e, out, scale=1.0, after=()):
        super().__init__(lane)
        self.k, self.x, self.e, self.out, self.scale, self.after = k, x, e, out, scale, after
        self.tile = lane.tile("V")
        self.done = self.tile.drained

    def t(self, pe):
        wait_all(pe, self.after)
        fill(pe, self.tile)
        for t in range(NT):
            mm = pe.transpose(self.tile.ps[0:self.e, t * P:(t + 1) * P], self.x[:, t, :], self.k.ident)
        mm.then_inc(*self.tile.filled.by)
        yield self.time

    def v(self, dve):
        dve.wait_ge(*self.tile.filled.at)
        dve.tensor_scalar(self.out, self.tile.ps[0:self.e, 0:N], self.scale, None, ALU.mult).then_inc(
            *self.tile.drained.by)
        yield self.time


class Experts(Stage):

    def __init__(self, lane, k, xT, x, combine, combineT, b2, hidden, parts, first, buffers, combined, after=()):
        super().__init__(lane)
        self.k, self.xT, self.x, self.combine, self.combineT, self.b2 = k, xT, x, combine, combineT, b2
        self.hidden, self.parts, self.combined, self.after = hidden, parts, combined, after
        self.panels, self.up, self.down = list(first), {}, {}
        self.rounded, self.split = [], []
        order = list(self.order())
        for e in range(8):
            self.rounded.append(lane.mark("A"))
            for kind, e2 in order[2 * e + 3:2 * e + 5]:
                self.add_panel(buffers, kind, e2)
        self.loads = [b2] + [panel.load for panel in self.panels[3:]]
        for n, (kind, e) in enumerate(order):
            if kind == "down" and e == 0:
                self.turned = lane.tile("V")
                self.bias_tiles = [lane.tile("V") for _ in range(2 * NT)]
                b2.freed = self.bias_tiles[-1].filled
            tiles = [lane.tile("A" if kind == "up" else "V") for _ in range(3 if kind == "up" else 4)]
            self.panels[n].used = tiles[-1].filled
            (self.up if kind == "up" else self.down)[e] = (self.panels[n], tiles)
        self.split = [lane.mark("V") for _ in range(8)]
        self.done = self.down[7][1][-1].drained
        self.time = 16 * 5.8

    def order(self):
        yield "up", 0
        for e in range(8):
            if e < 7:
                yield "up", e + 1
            yield "down", e

    def add_panel(self, buffers, kind, e):
        at = PANELS["l0_w1" if kind == "up" else "l0_w2"] + e
        self.panels.append(SplitPanel(self.lane, self.k, at, buffers))

    def bias_t(self, pe):
        wait_all(pe, self.combined)
        fill(pe, self.turned)
        for t in range(NT):
            mm = pe.transpose(self.turned.ps[0:8, t * P:(t + 1) * P], self.combine[:, t, :], self.k.ident)
        mm.then_inc(*self.turned.filled.by)
        pe.wait_ge(*self.b2.at)
        pe.wait_ge(*self.turned.drained.at)
        for i, tile in enumerate(self.bias_tiles):
            t, g = divmod(i, 2)
            fill(pe, tile)
            pe.matmul(tile.ps[:, 0:COLS], self.combineT[:, t * P:(t + 1) * P], self.b2.ap[:, g * COLS:(g + 1) * COLS],
                      start=True, stop=True).then_inc(*tile.filled.by)

    def t(self, pe):
        wait_all(pe, self.after)
        for kind, e in self.order():
            if kind == "down" and e == 0:
                self.bias_t(pe)
            panel, tiles = (self.up if kind == "up" else self.down)[e]
            pe.wait_ge(*panel.ready.at)
            w = [ap.rearrange("p (k n) -> p k n", k=KC if kind == "up" else 3) for ap in (panel.high, panel.low)]
            if kind == "up":
                for o, tile in enumerate(tiles):
                    fill(pe, tile)
                    for c in range(KC):
                        mm = three_passes(pe, tile.ps[:, 0:N], [part[:, c, o * P:(o + 1) * P] for part in w],
                                          [part[:, c, :] for part in self.xT], c == 0, c == KC - 1)
                    mm.then_inc(*tile.filled.by)
            else:
                pe.wait_ge(*self.split[e].at)
                for i, tile in enumerate(tiles):
                    t, g = divmod(i, 2)
                    fill(pe, tile)
                    for c in range(3):
                        mm = three_passes(pe, tile.ps[:, 0:COLS],
                                          [part[:, c, t * P:(t + 1) * P] for part in self.parts[e % 2]],
                                          [part[:, c, g * COLS:(g + 1) * COLS] for part in w], c == 0, c == 2)
                    mm.then_inc(*tile.filled.by)
            yield 5.8

    def a(self, act):
        for e in range(8):
            if e >= 2:
                act.wait_ge(*self.split[e - 2].at)
            for o, tile in enumerate(self.up[e][1]):
                act.wait_ge(*tile.filled.at)
                act.activation(self.hidden[e % 2][:, o, :], tile.ps[:, 0:N], ACT.Gelu,
                               bias=self.k.col("l0_b1", 3 * e + o)).then_inc(*tile.drained.by)
            act.wait_ge(*self.up[e][1][-1].drained.at)
            if e >= 2:
                act.wait_ge(*self.panels_down_used(e - 2).at)
            act.activation(self.parts[e % 2][0], self.hidden[e % 2], ACT.Copy).then_inc(*self.rounded[e].by)
            for panel in self.panels[2 * e + 3:2 * e + 5]:
                panel.round(act)
            yield 11.6

    def panels_down_used(self, e):
        return self.down[e][0].used

    def p(self, pool):
        for panel in self.panels[3:]:
            panel.subtract(pool)
            yield 5.8

    def split_hidden(self, dve, e):
        dve.wait_ge(*self.rounded[e].at)
        high, low = self.parts[e % 2]
        dve.tensor_tensor(low, self.hidden[e % 2], high, ALU.subtract).then_inc(*self.split[e].by)

    def v(self, dve):
        self.split_hidden(dve, 0)
        dve.wait_ge(*self.turned.filled.at)
        dve.tensor_copy(self.combineT, self.turned.ps[0:8, 0:N]).then_inc(*self.turned.drained.by)
        for i, tile in enumerate(self.bias_tiles):
            x = half(self.x, *divmod(i, 2))
            dve.wait_ge(*tile.filled.at)
            dve.tensor_tensor(x, tile.ps[:, 0:COLS], x, ALU.add).then_inc(*tile.drained.by)
        before = self.bias_tiles
        for e in range(8):
            if e < 7:
                self.split_hidden(dve, e + 1)
            for i, tile in enumerate(self.down[e][1]):
                t, g = divmod(i, 2)
                x = half(self.x, t, g)
                dve.wait_ge(*before[i].drained.at)
                dve.wait_ge(*tile.filled.at)
                dve.scalar_tensor_tensor(out=x, in0=tile.ps[:, 0:COLS], scalar=self.combine[:, t, e:e + 1], in1=x,
                                         op0=ALU.mult, op1=ALU.add).then_inc(*tile.drained.by)
            yield 11.6
            before = self.down[e][1]


class SoftmaxAttention(Stage):

    def __init__(self, lane, k, qT, kT, v, outT, scale, probs, turned, small, gates=None, after=()):
        super().__init__(lane)
        self.k, self.qT, self.kT, self.value, self.outT, self.scale = k, qT, kT, v, outT, scale
        self.probs, self.turned, self.gates, self.after = probs, turned, gates, after
        self.nmax = small[:, 0:24].rearrange("p (h t) -> p h t", t=NT)
        self.rsum = small[:, 24:48].rearrange("p (h t) -> p h t", t=NT)
        self.maxed = {}
        self.exped, self.normed = {}, {}
        self.score, self.turn, self.out = {}, {}, {}
        for i in range(H + 3):
            if i < H:
                self.score[i] = lane.tile("A")
            if 0 <= i - 2 < H:
                self.turn[i - 2] = lane.tile("V")
            if 0 <= i - 3 < H:
                self.out[i - 3] = lane.tile("A")
            if i < H:
                self.maxed[i] = lane.mark("V")
            if 0 <= i - 1 < H:
                self.normed[i - 1] = lane.mark("V")
        self.done = self.out[H - 1].drained
        self.time = 4.0 * (H + 3)

    def t(self, pe):
        wait_all(pe, self.after)
        for i in range(H + 3):
            if i < H:
                c, r = i // 2, (i % 2) * DH
                tile = self.score[i]
                fill(pe, tile)
                for t in range(NT):
                    mm = pe.matmul(tile.ps[:, t * N:(t + 1) * N], self.qT[r:r + DH, c, t * P:(t + 1) * P],
                                   self.kT[r:r + DH, c, :], start=True, stop=True)
                mm.then_inc(*tile.filled.by)
            if 0 <= i - 2 < H:
                h = i - 2
                tile = self.turn[h]
                fill(pe, tile)
                pe.wait_ge(*self.normed[h].at)
                for m in range(NT):
                    for t in range(NT):
                        mm = pe.transpose(tile.ps[:, m * N + t * P:m * N + (t + 1) * P],
                                          self.probs[h % 3][:, t, m * P:(m + 1) * P], self.k.ident)
                mm.then_inc(*tile.filled.by)
            if 0 <= i - 3 < H:
                h = i - 3
                tile = self.out[h]
                fill(pe, tile)
                pe.wait_ge(*self.turn[h].drained.at)
                for m in range(NT):
                    mm = pe.matmul(tile.ps[:, 0:N], self.value[:, m, (h // 2) * P:(h // 2 + 1) * P],
                                   self.turned[h % 2][:, m, :], start=(m == 0), stop=(m == NT - 1))
                mm.then_inc(*tile.filled.by)
            yield 4.0

    def v(self, dve):
        step = lambda ins: self.lane.step("V", dve, ins)
        for i in range(H + 3):
            if i < H:
                dve.wait_ge(*self.score[i].filled.at)
                step(dve.tensor_reduce(self.nmax[:, i, :], self.score[i].ps.rearrange("p (t n) -> p t n", t=NT),
                                       AX.X, ALU.max))
                dve.tensor_scalar(self.nmax[:, i, :], self.nmax[:, i, :], -self.scale, None,
                                  ALU.mult).then_inc(*self.maxed[i].by)
            if 0 <= i - 1 < H:
                h = i - 1
                dve.wait_ge(*self.score[h].drained.at)
                step(dve.reciprocal(self.rsum[:, h, :], self.rsum[:, h, :]))
                if self.gates is not None:
                    step(dve.tensor_tensor(self.rsum[:, h, :], self.rsum[:, h, :], self.gates[:, :, h], ALU.mult))
                for t in range(NT):
                    p = self.probs[h % 3][:, t, :]
                    ins = dve.tensor_scalar(p, p, self.rsum[:, h, t:t + 1], None, ALU.mult)
                ins.then_inc(*self.normed[h].by)
            if 0 <= i - 2 < H:
                h = i - 2
                if h >= 2:
                    dve.wait_ge(*self.out[h - 2].filled.at)
                dve.wait_ge(*self.turn[h].filled.at)
                dve.tensor_copy(self.turned[h % 2], self.turn[h].ps.rearrange("p (m n) -> p m n", m=NT)).then_inc(
                    *self.turn[h].drained.by)
            yield 4.0

    def a(self, act):
        for i in range(H + 3):
            if i < H:
                if i >= 3:
                    act.wait_ge(*self.turn[i - 3].filled.at)
                act.wait_ge(*self.maxed[i].at)
                for t in range(NT):
                    ins = act.activation(self.probs[i % 3][:, t, :], self.score[i].ps[:, t * N:(t + 1) * N], ACT.Exp,
                                         bias=self.nmax[:, i, t:t + 1], scale=self.scale,
                                         accum_out=self.rsum[:, i, t:t + 1])
                ins.then_inc(*self.score[i].drained.by)
            if 0 <= i - 3 < H:
                h = i - 3
                r = (h % 2) * DH
                act.wait_ge(*self.out[h].filled.at)
                act.activation(self.outT[r:r + DH, h // 2, :], self.out[h].ps[r:r + DH, 0:N],
                               ACT.Copy).then_inc(*self.out[h].drained.by)
            yield 4.0


class RandomFeatures(Stage):
    time = 30.0

    def __init__(self, lane, k, qsT, sqT, rand, rf, tmp, small, after=()):
        super().__init__(lane)
        self.k, self.qsT, self.sqT, self.rand, self.rf, self.tmp = k, qsT, sqT, rand, rf, tmp
        self.ss, self.after = small[:, 0:H], after
        self.loads = [rand]
        self.squared = lane.mark("V")
        self.tiles = [lane.tile("A") for _ in range(H)]
        rand.freed = self.tiles[-1].filled
        self.power = Power(lane, k, self.ss, ROOT)
        self.done = lane.mark("V")

    def p(self, pool):
        self.power.p(pool)
        yield self.time

    def t(self, pe):
        pe.wait_ge(*self.squared.at)
        pe.wait_ge(*self.rand.at)
        rand = self.rand.ap.rearrange("p (c m) -> p c m", c=KC)
        for h, tile in enumerate(self.tiles):
            c, r = h // 2, (h % 2) * DH
            fill(pe, tile)
            pe.matmul(tile.ps[:, 0:N], rand[r:r + DH, c, :], self.qsT[r:r + DH, c, :], start=True, stop=False)
            pe.matmul(tile.ps[:, 0:N], self.k.minus_half[r:r + DH, :], self.sqT[r:r + DH, c, :],
                      start=False, stop=True).then_inc(*tile.filled.by)
            yield 1.0

    def a(self, act):
        for h, tile in enumerate(self.tiles):
            act.wait_ge(*tile.filled.at)
            act.activation(self.rf[:, h, :], tile.ps[:, 0:N], ACT.Exp).then_inc(*tile.drained.by)
            yield 1.0

    def v(self, dve):
        step = lambda ins: self.lane.step("V", dve, ins)
        wait_all(dve, self.after)
        dve.tensor_tensor(self.sqT, self.qsT, self.qsT, ALU.mult).then_inc(*self.squared.by)
        yield 12.0
        features = 2 * DH
        dve.wait_ge(*self.tiles[-1].drained.at)
        step(dve.tensor_tensor(self.tmp, self.rf, self.rf, ALU.mult))
        step(dve.tensor_reduce(self.ss, self.tmp, AX.X, ALU.add))
        dve.tensor_scalar(self.ss, self.ss, 1.0 / features, None, ALU.mult).then_inc(*self.power.ready.by)
        dve.wait_ge(*self.power.done.at)
        step(dve.tensor_scalar(self.ss, self.ss, 1e-12, None, ALU.max))
        step(dve.reciprocal(self.ss, self.ss))
        step(dve.tensor_scalar(self.ss, self.ss, float(features) ** -0.5, None, ALU.mult))
        dve.tensor_tensor(self.rf, self.rf, self.ss.unsqueeze(2).to_broadcast([P, H, N]), ALU.mult).then_inc(
            *self.done.by)
        dve.wait_ge(*self.done.at)
        yield 15.0


class SparseCodes(Stage):
    time = 75.0
    LAM, STEPS = 0.3, 5

    def __init__(self, lane, k, rf, v, qn, kk, kv, s, g, z, outT, small, after=()):
        super().__init__(lane)
        self.k, self.rf, self.value, self.qn, self.kk, self.kv, self.sparse, self.g, self.z = k, rf, v, qn, kk, kv, s, g, z
        self.outT, self.after = outT, after
        self.row = small[:, 0:H]
        self.diag = small[:, H:2 * H]
        self.inv = small[:, 2 * H:3 * H]
        self.lipschitz = small[:, 3 * H:4 * H]
        self.turned = [lane.tile("V") for _ in range(H // 2)]
        self.gram = [lane.tile("V") for _ in range(3)]
        self.cross = [lane.tile("V") for _ in range(2)]
        self.summed = lane.mark("V")
        self.sums = lane.tile("V")
        self.diagonal = lane.mark("V")
        self.spread = lane.tile("V")
        self.code = [lane.mark("V") for _ in range(self.STEPS + 1)]
        self.grad = [[lane.tile("V") for _ in range(2)] for _ in range(self.STEPS)]
        self.out = [lane.tile("V") for _ in range(KC)]
        self.done = self.out[-1].drained

    HEADS = ((0, 8), (8, 12))

    def t(self, pe):
        k = self.k
        wait_all(pe, self.after)
        for i, tile in enumerate(self.turned):
            fill(pe, tile)
            for t in range(NT):
                for j in range(2):
                    mm = pe.transpose(tile.ps[:, (2 * t + j) * P:(2 * t + j + 1) * P],
                                      self.rf[:, 2 * i + j, t * P:(t + 1) * P], k.ident)
            mm.then_inc(*tile.filled.by)
        pe.wait_ge(*self.turned[-1].drained.at)
        for i, tile in enumerate(self.gram):
            fill(pe, tile)
            for j in range(4):
                for t in range(NT):
                    qn = self.qn[:, t, 4 * i + j, :]
                    mm = pe.matmul(tile.ps[:, j * P:(j + 1) * P], qn, qn, start=(t == 0), stop=(t == NT - 1))
            mm.then_inc(*tile.filled.by)
        for (a, z), tile in zip(self.HEADS, self.cross):
            fill(pe, tile)
            for h in range(a, z):
                for t in range(NT):
                    mm = pe.matmul(tile.ps[:, (h - a) * DH:(h - a + 1) * DH], self.qn[:, t, h, :],
                                   self.value[:, t, h * DH:(h + 1) * DH], start=(t == 0), stop=(t == NT - 1))
            mm.then_inc(*tile.filled.by)
        yield 25.0
        fill(pe, self.sums)
        pe.wait_ge(*self.summed.at)
        pe.transpose(self.sums.ps[0:H, 0:P], self.row, k.ident).then_inc(*self.sums.filled.by)
        fill(pe, self.spread)
        pe.wait_ge(*self.diagonal.at)
        pe.matmul(self.spread.ps[:, 0:H], k.ones[0:H, :], self.diag[0:H, :], start=True, stop=True).then_inc(
            *self.spread.filled.by)
        yield 9.0
        for n in range(self.STEPS):
            pe.wait_ge(*self.code[n].at)
            for (a, z), tile in zip(self.HEADS, self.grad[n]):
                fill(pe, tile)
                for h in range(a, z):
                    mm = pe.matmul(tile.ps[:, (h - a) * DH:(h - a + 1) * DH], self.kk[:, h, :],
                                   self.sparse[:, h * DH:(h + 1) * DH], start=True, stop=True)
                mm.then_inc(*tile.filled.by)
            yield 6.0
        pe.wait_ge(*self.code[self.STEPS].at)
        for c, tile in enumerate(self.out):
            fill(pe, tile)
            for j in range(2):
                mm = pe.matmul(tile.ps[:, j * N:(j + 1) * N], self.sparse[:, c * P:(c + 1) * P], self.rf[:, 2 * c + j, :],
                               start=True, stop=True)
            mm.then_inc(*tile.filled.by)
            yield 1.5

    def threshold(self, dve, step, z):
        step(dve.tensor_scalar(self.g, z, -self.LAM, self.LAM, ALU.max, ALU.min))
        return dve.tensor_tensor(self.sparse, z, self.g, ALU.subtract)

    def v(self, dve):
        step = lambda ins: self.lane.step("V", dve, ins)
        for i, tile in enumerate(self.turned):
            dve.wait_ge(*tile.filled.at)
            dve.tensor_copy(self.qn[:, :, 2 * i:2 * i + 2, :].rearrange("p t h m -> p t (h m)"),
                            tile.ps.rearrange("p (t x) -> p t x", t=NT)).then_inc(*tile.drained.by)
        for i, tile in enumerate(self.gram):
            dve.wait_ge(*tile.filled.at)
            dve.tensor_copy(self.kk[:, 4 * i:4 * i + 4, :].rearrange("p h m -> p (h m)"), tile.ps).then_inc(
                *tile.drained.by)
        for (a, z), tile in zip(self.HEADS, self.cross):
            dve.wait_ge(*tile.filled.at)
            dve.tensor_copy(self.kv[:, a * DH:z * DH], tile.ps[:, 0:(z - a) * DH]).then_inc(*tile.drained.by)
        dve.wait_ge(*self.cross[-1].drained.at)
        yield 25.0
        dve.tensor_reduce(self.row, self.kk, AX.X, ALU.add, apply_absolute_value=True).then_inc(*self.summed.by)
        dve.wait_ge(*self.sums.filled.at)
        dve.tensor_reduce(self.inv[0:H, 0:1], self.sums.ps[0:H, 0:P], AX.X, ALU.max).then_inc(*self.sums.drained.by)
        dve.wait_ge(*self.sums.drained.at)
        dve.tensor_scalar(self.diag[0:H, :], self.k.ident[0:H, 0:H], self.inv[0:H, 0:1], None, ALU.mult).then_inc(
            *self.diagonal.by)
        dve.wait_ge(*self.spread.filled.at)
        dve.wait_ge(*self.diagonal.at)
        dve.tensor_scalar(self.lipschitz, self.spread.ps[:, 0:H], 1.0, None, ALU.add).then_inc(
            *self.spread.drained.by)
        dve.wait_ge(*self.spread.drained.at)
        wide = lambda ap, n: ap.unsqueeze(2).to_broadcast([P, H, n])
        heads = self.sparse.rearrange("p (h d) -> p h d", h=H)
        step(dve.reciprocal(self.inv, self.lipschitz))
        step(dve.tensor_tensor(self.kk, self.kk, wide(self.inv, P), ALU.mult))
        dve.tensor_tensor(self.kk, self.k.ident.unsqueeze(1).to_broadcast([P, H, P]), self.kk, ALU.subtract)
        step(self.threshold(dve, step, self.kv))
        dve.tensor_tensor(heads, heads, wide(self.lipschitz, DH), ALU.mult).then_inc(*self.code[0].by)
        dve.wait_ge(*self.code[0].at)
        yield 9.0
        for n in range(self.STEPS):
            for (a, z), tile in zip(self.HEADS, self.grad[n]):
                dve.wait_ge(*tile.filled.at)
                dve.tensor_tensor(self.z[:, a * DH:z * DH], tile.ps[:, 0:(z - a) * DH],
                                  self.kv[:, a * DH:z * DH], ALU.add).then_inc(*tile.drained.by)
            dve.wait_ge(*self.grad[n][-1].drained.at)
            ins = self.threshold(dve, step, self.z)
            if n == self.STEPS - 1:
                step(ins)
                ins = dve.tensor_tensor(heads, heads, wide(self.inv, DH), ALU.mult)
            ins.then_inc(*self.code[n + 1].by)
            dve.wait_ge(*self.code[n + 1].at)
            yield 6.0
        for c, tile in enumerate(self.out):
            dve.wait_ge(*tile.filled.at)
            for j in range(2):
                ins = dve.tensor_copy(self.outT[j * DH:(j + 1) * DH, c, :],
                                      tile.ps[j * DH:(j + 1) * DH, j * N:(j + 1) * N])
            ins.then_inc(*tile.drained.by)
            yield 1.5


class EdgeSoftmax(Stage):

    def __init__(self, lane, k, a_src, a_dst, heads, adj, cap, diag, e, small, out, guard, after=()):
        super().__init__(lane)
        self.k, self.a_src, self.a_dst, self.heads, self.adj, self.cap = k, a_src, a_dst, heads, adj, cap
        self.diag, self.e, self.out, self.guard, self.after = diag, e, out, guard, after
        self.top = small[:, 0:6].rearrange("p (b t) -> p b t", t=NT)
        self.total = small[:, 6:12].rearrange("p (b t) -> p b t", t=NT)
        self.diagonal, self.row, self.added, self.shifted, self.exped, self.normed, self.turn = (
            {}, {}, {}, {}, {}, {}, {})
        for i in range(heads + 4):
            if i < heads:
                self.diagonal[i] = lane.mark("V")
                self.row[i] = lane.tile("A")
            if 0 <= i - 1 < heads:
                self.shifted[i - 1] = lane.mark("V")
            if 0 <= i - 2 < heads:
                self.exped[i - 2] = lane.mark("A")
                self.normed[i - 2] = lane.mark("V")
            if 0 <= i - 3 < heads:
                self.turn[i - 3] = lane.tile("A")
        self.done = self.turn[heads - 1].drained
        self.time = 4.0 * (heads + 4)

    def t(self, pe):
        k = self.k
        wait_all(pe, self.after)
        for i in range(self.heads + 4):
            if i < self.heads:
                fill(pe, self.row[i])
                pe.wait_ge(*self.diagonal[i].at)
                for t in range(NT):
                    mm = pe.matmul(self.row[i].ps[:, t * P:(t + 1) * P], k.ones, self.diag[i % 2][:, t, :],
                                   start=True, stop=True)
                mm.then_inc(*self.row[i].filled.by)
            if 0 <= i - 3 < self.heads:
                h = i - 3
                fill(pe, self.turn[h])
                pe.wait_ge(*self.normed[h].at)
                for s in range(NT):
                    for t in range(NT):
                        mm = pe.transpose(self.turn[h].ps[:, s * N + t * P:s * N + (t + 1) * P],
                                          self.e[h % 3][:, t, s * P:(s + 1) * P], k.ident)
                mm.then_inc(*self.turn[h].filled.by)
            yield 4.0

    def v(self, dve):
        step = lambda ins: self.lane.step("V", dve, ins)
        wait_all(dve, self.after)
        for i in range(self.heads + 4):
            if i < self.heads:
                if i >= 2:
                    dve.wait_ge(*self.row[i - 2].filled.at)
                for t in range(NT):
                    ins = dve.tensor_scalar(self.diag[i % 2][:, t, :], self.k.ident, self.a_src[:, t, i:i + 1], None,
                                            ALU.mult)
                ins.then_inc(*self.diagonal[i].by)
            if 0 <= i - 1 < self.heads:
                h = i - 1
                e, top = self.e[h % 3], self.top[:, h % 3, :]
                dve.wait_ge(*self.row[h].drained.at)
                step(dve.scalar_tensor_tensor(out=e, in0=e, scalar=0.2, in1=e, op0=ALU.mult, op1=ALU.max))
                step(dve.tensor_tensor(e, e, self.cap, ALU.min))
                step(dve.tensor_reduce(top, e, AX.X, ALU.max))
                dve.tensor_scalar(top, top, -1.0, None, ALU.mult).then_inc(*self.shifted[h].by)
            if 0 <= i - 2 < self.heads:
                h = i - 2
                e, total = self.e[h % 3], self.total[:, h % 3, :]
                dve.wait_ge(*self.exped[h].at)
                step(dve.tensor_tensor(e, e, self.adj, ALU.mult))
                step(dve.tensor_reduce(total, e, AX.X, ALU.add))
                if self.guard:
                    step(dve.tensor_scalar(total, total, 0.5, None, ALU.max))
                step(dve.reciprocal(total, total))
                for t in range(NT):
                    ins = dve.tensor_scalar(e[:, t, :], e[:, t, :], total[:, t:t + 1], None, ALU.mult)
                ins.then_inc(*self.normed[h].by)
            yield 4.0

    def a(self, act):
        for i in range(self.heads + 4):
            if i < self.heads:
                e, row = self.e[i % 3], self.row[i]
                if i >= 3:
                    act.wait_ge(*self.turn[i - 3].filled.at)
                act.wait_ge(*row.filled.at)
                for t in range(NT):
                    ins = act.activation(e[:, t, :], row.ps[:, 0:N], ACT.Identity, bias=self.a_dst[:, t, i:i + 1])
                ins.then_inc(*row.drained.by)
            if 0 <= i - 2 < self.heads:
                h = i - 2
                act.wait_ge(*self.shifted[h].at)
                for t in range(NT):
                    ins = act.activation(self.e[h % 3][:, t, :], self.e[h % 3][:, t, :], ACT.Exp,
                                         bias=self.top[:, h % 3, t:t + 1])
                ins.then_inc(*self.exped[h].by)
            if 0 <= i - 3 < self.heads:
                h = i - 3
                act.wait_ge(*self.turn[h].filled.at)
                act.activation(self.out[:, h, :, :], self.turn[h].ps.rearrange("p (s n) -> p s n", s=NT),
                               ACT.Copy).then_inc(*self.turn[h].drained.by)
            yield 4.0


class AggregateTokens(Stage):
    time = 8.0

    def __init__(self, lane, k, probsT, heads, h, drain, after=(), drain_after=()):
        super().__init__(lane)
        self.probsT, self.heads, self.h, self.drain = probsT, heads, h, drain
        self.after, self.drain_after = after, drain_after
        self.tiles = [lane.tile("V") for _ in range(2 * NT)]
        self.done = self.tiles[-1].drained

    def t(self, pe):
        wait_all(pe, self.after)
        width = min(D // self.heads, COLS)
        for i, tile in enumerate(self.tiles):
            t, g = divmod(i, 2)
            fill(pe, tile)
            for a in range(0, COLS, width):
                head = (g * COLS + a) * self.heads // D
                for s in range(NT):
                    mm = pe.matmul(tile.ps[:, a:a + width], self.probsT[:, head, s, t * P:(t + 1) * P],
                                   self.h[:, s, g * COLS + a:g * COLS + a + width], start=(s == 0), stop=(s == NT - 1))
            mm.then_inc(*tile.filled.by)
            yield self.time / 4

    def v(self, dve):
        wait_all(dve, self.drain_after)
        for i, tile in enumerate(self.tiles):
            t, g = divmod(i, 2)
            dve.wait_ge(*tile.filled.at)
            self.drain(dve, t, g, tile.ps[:, 0:COLS]).then_inc(*tile.drained.by)
            yield self.time / 4


class HeadMatrices(Stage):
    time = 8.0

    def __init__(self, lane, k, xT, both, outs, after=()):
        super().__init__(lane)
        self.xT, self.both, self.outs, self.after = xT, both, outs, after
        self.loads = [both]
        self.tiles = [lane.tile("V") for _ in range(2 * 2 * NT)]
        both.freed = self.tiles[-1].filled
        self.done = self.tiles[-1].drained

    def t(self, pe):
        wait_all(pe, self.after)
        pe.wait_ge(*self.both.at)
        for i, tile in enumerate(self.tiles):
            o, t, g = i // 4, i // 2 % 2, i % 2
            fill(pe, tile)
            for c in range(3):
                mm = pe.matmul(tile.ps[:, c * P:(c + 1) * P], self.xT[:, 3 * g + c, t * P:(t + 1) * P],
                               self.both.ap[:, o * P:(o + 1) * P], start=True, stop=True)
            mm.then_inc(*tile.filled.by)
            yield 1.0

    def v(self, dve):
        for i, tile in enumerate(self.tiles):
            o, t, g = i // 4, i // 2 % 2, i % 2
            dve.wait_ge(*tile.filled.at)
            dve.tensor_copy(half(self.outs[o], t, g), tile.ps[:, 0:COLS]).then_inc(*tile.drained.by)
            yield 1.0


class PolynomialAttention(Stage):

    def __init__(self, lane, k, qT, kT, v, outT, num, inv, scale, after=()):
        super().__init__(lane)
        self.k, self.qT, self.kT, self.value, self.outT, self.num, self.inv = k, qT, kT, v, outT, num, inv
        self.scale, self.after = scale, after
        self.score, self.out, self.raised = [], [], []
        for i in range(H + 1):
            if i < H:
                self.score.append(lane.tile("A"))
                self.raised.append(lane.mark("V"))
            if i >= 1:
                self.out.append(lane.tile("V"))
        self.done = self.out[-1].drained
        self.time = 3.2 * (H + 1)

    def t(self, pe):
        wait_all(pe, self.after)
        for i in range(H + 1):
            if i < H:
                c, r = i // 2, (i % 2) * DH
                fill(pe, self.score[i])
                for m in range(NT):
                    mm = pe.matmul(self.score[i].ps[:, m * N:(m + 1) * N], self.kT[r:r + DH, c, m * P:(m + 1) * P],
                                   self.qT[r:r + DH, c, :], start=True, stop=True)
                mm.then_inc(*self.score[i].filled.by)
            if i >= 1:
                h = i - 1
                fill(pe, self.out[h])
                pe.wait_ge(*self.raised[h].at)
                num = self.num[h % 2]
                for m in range(NT):
                    pe.matmul(self.out[h].ps[:, 0:N], self.value[:, m, (h // 2) * P:(h // 2 + 1) * P], num[:, m, :],
                              start=(m == 0), stop=(m == NT - 1))
                for m in range(NT):
                    mm = pe.matmul(self.out[h].ps[:, N:2 * N], self.k.ones, num[:, m, :],
                                   start=(m == 0), stop=(m == NT - 1))
                mm.then_inc(*self.out[h].filled.by)
            yield 3.2

    def a(self, act):
        for i in range(H + 1):
            if i < H:
                act.wait_ge(*self.score[i].filled.at)
                if i >= 2:
                    act.wait_ge(*self.out[i - 2].filled.at)
                act.activation(self.num[i % 2], self.score[i].ps.rearrange("p (m n) -> p m n", m=NT), ACT.Square,
                               bias=self.k.ones[:, 0:1], scale=self.scale).then_inc(*self.score[i].drained.by)
            yield 3.2

    def v(self, dve):
        for i in range(H + 1):
            if i < H:
                dve.wait_ge(*self.score[i].drained.at)
                dve.tensor_scalar(self.num[i % 2], self.num[i % 2], 1.0, None, ALU.add).then_inc(*self.raised[i].by)
            if i >= 1:
                h = i - 1
                c, r = h // 2, (h % 2) * DH
                dve.wait_ge(*self.out[h].filled.at)
                if h:
                    dve.wait_ge(*self.out[h - 1].drained.at)
                self.lane.step("V", dve, dve.reciprocal(self.inv[r:r + DH, :], self.out[h].ps[r:r + DH, N:2 * N]))
                dve.tensor_tensor(self.outT[r:r + DH, c, :], self.out[h].ps[r:r + DH, 0:N], self.inv[r:r + DH, :],
                                  ALU.mult).then_inc(*self.out[h].drained.by)
            yield 3.2


class RouteScores(Stage):
    time = 25.0

    def __init__(self, lane, k, xT, wr_rep, scores, tmp, mixT, mask, small, take, after=()):
        super().__init__(lane)
        self.k, self.xT, self.wr_rep, self.scores, self.tmp, self.mixT = k, xT, wr_rep, scores, tmp, mixT
        self.mask, self.small, self.take, self.after = mask, small, take, after
        self.spread = lane.mark("V")
        self.tile = lane.tile("A")
        self.mixed, self.done = lane.mark("V"), lane.mark("V")

    def t(self, pe):
        wait_all(pe, self.after)
        pe.wait_ge(*self.spread.at)
        fill(pe, self.tile)
        for c in range(KC):
            mm = pe.matmul(self.tile.ps[:, 0:N], self.wr_rep[:, c, :], self.xT[:, c, :], start=(c == 0),
                           stop=(c == KC - 1))
        mm.then_inc(*self.tile.filled.by)
        yield self.time

    def a(self, act):
        act.wait_ge(*self.tile.filled.at)
        act.activation(self.scores, self.tile.ps[:, 0:N], ACT.Sigmoid, bias=self.k.short("br")).then_inc(
            *self.tile.drained.by)
        yield self.time

    def v(self, dve):
        k = self.k
        step = lambda ins: self.lane.step("V", dve, ins)
        wait_all(dve, self.after)
        a, z = NARROW["wr"][0], NARROW["wr"][0] + 1
        dve.tensor_copy(self.wr_rep, k.narrow[:, :, a:z].to_broadcast([P, KC, P])).then_inc(*self.spread.by)
        dve.wait_ge(*self.tile.drained.at)
        own, rank, total = self.small[:, 0:2], self.small[:, 2:4], self.small[:, 4:5]
        pooled = self.small[:, 8:8 + KC]
        two = self.tmp[:, 0, :].rearrange("p (t j) -> p t j", t=NT)
        step(dve.tensor_tensor(self.tmp, self.xT, self.scores.unsqueeze(1).to_broadcast([P, KC, N]), ALU.mult))
        step(dve.tensor_reduce(pooled, self.tmp, AX.X, ALU.add))
        step(dve.tensor_reduce(total, self.scores, AX.X, ALU.add))
        step(dve.tensor_scalar(total, total, 1e-6, None, ALU.add))
        step(dve.reciprocal(total, total))
        step(dve.tensor_scalar(pooled, pooled, total, None, ALU.mult))
        for c in range(KC):
            ins = dve.scalar_tensor_tensor(out=self.mixT[:, c, :], in0=self.scores, scalar=pooled[:, c:c + 1],
                                           in1=self.xT[:, c, :], op0=ALU.mult, op1=ALU.add)
        ins.then_inc(*self.mixed.by)
        dve.wait_ge(*self.mixed.at)
        step(dve.tensor_tensor(two, self.scores.rearrange("p (t j) -> p t j", t=NT),
                               k.ident.unsqueeze(1).to_broadcast([P, NT, P]), ALU.mult))
        step(dve.tensor_reduce(own, two, AX.X, ALU.add))
        for t in range(NT):
            step(dve.tensor_scalar(self.tmp[:, 0, :], self.scores, own[:, t:t + 1], None, ALU.is_equal))
            step(dve.tensor_scalar(self.tmp[:, 1, :], k.iota, k.rowid[:, t:t + 1], None, ALU.is_lt))
            step(dve.tensor_tensor(self.tmp[:, 0, :], self.tmp[:, 0, :], self.tmp[:, 1, :], ALU.mult))
            step(dve.tensor_scalar(self.tmp[:, 1, :], self.scores, own[:, t:t + 1], None, ALU.is_lt))
            step(dve.tensor_tensor(self.tmp[:, 0, :], self.tmp[:, 0, :], self.tmp[:, 1, :], ALU.add))
            step(dve.tensor_reduce(rank[:, t:t + 1], self.tmp[:, 0, :], AX.X, ALU.add))
        dve.tensor_scalar(self.mask, rank, float(self.take), None, ALU.is_lt).then_inc(*self.done.by)
        dve.wait_ge(*self.done.at)
        yield self.time


class HeadNorm(Stage):
    time = 10.0

    def __init__(self, lane, k, x, tmp, small, after=()):
        super().__init__(lane)
        self.x, self.tmp, self.small, self.after = x, tmp, small[:, 0:NT * H], after
        self.power = Power(lane, k, self.small, INVERSE_ROOT)
        self.done = lane.mark("V")

    def p(self, pool):
        self.power.p(pool)
        yield self.time

    def v(self, dve):
        step = lambda ins: self.lane.step("V", dve, ins)
        heads = lambda ap: ap.rearrange("p t (h d) -> p (t h) d", d=DH)
        x, tmp, m = heads(self.x), heads(self.tmp), self.small
        wide = m.unsqueeze(2).to_broadcast([P, NT * H, DH])
        wait_all(dve, self.after)
        step(dve.tensor_reduce(m, x, AX.X, ALU.add))
        step(dve.tensor_scalar(m, m, 1.0 / DH, None, ALU.mult))
        step(dve.tensor_tensor(x, x, wide, ALU.subtract))
        step(dve.tensor_tensor(tmp, x, x, ALU.mult))
        step(dve.tensor_reduce(m, tmp, AX.X, ALU.add))
        dve.tensor_scalar(m, m, 1.0 / DH, 1e-5, ALU.mult, ALU.add).then_inc(*self.power.ready.by)
        dve.wait_ge(*self.power.done.at)
        dve.tensor_tensor(x, x, wide, ALU.mult).then_inc(*self.done.by)
        dve.wait_ge(*self.done.at)
        yield self.time


class Adapters(Stage):
    time = 6.0

    def __init__(self, lane, k, xT, a_t, combine2, hw, experts, rank, after=()):
        super().__init__(lane)
        self.k, self.xT, self.a_t, self.combine2, self.hw, self.after = k, xT, a_t, combine2, hw, after
        self.experts, self.rank = experts, rank
        self.loads = [a_t]
        self.tile = lane.tile("V")
        a_t.freed = self.tile.filled
        self.done = lane.mark("V")

    def t(self, pe):
        wait_all(pe, self.after)
        pe.wait_ge(*self.a_t.at)
        fill(pe, self.tile)
        w = self.a_t.ap.rearrange("p (c n) -> p c n", c=KC)
        for t in range(NT):
            for c in range(KC):
                mm = pe.matmul(self.tile.ps[:, t * P:(t + 1) * P], self.xT[:, c, t * P:(t + 1) * P], w[:, c, :],
                               start=(c == 0), stop=(c == KC - 1))
        mm.then_inc(*self.tile.filled.by)
        yield self.time

    def v(self, dve):
        dve.wait_ge(*self.tile.filled.at)
        dve.tensor_tensor(self.hw, self.tile.ps[:, 0:N].rearrange("p (t n) -> p t n", t=NT),
                          self.k.short("ba").unsqueeze(1).to_broadcast([P, NT, P]), ALU.add).then_inc(
            *self.tile.drained.by)
        dve.wait_ge(*self.tile.drained.at)
        for t in range(NT):
            grouped = self.hw[:, t, :].rearrange("p (e r) -> p e r", e=self.experts)
            ins = dve.tensor_tensor(grouped, grouped,
                                    self.combine2[:, t, :].unsqueeze(2).to_broadcast([P, self.experts, self.rank]),
                                    ALU.mult)
        ins.then_inc(*self.done.by)
        dve.wait_ge(*self.done.at)
        yield self.time


class Activation(Stage):
    time = 1.5

    def __init__(self, lane, body, after=()):
        super().__init__(lane)
        self.body, self.after = body, after
        self.done = lane.mark("A")

    def a(self, act):
        wait_all(act, self.after)
        self.body(act).then_inc(*self.done.by)
        yield self.time


class AggregateRelu(Stage):
    time = 6.0

    def __init__(self, lane, k, h, probsT, out, bias, after=()):
        super().__init__(lane)
        self.k, self.h, self.probsT, self.out, self.bias, self.after = k, h, probsT, out, bias, after
        self.tiles = [lane.tile("A") for _ in range(KC)]
        self.done = self.tiles[-1].drained

    def t(self, pe):
        wait_all(pe, self.after)
        for c, tile in enumerate(self.tiles):
            fill(pe, tile)
            for s in range(NT):
                mm = pe.matmul(tile.ps[:, 0:N], self.h[:, s, c * P:(c + 1) * P], self.probsT[:, s, :],
                               start=(s == 0), stop=(s == NT - 1))
            mm.then_inc(*tile.filled.by)
            yield 1.0

    def a(self, act):
        for c, tile in enumerate(self.tiles):
            act.wait_ge(*tile.filled.at)
            act.activation(self.out[:, c, :], tile.ps[:, 0:N], ACT.Relu, bias=self.k.col(self.bias, c)).then_inc(
                *tile.drained.by)
            yield 1.0


class HalfDown(Stage):
    time = 8.0

    def __init__(self, lane, k, panel, xT, drain, after=()):
        super().__init__(lane)
        self.xT, self.drain, self.after = xT, drain, after
        self.panel = lane.panel(k.panel[panel])
        self.tiles = [lane.tile("V") for _ in range(2 * NT)]
        self.panel.freed = self.tiles[-1].filled
        self.loads = [self.panel]
        self.done = self.tiles[-1].drained

    def t(self, pe):
        wait_all(pe, self.after)
        pe.wait_ge(*self.panel.at)
        w = self.panel.ap.rearrange("p (k n) -> p k n", k=3)
        for i, tile in enumerate(self.tiles):
            t, g = divmod(i, 2)
            fill(pe, tile)
            for c in range(3):
                mm = pe.matmul(tile.ps[:, 0:COLS], self.xT[:, c, t * P:(t + 1) * P], w[:, c, g * COLS:(g + 1) * COLS],
                               start=(c == 0), stop=(c == 2))
            mm.then_inc(*tile.filled.by)
            yield 2.0

    def v(self, dve):
        for i, tile in enumerate(self.tiles):
            dve.wait_ge(*tile.filled.at)
            self.drain(dve, *divmod(i, 2), tile.ps[:, 0:COLS]).then_inc(*tile.drained.by)
            yield 2.0


class Idle(Stage):

    def __init__(self, lane, time):
        super().__init__(lane)
        self.time = time


class Fetch(Stage):
    time = 1.0

    def __init__(self, lane, sem, pairs, after=()):
        super().__init__(lane)
        self.sem, self.pairs, self.after = sem, pairs, after
        self.at = (sem, 16 * len(pairs))

    def s(self, sp):
        wait_all(sp, self.after)
        for ap, src in self.pairs:
            sp.dma_start(ap, src).then_inc(self.sem, 16)
        yield self.time


GATE_PACE = (2.2, 1.5)
GATE_FC = 0
GATE_UNIT = (3.2, 3.6)
POOL_NODES = (24, 21)


class Constants:

    def __init__(self, panel, ident, ones, blocks, minus_half, iota, rowid, adjT, adj, gcn, cols, narrow, shorts,
                 exponents, iota_int, rowid_int, edges_int, iota_bf, edges, dst_of, dis_diag, dis_col, inv):
        self.panel, self.ident, self.ones, self.blocks, self.minus_half = panel, ident, ones, blocks, minus_half
        self.iota, self.rowid, self.adjT, self.adj, self.gcn = iota, rowid, adjT, adj, gcn
        self.cols, self.narrow, self.shorts, self.exponents = cols, narrow, shorts, exponents
        self.iota_int, self.rowid_int, self.edges_int, self.iota_bf = iota_int, rowid_int, edges_int, iota_bf
        self.edges, self.dst_of, self.dis_diag, self.dis_col, self.inv = edges, dst_of, dis_diag, dis_col, inv

    def col(self, name, c=0):
        a, n = COLUMNS[name]
        return self.cols[:, a + c:a + c + 1]

    def short(self, name):
        a, n = SHORT[name]
        return self.shorts[:, a:a + n]

    def narrow_of(self, name):
        a, n = NARROW[name]
        return self.narrow[:, :, a:a + n]


def copy(dst):
    return lambda eng, i, ps: eng.tensor_copy(dst[:, i, :], ps)


def copy_half(dst):
    return lambda eng, t, g, ps: eng.tensor_copy(half(dst, t, g), ps)


def scaled(dst, factor):
    return lambda eng, i, ps: eng.tensor_scalar(dst[:, i, :], ps, factor, None, ALU.mult)


def plus_col(k, dst, name, first=0):
    return lambda eng, i, ps: eng.tensor_scalar(dst[:, i, :], ps, k.col(name, first + i), None, ALU.add)


def affine(k, dst, weight, bias):
    return lambda eng, i, ps: eng.tensor_scalar(dst[:, i, :], ps, k.col(weight, i), k.col(bias, i), ALU.mult, ALU.add)


def head_affine(k, dst, weight, bias):
    return lambda eng, i, ps: eng.tensor_scalar(dst[:, i, :], ps, k.col(weight), k.col(bias), ALU.mult, ALU.add)


def plus_row(dst, row):
    return lambda eng, t, g, ps: eng.tensor_tensor(half(dst, t, g), ps, row.ap[:, g * COLS:(g + 1) * COLS], ALU.add)


def onto(dst):
    return lambda eng, t, g, ps: eng.tensor_tensor(half(dst, t, g), ps, half(dst, t, g), ALU.add)


def act_col(k, dst, func, name=None, first=0):
    def drain(eng, i, ps):
        if name is None:
            return eng.activation(dst[:, i, :], ps, func)
        return eng.activation(dst[:, i, :], ps, func, bias=k.col(name, first + i))
    return drain


def build(nc, x_in, src, dst, edge_type, panels, cols, rows, narrow, shorts, query_t, b2, rand, head_mats,
          a_t, bm, bb, out, last_layer=3):
    with ExitStack() as ctx:
        sb = lambda name, shape, dt=F32: ctx.enter_context(nc.sbuf_tensor(name, shape, dt))
        sem = lambda name: ctx.enter_context(nc.semaphore(name))
        with ExitStack() as over:
            rounded = lambda name, n: over.enter_context(nc.sbuf_tensor(name, [P, n], F32R))[:, :]
            low = [rounded(f"gate_low{i}", D) for i in range(2)]
            pairs = rounded("gate_pairs", 6 * COLS)[:, 0:NB * L]
            rounded("before_unit_2", 2 * UNIT)
            high = [rounded(f"gate_high{i}", D) for i in range(2)]
            weight_parts = [(rounded(f"weight_high{i}", 6 * COLS), rounded(f"weight_low{i}", 6 * COLS))
                            for i in range(3)]
            rounded("before_unit_15", 3 * UNIT)
            input_parts = [rounded("input_high", UNIT), rounded("input_low", UNIT)]
            hidden_parts = [[rounded(f"hidden_{name}{i}", 3 * N) for name in ("high", "low")] for i in range(2)]
        with ExitStack() as over:
            rounded = lambda name, n: over.enter_context(nc.sbuf_tensor(name, [P, n], F32R))[:, :]
            rounded("before_unit_1", 2 * D + 6 * COLS + UNIT)
            later_low = rounded("later_input_low", UNIT)
            rounded("before_unit_14", 12 * UNIT)
            later_buffers = SplitBuffers([(rounded(f"later_weight_high{i}", 6 * COLS),
                                           rounded(f"later_weight_low{i}", 6 * COLS)) for i in range(2)])
            later_high = rounded("later_input_high", UNIT)
        later_parts = [ap.rearrange("p (c n) -> p c n", c=KC) for ap in (later_high, later_low)]
        row_ring = [sb(f"row{i}", [P, D]) for i in range(2)]
        panel3 = sb("panel3", [P, 6 * COLS])
        arena = sb("arena", [P, 21 * UNIT])
        row_ring.append(sb("row2", [P, D]))
        panel_ring = [panel3 if i == 3 else sb(f"panel{i}", [P, 6 * COLS]) for i in range(7)]
        u = lambda i, n=1: arena[:, i * UNIT:(i + n) * UNIT]
        tok = lambda i: u(i).rearrange("p (t d) -> p t d", t=NT)
        fea = lambda i: u(i).rearrange("p (c n) -> p c n", c=KC)

        small_g, small_m = sb("small_g", [P, 188]), sb("small_m", [P, 104])
        shared_ints = u(12)[:, 0:512 + 96].bitcast(I32)
        graph_f = u(13)
        k = Constants(
            panel=[panels[i] for i in range(N_PANELS)],
            ident=sb("ident", [P, P])[:, :], ones=sb("ones", [P, P])[:, :], blocks=sb("blocks", [P, P])[:, :],
            minus_half=u(12)[:, 0:P], iota=sb("iota", [P, N])[:, :], rowid=sb("rowid", [P, NT])[:, :],
            adjT=u(14)[:, 0:512].rearrange("p (t n) -> p t n", t=NT), adj=sb("adj", [P, NT, N])[:, :, :],
            gcn=sb("gcn", [P, NT, N])[:, :, :],
            cols=sb("cols", [P, N_COLUMNS])[:, :], narrow=sb("narrow", [P, KC, N_NARROW])[:, :, :],
            shorts=sb("shorts", [P, N_SHORT])[:, :], exponents=sb("exponents", [P, 2])[:, :],
            iota_int=shared_ints[:, 0:256], rowid_int=shared_ints[:, 256:258],
            edges_int=shared_ints[:, 512:608].rearrange("p (i c) -> p i c", i=3),
            iota_bf=graph_f[:, 0:128].bitcast(BF16), edges=graph_f[:, 128:224].rearrange("p (i c) -> p i c", i=3),
            dst_of=graph_f[:, 224:320].rearrange("p (r c) -> p r c", r=R), dis_diag=graph_f[:, 320:576],
            dis_col=graph_f[:, 576:578], inv=graph_f[:, 640:1408])

        banks = [ctx.enter_context(nc.psum_tensor(f"bank{i}", [P, 512], F32))[:, :] for i in range(8)]
        users = [None] * 8
        slots = Slots([r[:, :] for r in panel_ring], [sem(f"panel{i}_arrived") for i in range(7)])
        row_slots = Slots([r[:, :] for r in row_ring], [sem(f"row{i}_arrived") for i in range(3)])
        x_arrived, edges_arrived, small_arrived, query_arrived = (
            sem("x_arrived"), sem("edges_arrived"), sem("small_arrived"), sem("query_arrived"))
        adapters_arrived, out_written = sem("adapters_arrived"), sem("out_written")

        class At:
            def __init__(self, s, v):
                self.at = (s, v)

        def lane(name, which, pslots, rslots):
            return Lane(sem, name, [(banks[i], i) for i in which], users, slots, pslots, row_slots, rslots)

        def row(lane_, name):
            return lane_.row(rows[ROWS[name]:ROWS[name] + 1, :].to_broadcast([P, D]))

        k.edges_at = (edges_arrived, 48)
        cols_at = At(small_arrived, 48)
        X, XN, XNT = tok(0), tok(1), fea(2)
        segments = []

        S = lane("start", range(8), range(7), range(3))
        segments.append((S,))
        averages = tok(3)
        agg = u(4, 3).rearrange("p (c n) -> p c n", c=KC)
        zs = [arena[:, 4 * UNIT + i * 2048:4 * UNIT + (i + 1) * 2048] for i in range(3)]
        QG = u(8, 2).rearrange("p (t d) -> p t d", t=B * L // P)
        QT = u(10, 2).rearrange("p (c n) -> p c n", c=KC)
        H1, H2, H3 = fea(12), fea(13), fea(14)

        consts = Setup(S, k)
        norm = LayerNorm(S, k, X, XN, 1e-5, small_g, after=[At(x_arrived, 16)])
        turn = ToFeatures(S, k, XN, copy(XNT), after=[norm.done])

        gate_rows = [row_ring[i][:, :] for i in range(2)]
        rows_arrived = [sem(f"gate_rows{i}_arrived") for i in range(2)]

        G = lane("graph", (0, 1, 2, 3), (0, 1, 2), ())
        M = lane("mix", (4, 5, 6, 7), (4, 5, 6), (2,))
        segments.append((G, M))
        graph = Graph(G, k, (u(4, 2), u(6, 2)), averages, consts.done)
        Idle(M, 6.0)
        M.pace = 1.3
        bg = row(M, "bg")
        qg = LinearTokens(M, k, [(PANELS["qg_w"], QT)], 2, plus_row(QG, bg), after=[At(query_arrived, 16)],
                          drain_after=[bg], rows=[bg], tokens=B * L)
        bg.freed = qg.done
        code = PairCode(M, k, pairs, after=[consts.done])

        gates_at, gates = [], []

        def rgcn(h, hT, panels_at, bias, after):
            a = Aggregate(G, k, h, averages, 768, agg, after=after)
            inputs = [(panels_at + 2 * r, agg[:, :, r * N:(r + 1) * N]) for r in range(R)]
            inputs.append((panels_at + 2 * R, hT))
            lin = LinearFeatures(G, k, inputs, KC, act_col(k, H1, ACT.Relu, bias), "A", after=[a.done])
            hg = LinearTokens(G, k, [(PANELS["hg_w"], H1)], 2, copy_half(tok(13)), after=[lin.done])
            gates_at.append(G.time())
            gate = GateSum(G, tok(13), QG, QT, H3, zs, pairs, gate_rows, high, low,
                           [(s, (len(gates_at) - 1) * 16 * B) for s in rows_arrived],
                           GATE_UNIT[len(gates)], POOL_NODES[len(gates)],
                           after=[hg.done, lin.done, qg.done, code.done])
            gates.append(gate)
            alpha = LinearFeatures(G, k, [(PANELS["alpha_w"], H1), (PANELS["alpha_w"] + 2, H3)], KC,
                                   act_col(k, H2, ACT.Sigmoid, "bq"), "A", after=[gate.done])
            return GateMix(G, u(13), u(14), u(12), u(13), after=[alpha.done])

        first = rgcn(XN, XNT, PANELS["rel1"], "b1", [graph.averaged, turn.done])
        h_tok = tok(14)
        back = ToTokens(G, k, H2, copy_half(h_tok), after=[first.done])
        second = rgcn(h_tok, H2, PANELS["rel2"], "b2", [back.done])
        gnn_out = ToTokens(G, k, H2, onto(X), after=[second.done])

        for s, which in ((slots, 3), (row_slots, 0), (row_slots, 1)):
            s.last[which] = Load(None, None, None, 0, None)
            s.last[which].freed = gates[1].used[-1]

        a_, b_, c_, d_, e_, f_ = 15, 16, 17, 18, 19, 20
        m_after = [turn.done, cols_at]
        m_norm = LayerNorm(M, k, XN, tok(e_), 1e-8, small_m, after=m_after)
        m_turn = ToFeatures(M, k, tok(e_), affine(k, fea(a_), "ln1w", "ln1b"), after=[m_norm.done])
        q = LinearFeatures(M, k, [(PANELS["l0_qkv"], fea(a_))], KC, plus_col(k, fea(b_), "l0_qb"), "V",
                           after=[m_turn.done])
        M.pace = 1.0
        Idle(M, gates_at[0] - M.time())
        M.pace = GATE_PACE[0]
        kb, vb = row(M, "l0_kb"), row(M, "l0_vb")
        key = LinearTokens(M, k, [(PANELS["l0_qkv"] + 2, fea(a_))], 2, plus_row(tok(c_), kb), drain_after=[kb],
                           rows=[kb])
        kb.freed = key.done
        val = LinearTokens(M, k, [(PANELS["l0_qkv"] + 4, fea(a_))], 2, plus_row(tok(d_), vb), drain_after=[vb],
                           rows=[vb])
        vb.freed = val.done
        elu_q = EluPlusOne(M, u(b_), u(e_), after=[q.done])
        elu_k = EluPlusOne(M, u(c_), u(f_), after=[key.done])
        states = u(a_)[:, 0:KC * P].rearrange("p (c e) -> p c e", c=KC)
        norms = u(a_)[:, KC * P:2 * KC * P].rearrange("p (c e) -> p c e", c=KC)

        def keep_states(eng, c, ps, step):
            eng.tensor_scalar(norms[:, c, :], k.blocks, ps[:, P:P + 1], None, ALU.mult)
            return eng.tensor_tensor(states[:, c, :], ps[:, 0:P], k.blocks, ALU.mult)

        kv = KeyValues(M, k, tok(c_), tok(d_), True, keep_states, after=[elu_k.done, val.done, elu_q.done])
        att = QueryStates(M, k, states, norms, fea(b_), fea(f_), u(e_)[:, 0:N], after=[kv.done])
        pb = row(M, "l0_projb")
        pre = Vector(M, lambda dve, step: dve.tensor_tensor(
            tok(e_), XN, pb.ap.unsqueeze(1).to_broadcast([P, NT, D]), ALU.add), rows=[pb], after=[att.done])
        proj = LinearTokens(M, k, [(PANELS["l0_proj"], fea(f_))], 2, onto(tok(e_)), after=[att.done])
        m_norm2 = LayerNorm(M, k, tok(e_), tok(b_), 1e-8, small_m, after=[proj.done])
        m_turn2 = ToFeatures(M, k, tok(b_), affine(k, fea(a_), "ln2w", "ln2b"), after=[m_norm2.done])
        hidden = [fea(b_), fea(c_), fea(d_), fea(f_)]
        for i in range(4):
            if i == GATE_FC:
                M.pace = 1.0
                Idle(M, gates_at[1] - M.time())
                M.pace = GATE_PACE[1]
            fc1 = LinearFeatures(M, k, [(PANELS["l0_fc1"] + 2 * i, fea(a_))], KC,
                                 act_col(k, hidden[i], ACT.Gelu, "l0_fc1b", 6 * i), "A", together=True, after=[m_turn2.done])
        fb = row(M, "l0_fc2b")
        pre2 = Vector(M, lambda dve, step: dve.tensor_tensor(
            tok(e_), tok(e_), fb.ap.unsqueeze(1).to_broadcast([P, NT, D]), ALU.add), rows=[fb])
        fc2 = LinearTokens(M, k, [(PANELS["l0_fc2"] + 2 * i, hidden[i]) for i in range(4)], 2, onto(tok(e_)),
                           after=[fc1.done])

        added0 = Vector(M, lambda dve, step: dve.tensor_tensor(X, X, tok(e_), ALU.add), after=[fc2.done])
        gnn_out.drain_after = [added0.done]

        S = lane("main", range(8), range(7), range(3))
        segments.append((S,))

        joined = []

        def join(other, after, eps=1e-5):
            if other is not None:
                after = [Vector(S, lambda dve, step: dve.tensor_tensor(X, X, other, ALU.add), after=after).done]
            joined.append(after[-1])
            n = LayerNorm(S, k, X, XN, eps, small_g, after=after)
            return ToFeatures(S, k, XN, copy(XNT), after=[n.done])

        t0 = join(None, [gnn_out.done])
        expert_buffers = SplitBuffers(weight_parts)
        first_experts = PanelParts(S, k, [PANELS["l0_w1"], PANELS["l0_w1"] + 1, PANELS["l0_w2"]], expert_buffers,
                                   after=[joined[0]]).parts
        split_x0 = SplitActivation(S, u(2), *input_parts, after=[t0.done])
        rank = sb("rank", [P, 16])[:, :]
        Vector(S, lambda dve, step: dve.tensor_scalar(rank, k.iota[:, 0:16], -1.0, 16.0, ALU.mult, ALU.add))

        def narrow_place(i, e, at=0):
            return u(i)[:, at:at + NT * e].rearrange("p (t e) -> p t e", t=NT)

        comb0, picked0 = narrow_place(12, 8), narrow_place(12, 8, 32)
        left = [narrow_place(12, 10, 64 + 32 * i) for i in range(3)]
        left8 = [narrow_place(12, 8, 64 + 32 * i) for i in range(3)]
        gates0 = Logits(S, k, XNT, k.narrow_of("gate"), 8, [(0, 8)], comb0, small_g[:, 0:2], after=[t0.done])

        def combine0(dve, step):
            step(top_two(dve, step, comb0, picked0, small_g[:, 0:2], rank[:, 0:8], left8, 8))
            step(dve.tensor_tensor(comb0, comb0, picked0, ALU.mult))
            step(dve.tensor_reduce(small_g[:, 0:2], comb0, AX.X, ALU.add))
            step(dve.reciprocal(small_g[:, 0:2], small_g[:, 0:2]))
            return dve.tensor_tensor(comb0, comb0, small_g[:, 0:2].unsqueeze(2).to_broadcast([P, NT, 8]), ALU.mult)

        picked = Vector(S, combine0, time=4.0, after=[gates0.done])
        comb0T = u(13)[0:8, 0:N]
        b2_row = S.row(b2, (8, D))
        ffn0 = Experts(S, k, [ap.rearrange("p (c n) -> p c n", c=KC) for ap in input_parts], X, comb0, comb0T, b2_row,
                       [u(14)[:, i * 768:(i + 1) * 768].rearrange("p (c n) -> p c n", c=3) for i in range(2)],
                       [[ap.rearrange("p (c n) -> p c n", c=3) for ap in pair] for pair in hidden_parts],
                       first_experts, expert_buffers, combined=[picked.done], after=[split_x0.done])
        end = ffn0.done

        def next_norm(after):
            n = LayerNorm(S, k, X, XN, 1e-5, small_g, after=after)
            return ToFeatures(S, k, XN, copy(XNT), after=[n.done])

        if last_layer >= 1:
            t1 = next_norm([end])
            G = lane("graph1", (0, 1, 2, 3), (0, 1, 2), (0, 1))
            M = lane("mix1", (4, 5, 6, 7), (3, 4, 5, 6), (2,))
            segments.append((G, M))
            a = Aggregate(G, k, XN, k.gcn, N, fea(3), after=[t1.done])
            gb = row(G, "gcn_b")
            pre = Vector(G, lambda dve, step: dve.tensor_tensor(
                X, X, gb.ap.unsqueeze(1).to_broadcast([P, NT, D]), ALU.add), rows=[gb], after=[t1.done])
            gcn = LinearTokens(G, k, [(PANELS["l1_gcn"], fea(3))], 2, onto(X), after=[a.done])

            qs = LinearFeatures(M, k, [(PANELS["l1_q"], XNT)], KC, scaled(fea(15), float(DH) ** -0.25), "V",
                                after=[t1.done])
            Vector(M, lambda dve, step: dve.memset(k.minus_half, -0.5))
            rf = u(4, 2).rearrange("p (h n) -> p h n", h=H)
            features = RandomFeatures(M, k, fea(15), fea(17), M.row(rand), rf,
                                      u(6, 2).rearrange("p (h n) -> p h n", h=H), small_m, after=[qs.done])
            v1 = LinearTokens(M, k, [(PANELS["l1_v"], XNT)], 2, copy_half(tok(16)))
            pb1 = row(M, "l1_projb")
            biased1 = Vector(M, lambda dve, step: dve.tensor_tensor(
                X, X, pb1.ap.unsqueeze(1).to_broadcast([P, NT, D]), ALU.add), rows=[pb1], after=[gcn.done])
            codes = SparseCodes(M, k, rf, tok(16), u(8, 2).rearrange("p (t h m) -> p t h m", t=NT, h=H),
                                u(10).rearrange("p (h m) -> p h m", h=H), u(18)[:, 0:D], u(18)[:, D:2 * D],
                                u(11)[:, 0:D], u(11)[:, D:2 * D], fea(17), small_m, after=[features.done, v1.done])
            mix1 = LinearTokens(M, k, [(PANELS["l1_proj"], fea(17))], 2, onto(X), after=[codes.done],
                                drain_after=[biased1.done])

            S = lane("main1", range(8), range(7), range(3))
            segments.append((S,))
            hid = LayerNorm(S, k, X, tok(3), 1e-5, small_g, after=[mix1.done])
            nrm = LayerNorm(S, k, tok(3), tok(4), 1e-5, small_g, after=[hid.done])
            nT = ToFeatures(S, k, tok(4), affine(k, fea(5), "g1", "gb1"), after=[nrm.done])
            qkv1 = PanelParts(S, k, [PANELS["l1_wq"], PANELS["l1_wq"] + 1], later_buffers, after=[mix1.done]).parts
            sx1 = SplitActivation(S, u(5), later_high, later_low, after=[nT.done])
            qkv1 = qkv1 + PanelParts(S, k, [PANELS[name] + i for name in ("l1_wk", "l1_wv") for i in range(2)],
                                     later_buffers).parts
            q1 = LinearFeatures(S, k, [(PANELS["l1_wq"], later_parts)], KC, plus_col(k, fea(6), "l1_bq"), "V",
                                after=[sx1.done], parts=qkv1[0:2])
            k1 = LinearFeatures(S, k, [(PANELS["l1_wk"], later_parts)], KC, plus_col(k, fea(7), "l1_bk"), "V",
                                parts=qkv1[2:4])
            vb1 = row(S, "l1_bv")
            v1b = LinearTokens(S, k, [(PANELS["l1_wv"], later_parts)], 2, plus_row(tok(8), vb1), drain_after=[vb1],
                               rows=[vb1], parts=qkv1[4:6])
            vb1.freed = v1b.done
            att1 = SoftmaxAttention(S, k, fea(6), fea(7), tok(8), fea(9), DH ** -0.5,
                                    [u(15)[:, i * 512:(i + 1) * 512].rearrange("p (t n) -> p t n", t=NT)
                                     for i in range(3)],
                                    [u(16)[:, i * 512:(i + 1) * 512].rearrange("p (t n) -> p t n", t=NT)
                                     for i in range(2)], small_m, after=[q1.done, k1.done, v1b.done])
            mask = small_g[:, 180:182]
            route = RouteScores(S, k, fea(5), u(17)[:, 0:D].rearrange("p (c n) -> p c n", c=KC), u(18)[:, 0:N],
                                fea(19), fea(10), mask, small_g, int(round(0.15 * N)), after=[v1b.done])
            bo, bmr = row(S, "l1_bo"), row(S, "l1_bm")
            ao = LinearTokens(S, k, [(PANELS["l1_wo"], fea(9))], 2, plus_row(tok(11), bo), after=[att1.done],
                              drain_after=[bo], rows=[bo])
            bo.freed = ao.done
            def merge_attention(dve, step):
                step(dve.tensor_scalar(small_g[:, 184:186], mask, -1.0, 1.0, ALU.mult, ALU.add))
                for t in range(NT):
                    ins = dve.scalar_tensor_tensor(out=tok(11)[:, t, :], in0=tok(11)[:, t, :],
                                                   scalar=mask[:, t:t + 1], in1=tok(3)[:, t, :],
                                                   op0=ALU.mult, op1=ALU.add)
                return ins

            def merge_mixed(dve, step):
                for t in range(NT):
                    ins = dve.scalar_tensor_tensor(out=tok(12)[:, t, :], in0=tok(12)[:, t, :],
                                                   scalar=small_g[:, 184 + t:185 + t], in1=tok(11)[:, t, :],
                                                   op0=ALU.mult, op1=ALU.add)
                return ins

            merged_attention = Vector(S, merge_attention, after=[ao.done, route.done])
            mo = LinearTokens(S, k, [(PANELS["l1_wm"], fea(10))], 2, plus_row(tok(12), bmr), after=[route.mixed],
                              drain_after=[bmr], rows=[bmr])
            bmr.freed = mo.done

            merged = Vector(S, merge_mixed, after=[merged_attention.done, mo.done])
            n2 = LayerNorm(S, k, tok(12), tok(13), 1e-5, small_g, after=[merged.done])
            n2T = ToFeatures(S, k, tok(13), affine(k, fea(14), "g2", "gb2"), after=[n2.done])
            f1T = u(15)[:, 0:768].rearrange("p (c n) -> p c n", c=3)
            f1 = LinearFeatures(S, k, [(PANELS["l1_f1"], fea(14))], 3, act_col(k, f1T, ACT.Gelu, "l1_bf1"), "A",
                                after=[n2T.done])
            bf2 = row(S, "l1_bf2")

            def add_merged(dve, step):
                step(dve.tensor_tensor(X, X, tok(12), ALU.add))
                return dve.tensor_tensor(X, X, bf2.ap.unsqueeze(1).to_broadcast([P, NT, D]), ALU.add)

            pre = Vector(S, add_merged, rows=[bf2], after=[merged.done])
            down = HalfDown(S, k, PANELS["l1_f2"], f1T, onto(X), after=[f1.done])
            end = down.done

        if last_layer >= 2:
            t2 = next_norm([end])
            G = lane("graph2", (0, 1, 2, 3), (0, 1, 2), (0, 1))
            M = lane("mix2", (4, 5, 6, 7), (3, 4, 5, 6), (2,))
            segments.append((G, M))
            view = lambda i, at: u(i)[:, at:at + 512].rearrange("p (t n) -> p t n", t=NT)
            edge_cap = view(6, 0)

            def masks(adj):
                def body(dve, step):
                    step(dve.tensor_scalar(edge_cap, adj, 0.5, None, ALU.is_gt))
                    return dve.tensor_scalar(edge_cap, edge_cap, -0.5, 2e30, ALU.add, ALU.mult)
                return body

            Vector(G, masks(k.adj), after=[t2.done])

            def gat(h, weights, inT, s_row, d_row, after):
                rs, rd = row(G, s_row), row(G, d_row)
                lin = LinearTokens(G, k, [(weights, inT)], 2, copy_half(h), after=after)

                def scores(dve, step):
                    for r_, at in ((rs, 32), (rd, 34)):
                        step(dve.tensor_tensor(tok(4), h, r_.ap.unsqueeze(1).to_broadcast([P, NT, D]), ALU.mult))
                        ins = dve.tensor_reduce(small_g[:, at:at + 2], tok(4), AX.X, ALU.add)
                        if at == 32:
                            step(ins)
                    return ins

                s_ = Vector(G, scores, time=7.0, after=[lin.done], rows=[rs, rd])
                return EdgeSoftmax(G, k, small_g[:, 32:34].unsqueeze(2), small_g[:, 34:36].unsqueeze(2), 1, k.adj,
                                   edge_cap,
                                   [u(5)[:, 512 + 256 * i:768 + 256 * i].rearrange("p (t n) -> p t n", t=NT)
                                    for i in range(2)], [view(5, 0)] * 3, small_g,
                                   u(5)[:, 1024:1536].rearrange("p (h s n) -> p h s n", h=1, s=NT), False,
                                   after=[s_.done])

            e1 = gat(tok(3), PANELS["l2_gat1"], XNT, "att_s1", "att_d1", [t2.done])
            g1 = AggregateRelu(G, k, tok(3), u(5)[:, 1024:1536].rearrange("p (s n) -> p s n", s=NT), fea(7),
                               "gat_b1", after=[e1.done])
            e2 = gat(tok(8), PANELS["l2_gat2"], fea(7), "att_s2", "att_d2", [g1.done])
            gb2 = row(G, "gat_b2")
            pre = Vector(G, lambda dve, step: dve.tensor_tensor(
                X, X, gb2.ap.unsqueeze(1).to_broadcast([P, NT, D]), ALU.add), rows=[gb2], after=[e2.done])
            g2 = AggregateTokens(G, k, u(5)[:, 1024:1536].rearrange("p (h s n) -> p h s n", h=1, s=NT), 1, tok(8),
                                 onto(X), after=[e2.done], drain_after=[pre.done])

            key = LinearTokens(M, k, [(PANELS["l2_kv"], XNT)], 2, copy_half(tok(15)), after=[t2.done])
            val = LinearTokens(M, k, [(PANELS["l2_kv"] + 2, XNT)], 2, copy_half(tok(16)))
            q = LinearFeatures(M, k, [(PANELS["l2_q"], XNT)], KC, act_col(k, fea(17), ACT.Gelu), "A")
            gstates = u(18)[:, 0:KC * P].rearrange("p (c e) -> p c e", c=KC)

            def keep2(eng, c, ps, step):
                return eng.scalar_tensor_tensor(out=gstates[:, c, :], in0=ps[:, 0:P], scalar=float(DH) ** -0.5,
                                                in1=k.blocks, op0=ALU.mult, op1=ALU.mult)

            kv = KeyValues(M, k, tok(15), tok(16), False, keep2, after=[key.done, val.done])
            kvg = Activation(M, lambda act: act.activation(gstates, gstates, ACT.Gelu), after=[kv.done])
            att = QueryStates(M, k, gstates, None, fea(17), fea(19), None, after=[kvg.done, q.done])
            pb2 = row(M, "l2_projb")
            mix2 = LinearTokens(M, k, [(PANELS["l2_proj"], fea(19))], 2, plus_row(tok(20), pb2), after=[att.done],
                                drain_after=[pb2], rows=[pb2])
            pb2.freed = mix2.done

            S = lane("main2", range(8), range(7), range(3))
            segments.append((S,))
            t2b = join(tok(20), [g2.done, mix2.done])
            qkv2 = PanelParts(S, k, [PANELS["l2_qkv"] + i for i in range(2)], later_buffers, after=[joined[-1]]).parts
            sx2 = SplitActivation(S, u(2), later_high, later_low, after=[t2b.done])
            E2 = 14
            probs2 = narrow_place(12, E2)
            picked2 = narrow_place(12, 10, 32)
            gates2 = narrow_place(12, H, 192)
            lg = Logits(S, k, XNT, k.narrow_of("gates"), E2, [(0, 10), (10, 12), (12, 14)], probs2, small_g[:, 0:2],
                        after=[t2b.done])

            qkv2 = qkv2 + PanelParts(S, k, [PANELS["l2_qkv"] + i for i in (2, 3)], later_buffers).parts

            def head_gates(dve, step):
                routed = probs2[:, :, 0:10]
                best = small_g[:, 0:2]
                step(top_two(dve, step, routed, picked2, best, rank[:, 0:10], left, 10))
                step(dve.tensor_tensor(routed, routed, picked2, ALU.mult))
                step(dve.tensor_reduce(best, routed, AX.X, ALU.add))
                step(dve.tensor_scalar(best, best, float(np.finfo(np.float32).eps), None, ALU.max))
                step(dve.reciprocal(best, best))
                step(dve.tensor_scalar(best, best, 4.0, None, ALU.mult))
                step(dve.tensor_tensor(best, best, probs2[:, :, 11], ALU.mult))
                step(dve.tensor_tensor(gates2[:, :, 2:H], routed, best.unsqueeze(2).to_broadcast([P, NT, 10]),
                                       ALU.mult))
                step(dve.tensor_scalar(best, probs2[:, :, 10], 4.0, None, ALU.mult))
                return dve.tensor_tensor(gates2[:, :, 0:2], probs2[:, :, 12:14],
                                         best.unsqueeze(2).to_broadcast([P, NT, 2]), ALU.mult)

            hg2 = Vector(S, head_gates, time=5.0, after=[lg.done])
            normed2 = []
            for dst_, name, at in ((3, "l2_qb", 0), (4, "l2_kb", 2), (5, "l2_vb", 4)):
                r_ = row(S, name)
                if dst_ == 4:
                    qkv2 = qkv2 + PanelParts(S, k, [PANELS["l2_qkv"] + i for i in (4, 5)], later_buffers).parts
                lin = LinearTokens(S, k, [(PANELS["l2_qkv"] + at, later_parts)], 2, plus_row(tok(dst_), r_),
                                   after=[sx2.done], drain_after=[r_], rows=[r_], parts=qkv2[at:at + 2])
                r_.freed = lin.done
                if dst_ < 5:
                    normed2.append(HeadNorm(S, k, tok(dst_), tok(6), small_g, after=[lin.done]))
            qn, kn = normed2
            qT = ToFeatures(S, k, tok(3), head_affine(k, fea(7), "qnw", "qnb"), after=[qn.done])
            kT = ToFeatures(S, k, tok(4), head_affine(k, fea(8), "knw", "knb"), after=[kn.done])
            att2 = SoftmaxAttention(S, k, fea(7), fea(8), tok(5), fea(9), DH ** -0.5,
                                    [view(15, i * 512) for i in range(3)], [view(16, i * 512) for i in range(2)],
                                    small_m, gates=gates2, after=[qT.done, kT.done, lin.done, hg2.done])
            bo2 = row(S, "l2_bo")
            pre = Vector(S, lambda dve, step: dve.tensor_tensor(
                X, X, bo2.ap.unsqueeze(1).to_broadcast([P, NT, D]), ALU.add), rows=[bo2])
            wo2 = LinearTokens(S, k, [(PANELS["l2_wo"], fea(9))], 2, onto(X), after=[att2.done])
            end = wo2.done

        if last_layer >= 3:
            t3 = next_norm([end])
            G = lane("graph3", (0, 1, 2, 3), (0, 1, 2), (0, 1))
            M = lane("mix3", (4, 5, 6, 7), (3, 4, 5, 6), (2,))
            segments.append((G, M))
            edge_cap3 = view(7, 0)

            def masks3(dve, step):
                for t in range(NT):
                    blk = k.adj[:, t, t * P:(t + 1) * P]
                    ins = dve.tensor_tensor(blk, blk, k.ident, ALU.subtract)
                step(ins)
                step(dve.tensor_scalar(edge_cap3, k.adj, 0.5, None, ALU.is_gt))
                return dve.tensor_scalar(edge_cap3, edge_cap3, -0.5, 2e30, ALU.add, ALU.mult)

            Vector(G, masks3, after=[t3.done])
            mats = G.load(row_slots, 0, head_mats, (P, 2 * P))
            ft = HeadMatrices(G, k, XNT, mats, (tok(3), tok(4)), after=[t3.done])
            G.nrow = 1
            al = row(G, "attn_l")
            ar = row(G, "attn_r")

            def head_scores(dve, step):
                for r_, at in ((al, 64), (ar, 96)):
                    step(dve.tensor_tensor(tok(5), tok(3), r_.ap.unsqueeze(1).to_broadcast([P, NT, D]), ALU.mult))
                    ins = dve.tensor_reduce(small_g[:, at:at + NT * H],
                                            tok(5).rearrange("p t (h d) -> p (t h) d", h=H), AX.X, ALU.add)
                    if at == 64:
                        step(ins)
                return ins

            hs = Vector(G, head_scores, time=7.0, after=[ft.done], rows=[al, ar])
            columns = lambda at: small_g[:, at:at + NT * H].rearrange("p (t h) -> p t h", t=NT)
            pT = u(8, 4).rearrange("p (h s n) -> p h s n", h=H, s=NT)
            es = EdgeSoftmax(G, k, columns(64), columns(96), H, k.adj, edge_cap3,
                             [u(7)[:, 1024 + 256 * i:1280 + 256 * i].rearrange("p (t n) -> p t n", t=NT)
                              for i in range(2)], [view(6, 0), view(6, 512), view(6, 1024)], small_g, pT, True, after=[hs.done])
            res = tok(4)
            ag = AggregateTokens(G, k, pT, H, tok(3), onto(res), after=[es.done])

            def add_relu(dve, step):
                step(dve.tensor_scalar(res, res, 0.0, None, ALU.max))
                return dve.tensor_tensor(X, X, res, ALU.add)

            g3 = Vector(G, add_relu, after=[ag.done])

            q = LinearFeatures(M, k, [(PANELS["l3_qk"], XNT)], KC, plus_col(k, fea(15), "l3_qb"), "V",
                               after=[t3.done])
            key = LinearFeatures(M, k, [(PANELS["l3_qk"] + 2, XNT)], KC, plus_col(k, fea(16), "l3_kb"), "V")
            vb3 = row(M, "l3_vb")
            val = LinearTokens(M, k, [(PANELS["l3_v"], XNT)], 2, plus_row(tok(17), vb3), drain_after=[vb3],
                               rows=[vb3])
            vb3.freed = val.done
            poly = PolynomialAttention(M, k, fea(15), fea(16), tok(17), fea(18),
                                       [view(19, 0), view(19, 512)], u(19)[:, 1024:1280], DH ** -0.5,
                                       after=[q.done, key.done, val.done])
            pb3 = row(M, "l3_projb")
            mix3 = LinearTokens(M, k, [(PANELS["l3_proj"], fea(18))], 2, plus_row(tok(20), pb3), after=[poly.done],
                                drain_after=[pb3], rows=[pb3])
            pb3.freed = mix3.done

            S = lane("main3", range(8), range(7), range(3))
            segments.append((S,))
            t3b = join(tok(20), [g3.done, mix3.done])
            EX, RK = 8, 16
            qkv3 = PanelParts(S, k, [PANELS["l3_wq"], PANELS["l3_wq"] + 1], later_buffers, after=[joined[-1]]).parts
            sx3 = SplitActivation(S, u(2), later_high, later_low, after=[t3b.done])
            bm_place, bb_place = u(7, 2)[:, 0:3 * D], u(9, 2)[0:EX, 0:3 * D]
            fetch = Fetch(S, adapters_arrived, [(bm_place, bm), (bb_place, bb)], after=[g3.done, mix3.done])
            comb3 = narrow_place(12, EX)
            picked3 = narrow_place(12, EX, 32)
            lg3 = Logits(S, k, XNT, k.narrow_of("l3_gate"), EX, [(0, EX)], comb3, small_g[:, 0:2],
                         bias=k.short("bg"), after=[t3b.done])

            def combine3(dve, step):
                step(top_two(dve, step, comb3, picked3, small_g[:, 0:2], rank[:, 0:EX], left8, EX))
                return dve.scalar_tensor_tensor(out=comb3, in0=comb3, scalar=2.0, in1=picked3, op0=ALU.mult,
                                                op1=ALU.mult)

            cb3 = Vector(S, combine3, time=4.0, after=[lg3.done])
            comb3T = u(13)[0:EX, 0:N]
            c3T = TurnNarrow(S, k, comb3, EX, comb3T, after=[cb3.done])
            hw = u(13)[:, N:2 * N].rearrange("p (t n) -> p t n", t=NT)
            hwT = u(13)[:, 2 * N:3 * N]
            ad = Adapters(S, k, XNT, S.row(a_t), comb3, hw, EX, RK, after=[cb3.done])
            hT = TurnNarrow(S, k, hw, P, hwT, after=[ad.done])

            def feature_tail(at):
                def tail(pe, o, ps):
                    c0 = at + o * P
                    pe.matmul(ps, bm_place[:, c0:c0 + P], hwT, start=False, stop=False)
                    return pe.matmul(ps, bb_place[:, c0:c0 + P], comb3T, start=False, stop=True)
                return tail

            def token_tail(pe, t, g, ps):
                c0 = 2 * D + g * COLS
                pe.matmul(ps, hwT[:, t * P:(t + 1) * P], bm_place[:, c0:c0 + COLS], start=False, stop=False)
                return pe.matmul(ps, comb3T[:, t * P:(t + 1) * P], bb_place[:, c0:c0 + COLS], start=False, stop=True)

            tail_after = [fetch, hT.done, c3T.done]
            qkv3 = qkv3 + PanelParts(S, k, [PANELS[name] + i for name in ("l3_wk", "l3_wv") for i in range(2)],
                                     later_buffers).parts
            q3 = LinearFeatures(S, k, [(PANELS["l3_wq"], later_parts)], KC, plus_col(k, fea(3), "l3_bqk"), "V",
                                after=[sx3.done], parts=qkv3[0:2], tail=feature_tail(0), tail_after=tail_after)
            k3 = LinearFeatures(S, k, [(PANELS["l3_wk"], later_parts)], KC, plus_col(k, fea(4), "l3_bqk", KC), "V", parts=qkv3[2:4],
                                tail=feature_tail(D))
            vb4 = row(S, "l3_bv")
            v3 = LinearTokens(S, k, [(PANELS["l3_wv"], later_parts)], 2, plus_row(tok(5), vb4), drain_after=[vb4],
                              rows=[vb4], parts=qkv3[4:6], tail=token_tail)
            vb4.freed = v3.done
            att3 = SoftmaxAttention(S, k, fea(3), fea(4), tok(5), fea(6), DH ** -0.5,
                                    [view(15, i * 512) for i in range(3)], [view(16, i * 512) for i in range(2)],
                                    small_m, after=[q3.done, k3.done, v3.done])
            bo3 = row(S, "l3_bo")
            pre = Vector(S, lambda dve, step: dve.tensor_tensor(
                X, X, bo3.ap.unsqueeze(1).to_broadcast([P, NT, D]), ALU.add), rows=[bo3])
            wo3 = LinearTokens(S, k, [(PANELS["l3_wo"], fea(6))], 2, onto(X), after=[att3.done])
            end = wo3.done

        def run(part, eng):
            for lanes in segments:
                side_by_side([lane_.stages for lane_ in lanes], part, eng)

        block = ctx.enter_context(nc.Block())

        @block.sync
        def _(sp):
            sp.dma_start(X, x_in.rearrange("(t p) d -> p t d", p=P)).then_inc(x_arrived, 16)
            for i, v_ in enumerate((src, dst, edge_type)):
                sp.dma_start(k.edges_int[:, i, :], v_.rearrange("(p c) -> p c", p=P)).then_inc(edges_arrived, 16)
            sp.dma_start(k.cols, cols).then_inc(small_arrived, 16)
            sp.dma_start(k.narrow, narrow).then_inc(small_arrived, 16)
            sp.dma_start(k.shorts, shorts.to_broadcast([P, N_SHORT])).then_inc(small_arrived, 16)
            sp.dma_start(QT, query_t).then_inc(query_arrived, 16)
            run("s", sp)
            sp.wait_ge(*end.at)
            sp.dma_start(out.rearrange("(t p) d -> p t d", p=P), X).then_inc(out_written, 16)
            sp.wait_ge(out_written, 16)

        @block.tensor
        def _(pe):
            run("t", pe)

        @block.vector
        def _(dve):
            run("v", dve)

        @block.scalar
        def _(act):
            run("a", act)

        @block.gpsimd
        def _(pool):
            run("p", pool)


def kernel(**inputs):
    import concourse.bacc as bacc
    from concourse.bass_utils import run_bass_kernel_spmd

    w = {name: np.asarray(a) for name, a in inputs.items()}

    def cut(m, k=KC, n=COLS):
        parts = []
        for c in range(0, m.shape[1], n):
            parts.append(np.ascontiguousarray(
                m[:, c:c + n].reshape(k, P, n).transpose(1, 0, 2)).reshape(P, k * n))
        return parts

    def stack(mats):
        return [p for m in mats for p in cut(m)]

    rel1, rel2 = w["L0_gnn_W_rel1"], w["L0_gnn_W_rel2"]
    wg, wq = w["L0_gnn_Wg"], w["L0_gnn_Wq"]
    fc2 = w["L0_mix_fc2_w"]
    l3_w = w["L3_ffn_Wqkv"]
    panel_groups = {
        "qg_w": stack([wg[:, D:].T]), "rel1": stack([*rel1, w["L0_gnn_W_root1"]]),
        "hg_w": stack([wg[:, :D].T]), "alpha_w": stack([wq[:, :D].T, wq[:, D:].T]),
        "rel2": stack([*rel2, w["L0_gnn_W_root2"]]),
        "l0_qkv": cut(w["L0_mix_qkv_w"]), "l0_proj": cut(w["L0_mix_proj_w"]), "l0_fc1": cut(w["L0_mix_fc1_w"]),
        "l0_fc2": stack([fc2[i * D:(i + 1) * D] for i in range(4)]),
        "l0_w1": stack(list(w["L0_ffn_w1"])), "l0_w2": [cut(m, 3, D)[0] for m in w["L0_ffn_w2"]],
        "l1_gcn": cut(w["L1_gnn_W"]), "l1_q": cut(w["L1_mix_Wqkv"][:, :D]), "l1_v": cut(w["L1_mix_Wqkv"][:, D:]),
        "l1_proj": cut(w["L1_mix_Wproj"]), "l1_wq": cut(w["L1_ffn_Wq"]), "l1_wk": cut(w["L1_ffn_Wk"]),
        "l1_wv": cut(w["L1_ffn_Wv"]), "l1_wo": cut(w["L1_ffn_Wo"]), "l1_wm": cut(w["L1_ffn_Wm"]),
        "l1_f1": cut(w["L1_ffn_W1"]), "l1_f2": cut(w["L1_ffn_W2"], 3, D),
        "l2_gat1": cut(w["L2_gnn_W1"]), "l2_gat2": cut(w["L2_gnn_W2"]),
        "l2_q": cut(w["L2_mix_w_qkv"][:, :D]), "l2_kv": cut(w["L2_mix_w_qkv"][:, D:]),
        "l2_proj": cut(w["L2_mix_w_proj"]), "l2_qkv": cut(w["L2_ffn_qkv_w"]), "l2_wo": cut(w["L2_ffn_proj_w"]),
        "l3_qk": cut(w["L3_mix_w_qkv"][:, :2 * D]), "l3_v": cut(w["L3_mix_w_qkv"][:, 2 * D:]),
        "l3_proj": cut(w["L3_mix_w_proj"]), "l3_wq": cut(l3_w[:D].T), "l3_wk": cut(l3_w[D:2 * D].T),
        "l3_wv": cut(l3_w[2 * D:].T), "l3_wo": cut(w["L3_ffn_Wproj"].T)}
    panels = np.stack([p for name in PANELS for p in panel_groups[name]])
    assert len(panels) == N_PANELS

    def col(v):
        return np.ascontiguousarray(v.reshape(-1, P).T)

    twice = lambda v: np.concatenate([v, v]).reshape(P, 1)
    qkv_b, mix3_b, ffn3_b = w["L0_mix_qkv_b"], w["L3_mix_b_qkv"], w["L3_ffn_bqkv"]
    columns = {"b1": col(w["L0_gnn_b1"]), "b2": col(w["L0_gnn_b2"]), "bq": col(w["L0_gnn_bq"]), "l0_qb": col(qkv_b[:D]), "l0_fc1b": col(w["L0_mix_fc1_b"]),
               "ln1w": col(w["L0_mix_ln1_w"]), "ln1b": col(w["L0_mix_ln1_b"]), "ln2w": col(w["L0_mix_ln2_w"]),
               "ln2b": col(w["L0_mix_ln2_b"]), "l0_b1": col(w["L0_ffn_b1"]), "g1": col(w["L1_ffn_g1"]),
               "gb1": col(w["L1_ffn_b1"]), "g2": col(w["L1_ffn_g2"]), "gb2": col(w["L1_ffn_b2"]),
               "l1_bq": col(w["L1_ffn_bq"]), "l1_bk": col(w["L1_ffn_bk"]), "l1_bf1": col(w["L1_ffn_bf1"]),
               "gat_b1": col(w["L2_gnn_b1"]), "qnw": twice(w["L2_ffn_q_norm_w"]), "qnb": twice(w["L2_ffn_q_norm_b"]),
               "knw": twice(w["L2_ffn_k_norm_w"]), "knb": twice(w["L2_ffn_k_norm_b"]), "l3_qb": col(mix3_b[:D]),
               "l3_kb": col(mix3_b[D:2 * D]), "l3_bqk": col(ffn3_b[:2 * D])}
    cols = np.concatenate([columns[name] for name in COLUMNS], axis=1)
    l2b = w["L2_ffn_qkv_b"]
    row_of = {"l0_kb": qkv_b[D:2 * D], "l0_vb": qkv_b[2 * D:], "l0_projb": w["L0_mix_proj_b"],
              "l0_fc2b": w["L0_mix_fc2_b"], "gcn_b": w["L1_gnn_b"], "l1_projb": w["L1_mix_bproj"],
              "l1_bv": w["L1_ffn_bv"], "l1_bo": w["L1_ffn_bo"], "l1_bm": w["L1_ffn_bm"], "l1_bf2": w["L1_ffn_bf2"],
              "att_s1": w["L2_gnn_att_src1"], "att_d1": w["L2_gnn_att_dst1"], "att_s2": w["L2_gnn_att_src2"],
              "att_d2": w["L2_gnn_att_dst2"], "gat_b2": w["L2_gnn_b2"], "l2_projb": w["L2_mix_b_proj"],
              "l2_qb": l2b[:D], "l2_kb": l2b[D:2 * D], "l2_vb": l2b[2 * D:], "l2_bo": w["L2_ffn_proj_b"],
              "attn_l": w["L3_gnn_attn_l"].reshape(-1), "attn_r": w["L3_gnn_attn_r"].reshape(-1),
              "l3_vb": mix3_b[2 * D:], "l3_projb": w["L3_mix_b_proj"], "l3_bv": ffn3_b[2 * D:],
              "l3_bo": w["L3_ffn_bproj"], "bg": w["L0_gnn_bg"]}
    rows = np.stack([row_of[name] for name in ROWS])
    narrow = np.concatenate([w["L0_ffn_gate_w"], w["L1_ffn_Wr"].reshape(D, 1), w["L2_ffn_wg_w"], w["L2_ffn_wg0_w"],
                             w["L2_ffn_wg1_w"], w["L3_ffn_Wg"].T], axis=1)
    narrow = np.ascontiguousarray(narrow.reshape(KC, P, N_NARROW).transpose(1, 0, 2))
    shorts = np.concatenate([w["L3_ffn_ba"].reshape(-1), w["L3_ffn_bg"], w["L1_ffn_br"].reshape(-1)]).reshape(1, -1)
    query_t = np.ascontiguousarray(w["L0_gnn_query_embs"].reshape(B * L, KC, P).transpose(2, 1, 0))
    rand = np.ascontiguousarray(w["L1_mix_rand_matrix"].reshape(KC, P, P).transpose(1, 0, 2)).reshape(P, D)
    head_mats = np.zeros((P, 2 * P), np.float32)
    for i, m in enumerate((w["L3_gnn_W_fc"], w["L3_gnn_W_res"])):
        for b in range(2):
            head_mats[b * DH:(b + 1) * DH, i * P + b * DH:i * P + (b + 1) * DH] = m.T
    a_t = cut(w["L3_ffn_A"].reshape(P, D).T, KC, P)[0]
    bm = np.ascontiguousarray(w["L3_ffn_Bm"].transpose(0, 2, 1)).reshape(P, 3 * D)

    arrays = {"x": w["x"], "src": w["src"], "dst": w["dst"], "edge_type": w["edge_type_3"], "panels": panels,
              "cols": cols, "rows": rows, "narrow": narrow, "shorts": shorts, "query_t": query_t,
              "b2": w["L0_ffn_b2"].reshape(8, D), "rand": rand, "head_mats": head_mats, "a_t": a_t, "bm": bm,
              "bb": w["L3_ffn_bb"]}
    nc = bacc.Bacc("TRN2", target_bir_lowering=False, num_devices=1)
    arrays = {f"in_{name}": np.ascontiguousarray(a) for name, a in arrays.items()}
    args = [nc.dram_tensor(name, a.shape, mybir.dt.from_np(a.dtype), kind="ExternalInput").ap()
            for name, a in arrays.items()]
    out = nc.dram_tensor("out", (N, D), F32, kind="ExternalOutput").ap()
    build(nc, *args, out)
    return run_bass_kernel_spmd(nc, [arrays], core_ids=[0]).results[0]["out"]
```
